# Optimizing a Trainium2 kernel written in Bass

```python
import numpy as np
import jax
import jax.numpy as jnp

def _softmax(x, axis=-1):
    return jax.nn.softmax(x, axis=axis)

def _gelu(x):
    return jax.nn.gelu(x, approximate=True)

def _silu(x):
    return jax.nn.silu(x)

def _sigmoid(x):
    return jax.nn.sigmoid(x)

def _layernorm(x, axis=-1, eps=1e-05):
    m = jnp.mean(x, axis=axis, keepdims=True)
    v = jnp.var(x, axis=axis, keepdims=True)
    return (x - m) / jnp.sqrt(v + eps)

def _scatter_add(tgt, idx, src, axis=0):
    return tgt.at[idx].add(src)

def _segment_sum(src, seg, n):
    return jax.ops.segment_sum(src, seg, n)
kernel_name = 'mk_prb_d2_jaxref_r4_7aa8d6'

def setup_inputs(seed: int=0):
    np.random.seed(seed)
    _w = jnp.asarray

    def _L0_attn_setup():
        import jax, jax.numpy as jnp
        import numpy as np
        N_HEADS = 16
        ROPE_THETA = 10000.0

        def _rope_tables(T, d, dtype=jnp.float32):
            inv = 1.0 / ROPE_THETA ** (jnp.arange(0, d, 2, dtype=dtype) / d)
            t = jnp.arange(T, dtype=dtype)
            freqs = jnp.outer(t, inv)
            return (jnp.cos(freqs), jnp.sin(freqs))

        def _apply_rope(x, cos, sin):
            x_even = x[..., ::2]
            x_odd = x[..., 1::2]
            cos = cos[None, None]
            sin = sin[None, None]
            rot_even = x_even * cos - x_odd * sin
            rot_odd = x_odd * cos + x_even * sin
            out = jnp.stack([rot_even, rot_odd], axis=-1)
            return out.reshape(x.shape)
        key = jax.random.key(seed)
        k1, k2, k3 = jax.random.split(key, 3)
        B, T, C = (1, 1024, 256)
        x = jax.random.normal(k1, (B, T, C), dtype=jnp.float32)
        w_qkv = jax.random.normal(k2, (C, 3 * C), dtype=jnp.float32) * (1.0 / np.sqrt(C))
        w_out = jax.random.normal(k3, (C, C), dtype=jnp.float32) * (1.0 / np.sqrt(C))
        return {'x': x, 'w_qkv': w_qkv, 'w_out': w_out}
    _L0_attn_in = _L0_attn_setup()

    def _L0_ffn_setup():
        import jax, jax.numpy as jnp
        import numpy as np

        def _binarize(w):
            alpha = jax.lax.stop_gradient(jnp.mean(jnp.abs(w), axis=1, keepdims=True))
            bw = alpha * jnp.sign(w)
            return w + jax.lax.stop_gradient(bw - w)
        key = jax.random.key(seed)
        k1, k2, k3, k4, k5 = jax.random.split(key, 5)
        D, H = (256, 1024)
        x = jax.random.normal(k1, (64, 196, D), dtype=jnp.float32)
        w1 = jax.random.normal(k2, (H, D), dtype=jnp.float32) * 0.02
        b1 = jax.random.normal(k3, (H,), dtype=jnp.float32) * 0.02
        w2 = jax.random.normal(k4, (D, H), dtype=jnp.float32) * 0.02
        b2 = jax.random.normal(k5, (D,), dtype=jnp.float32) * 0.02
        return {'x': x, 'w1': w1, 'b1': b1, 'w2': w2, 'b2': b2}
    _L0_ffn_in = _L0_ffn_setup()

    def _L1_attn_setup():
        import jax, jax.numpy as jnp
        import numpy as np
        B, T, D = (4, 1024, 256)
        NEG_CLAMP = -30.0
        EPS = 1e-09

        def _wkv_scan(k, v, w, u):
            Bn, Tn, Dn = k.shape
            p0 = jnp.full((Bn, Dn), -jnp.inf, k.dtype)
            q0 = jnp.zeros((Bn, Dn), k.dtype)

            def step(carry, kv_t):
                p, q = carry
                k_t, v_t = kv_t
                new_p = jnp.maximum(p, u + k_t)
                scale_old = jnp.exp(jnp.maximum(p - new_p, NEG_CLAMP))
                scale_cur = jnp.exp(jnp.maximum(u + k_t - new_p, NEG_CLAMP))
                wkv_t = (scale_old * q + scale_cur * v_t) / (scale_old + scale_cur + EPS)
                new_p2 = jnp.maximum(p + w, k_t)
                scale_prev = jnp.exp(jnp.maximum(p + w - new_p2, NEG_CLAMP))
                scale_new = jnp.exp(jnp.maximum(k_t - new_p2, NEG_CLAMP))
                q2 = scale_prev * q + scale_new * v_t
                return ((new_p2, q2), wkv_t)
            kT = jnp.swapaxes(k, 0, 1)
            vT = jnp.swapaxes(v, 0, 1)
            _, wkvT = jax.lax.scan(step, (p0, q0), (kT, vT))
            return jnp.swapaxes(wkvT, 0, 1)
        key = jax.random.key(seed)
        ks = jax.random.split(key, 10)
        s = 0.02
        return {'x': jax.random.normal(ks[0], (B, T, D), jnp.float32), 'time_mix_k': jax.random.uniform(ks[1], (D,), jnp.float32), 'time_mix_v': jax.random.uniform(ks[2], (D,), jnp.float32), 'time_mix_r': jax.random.uniform(ks[3], (D,), jnp.float32), 'W_k': jax.random.normal(ks[4], (D, D), jnp.float32) * s, 'W_v': jax.random.normal(ks[5], (D, D), jnp.float32) * s, 'W_r': jax.random.normal(ks[6], (D, D), jnp.float32) * s, 'W_o': jax.random.normal(ks[7], (D, D), jnp.float32) * s, 'time_decay': -(1.0 + jax.random.uniform(ks[8], (D,), jnp.float32)), 'time_first': 0.1 * jax.random.normal(ks[9], (D,), jnp.float32)}
    _L1_attn_in = _L1_attn_setup()

    def _L1_ffn_setup():
        import jax, jax.numpy as jnp
        import numpy as np
        TOP_K = 2
        NUM_EXPERTS = 8
        key = jax.random.key(seed)
        ks = jax.random.split(key, 8)
        h, d, ds, E = (256, 128, 256, NUM_EXPERTS)
        s = 1.0 / np.sqrt(h)
        return {'x': jax.random.normal(ks[0], (2, 512, h), jnp.float32), 'router': jax.random.normal(ks[1], (h, E), jnp.float32) * s, 'experts_gate': jax.random.normal(ks[2], (E, h, d), jnp.float32) * s, 'experts_up': jax.random.normal(ks[3], (E, h, d), jnp.float32) * s, 'experts_down': jax.random.normal(ks[4], (E, d, h), jnp.float32) * (1.0 / np.sqrt(d)), 'shared_gate': jax.random.normal(ks[5], (h, ds), jnp.float32) * s, 'shared_up': jax.random.normal(ks[6], (h, ds), jnp.float32) * s, 'shared_down': jax.random.normal(ks[7], (ds, h), jnp.float32) * (1.0 / np.sqrt(ds))}
    _L1_ffn_in = _L1_ffn_setup()
    _d = {'L0_attn_x': _L0_attn_in['x'], 'L0_attn_w_qkv': _L0_attn_in['w_qkv'], 'L0_attn_w_out': _L0_attn_in['w_out'], 'L0_ffn_w1': _L0_ffn_in['w1'], 'L0_ffn_b1': _L0_ffn_in['b1'], 'L0_ffn_w2': _L0_ffn_in['w2'], 'L0_ffn_b2': _L0_ffn_in['b2'], 'L1_attn_time_mix_k': _L1_attn_in['time_mix_k'], 'L1_attn_time_mix_v': _L1_attn_in['time_mix_v'], 'L1_attn_time_mix_r': _L1_attn_in['time_mix_r'], 'L1_attn_W_k': _L1_attn_in['W_k'], 'L1_attn_W_v': _L1_attn_in['W_v'], 'L1_attn_W_r': _L1_attn_in['W_r'], 'L1_attn_W_o': _L1_attn_in['W_o'], 'L1_attn_time_decay': _L1_attn_in['time_decay'], 'L1_attn_time_first': _L1_attn_in['time_first'], 'L1_ffn_router': _L1_ffn_in['router'], 'L1_ffn_experts_gate': _L1_ffn_in['experts_gate'], 'L1_ffn_experts_up': _L1_ffn_in['experts_up'], 'L1_ffn_experts_down': _L1_ffn_in['experts_down'], 'L1_ffn_shared_gate': _L1_ffn_in['shared_gate'], 'L1_ffn_shared_up': _L1_ffn_in['shared_up'], 'L1_ffn_shared_down': _L1_ffn_in['shared_down']}
    _x0 = _d['L0_attn_x']
    _d['L0_attn_x'] = jax.random.normal(jax.random.fold_in(jax.random.key(seed), 1), (2, 2048, 256), dtype=_x0.dtype)
    del _x0
    return _d

def reference(L0_attn_x, L0_attn_w_qkv, L0_attn_w_out, L0_ffn_w1, L0_ffn_b1, L0_ffn_w2, L0_ffn_b2, L1_attn_time_mix_k, L1_attn_time_mix_v, L1_attn_time_mix_r, L1_attn_W_k, L1_attn_W_v, L1_attn_W_r, L1_attn_W_o, L1_attn_time_decay, L1_attn_time_first, L1_ffn_router, L1_ffn_experts_gate, L1_ffn_experts_up, L1_ffn_experts_down, L1_ffn_shared_gate, L1_ffn_shared_up, L1_ffn_shared_down):

    def _L0_attn_ref(x, w_qkv, w_out):
        import jax, jax.numpy as jnp
        import numpy as np
        N_HEADS = 16
        ROPE_THETA = 10000.0

        def _rope_tables(T, d, dtype=jnp.float32):
            inv = 1.0 / ROPE_THETA ** (jnp.arange(0, d, 2, dtype=dtype) / d)
            t = jnp.arange(T, dtype=dtype)
            freqs = jnp.outer(t, inv)
            return (jnp.cos(freqs), jnp.sin(freqs))

        def _apply_rope(x, cos, sin):
            x_even = x[..., ::2]
            x_odd = x[..., 1::2]
            cos = cos[None, None]
            sin = sin[None, None]
            rot_even = x_even * cos - x_odd * sin
            rot_odd = x_odd * cos + x_even * sin
            out = jnp.stack([rot_even, rot_odd], axis=-1)
            return out.reshape(x.shape)
        B, T, C = x.shape
        H = N_HEADS
        D = C // H
        qkv = x @ w_qkv
        q, k, v = jnp.split(qkv, 3, axis=-1)
        to_heads = lambda t_: t_.reshape(B, T, H, D).transpose(0, 2, 1, 3)
        q, k, v = (to_heads(q), to_heads(k), to_heads(v))
        cos, sin = _rope_tables(T, D, x.dtype)
        q = _apply_rope(q, cos, sin)
        k = _apply_rope(k, cos, sin)
        scale = 1.0 / np.sqrt(D)
        att = jnp.einsum('bhtd,bhsd->bhts', q, k) * scale
        causal_mask = jnp.triu(jnp.ones((T, T), dtype=bool), 1)
        att = jnp.where(causal_mask[None, None], -jnp.inf, att)
        att = jax.nn.softmax(att, axis=-1)
        o = jnp.einsum('bhts,bhsd->bhtd', att, v)
        o = o.transpose(0, 2, 1, 3).reshape(B, T, C)
        return o @ w_out

    def _L0_ffn_ref(x, w1, b1, w2, b2):
        import jax, jax.numpy as jnp
        import numpy as np

        def _binarize(w):
            alpha = jax.lax.stop_gradient(jnp.mean(jnp.abs(w), axis=1, keepdims=True))
            bw = alpha * jnp.sign(w)
            return w + jax.lax.stop_gradient(bw - w)
        bw1 = _binarize(w1)
        h = jnp.einsum('bsd,hd->bsh', x, bw1) + b1
        h = jax.nn.gelu(h, approximate=False)
        bw2 = _binarize(w2)
        out = jnp.einsum('bsh,dh->bsd', h, bw2) + b2
        return out

    def _L1_attn_ref(x, time_mix_k, time_mix_v, time_mix_r, W_k, W_v, W_r, W_o, time_decay, time_first):
        import jax, jax.numpy as jnp
        import numpy as np
        B, T, D = (4, 1024, 256)
        NEG_CLAMP = -30.0
        EPS = 1e-09

        def _wkv_scan(k, v, w, u):
            Bn, Tn, Dn = k.shape
            p0 = jnp.full((Bn, Dn), -jnp.inf, k.dtype)
            q0 = jnp.zeros((Bn, Dn), k.dtype)

            def step(carry, kv_t):
                p, q = carry
                k_t, v_t = kv_t
                new_p = jnp.maximum(p, u + k_t)
                scale_old = jnp.exp(jnp.maximum(p - new_p, NEG_CLAMP))
                scale_cur = jnp.exp(jnp.maximum(u + k_t - new_p, NEG_CLAMP))
                wkv_t = (scale_old * q + scale_cur * v_t) / (scale_old + scale_cur + EPS)
                new_p2 = jnp.maximum(p + w, k_t)
                scale_prev = jnp.exp(jnp.maximum(p + w - new_p2, NEG_CLAMP))
                scale_new = jnp.exp(jnp.maximum(k_t - new_p2, NEG_CLAMP))
                q2 = scale_prev * q + scale_new * v_t
                return ((new_p2, q2), wkv_t)
            kT = jnp.swapaxes(k, 0, 1)
            vT = jnp.swapaxes(v, 0, 1)
            _, wkvT = jax.lax.scan(step, (p0, q0), (kT, vT))
            return jnp.swapaxes(wkvT, 0, 1)
        x_prev = jnp.pad(x[:, :-1, :], ((0, 0), (1, 0), (0, 0)))
        xk = x * time_mix_k + x_prev * (1.0 - time_mix_k)
        xv = x * time_mix_v + x_prev * (1.0 - time_mix_v)
        xr = x * time_mix_r + x_prev * (1.0 - time_mix_r)
        k = jnp.einsum('btd,ed->bte', xk, W_k)
        v = jnp.einsum('btd,ed->bte', xv, W_v)
        r = jax.nn.sigmoid(jnp.einsum('btd,ed->bte', xr, W_r))
        wkv = _wkv_scan(k, v, time_decay, time_first)
        y = r * wkv
        return jnp.einsum('btd,ed->bte', y, W_o)

    def _L1_ffn_ref(x, router, experts_gate, experts_up, experts_down, shared_gate, shared_up, shared_down):
        import jax, jax.numpy as jnp
        import numpy as np
        TOP_K = 2
        NUM_EXPERTS = 8
        b, s, h = x.shape
        E = router.shape[1]
        shared_act = jax.nn.silu(jnp.einsum('bsh,hd->bsd', x, shared_gate))
        shared_up_out = jnp.einsum('bsh,hd->bsd', x, shared_up)
        shared_out = jnp.einsum('bsd,dh->bsh', shared_act * shared_up_out, shared_down)
        router_probs = jax.nn.softmax(jnp.einsum('bsh,he->bse', x, router), axis=-1)
        topk_probs, topk_idx = jax.lax.top_k(router_probs, TOP_K)
        coef = jnp.sum(jax.nn.one_hot(topk_idx, E, dtype=x.dtype) * topk_probs[..., None], axis=2)
        coef = coef.reshape(b * s, E)
        x_flat = x.reshape(b * s, h)
        gate = jnp.einsum('th,ehd->etd', x_flat, experts_gate)
        up = jnp.einsum('th,ehd->etd', x_flat, experts_up)
        expert_out = jnp.einsum('etd,edh->eth', jax.nn.silu(gate) * up, experts_down)
        routed = jnp.einsum('eth,te->th', expert_out, coef)
        return routed.reshape(b, s, h) + shared_out
    x = L0_attn_x
    xn = _layernorm(x, axis=-1)
    x = x + _L0_attn_ref(xn, L0_attn_w_qkv, L0_attn_w_out) + _L0_ffn_ref(xn, L0_ffn_w1, L0_ffn_b1, L0_ffn_w2, L0_ffn_b2)
    xn = _layernorm(x, axis=-1)
    x = x + _L1_attn_ref(xn, L1_attn_time_mix_k, L1_attn_time_mix_v, L1_attn_time_mix_r, L1_attn_W_k, L1_attn_W_v, L1_attn_W_r, L1_attn_W_o, L1_attn_time_decay, L1_attn_time_first) + _L1_ffn_ref(xn, L1_ffn_router, L1_ffn_experts_gate, L1_ffn_experts_up, L1_ffn_experts_down, L1_ffn_shared_gate, L1_ffn_shared_up, L1_ffn_shared_down)
    return x

_drawn_inputs = setup_inputs


def setup_inputs(seed=0):
    import zlib

    import numpy as np

    out = dict(_drawn_inputs(seed))
    spreads = {}
    factors = {'L0_ffn_b1': 5.202,
     'L1_attn_time_mix_k': 8.0,
     'L1_attn_time_mix_v': 6.524,
     'L1_attn_time_mix_r': 8.0,
     'L1_attn_W_k': 8.0,
     'L1_attn_W_r': 8.0,
     'L1_attn_time_decay': 8.0,
     'L1_attn_time_first': 23.574}
    for name, (base, spread) in spreads.items():
        noise = np.random.default_rng([zlib.crc32(name.encode()), seed]).standard_normal(out[name].shape)
        drawn = base * np.exp(spread * noise) if base else spread * noise
        out[name] = jnp.asarray(drawn.astype(out[name].dtype))
    for name, factor in factors.items():
        out[name] = (out[name] * factor).astype(out[name].dtype)
    return out
```

```python
from contextlib import ExitStack

import numpy as np

import concourse.bass as bass
from concourse import mybir

F32 = mybir.dt.float32
BF16 = mybir.dt.bfloat16
F16 = mybir.dt.float16
I32 = mybir.dt.int32
ALU = mybir.AluOpType
ACT = mybir.ActivationFunctionType
AX = mybir.AxisListType

P = 128
B, T, C = 2, 2048, 256
N = B * T
KC = C // P
GT = 512
G = N // GT
TG = GT // P
HEADS, D = 16, C // 16
HG = 4
NIT = B * HEADS // HG
FF = 1024
FC = FF // P
E, ED, ES = 8, 128, 256
LN_EPS = 1e-5
LOWEST = -3.0e38
CLAMP = 30.0


class Step:

    def __init__(self, sem, credit=0, unit=1):
        self.sem, self.credit, self.unit = sem, credit, unit

    def open(self, eng):
        eng.sem_inc(self.sem, self.credit * self.unit)

    def done(self, n):
        return (n + (self.credit + 1)) * self.unit

    def freed(self, n, ring):
        return (n + (self.credit + 1 - ring)) * self.unit


class Space:

    def __init__(self, nc, ctx, phase):
        self.nc, self.ctx, self.phase = nc, ctx, phase

    def sb(self, name, shape, dt=F32):
        return self.ctx.enter_context(self.nc.sbuf_tensor(f"{self.phase}_{name}", shape, dt))

    def ps(self, name, shape, dt=F32):
        return self.ctx.enter_context(self.nc.psum_tensor(f"{self.phase}_{name}", shape, dt))

    def sem(self, name):
        return self.ctx.enter_context(self.nc.semaphore(f"{self.phase}_{name}"))

    def step(self, name, credit=0, unit=1):
        return Step(self.sem(name), credit, unit)


def parts_matmul(nc, out, weights, acts, weights_stationary=True):
    n = len(weights)
    last = None
    for k in range(n):
        (wh, wl), (xh, xl) = weights[k], acts[k]
        for m, (w, x) in enumerate(((wh, xh), (wl, xh), (wh, xl))):
            lhsT, rhs = (w, x) if weights_stationary else (x, w)
            last = nc.tensor.matmul(out, lhsT, rhs, start=(k == 0 and m == 0), stop=(k == n - 1 and m == 2))
    return last


class WeightSplit:

    STEPS, TURNS = 10, 2

    def __init__(self, s, name, width, after=None):
        self.width = width
        self.first_step = after.first_step + self.STEPS if after else 0
        self.first_turn = after.first_turn + self.TURNS if after else 0
        self.ready = self.first_step + self.STEPS
        self.w = s.sb(f"{name}_w", [P, width])
        self.hi = s.sb(f"{name}_hi", [P, width], F16)
        self.lo = s.sb(f"{name}_lo", [P, width], F16)
        self.top = s.sb(f"{name}_top", [P, 1])
        self.top_all = s.sb(f"{name}_top_all", [1, 1])
        self.power = s.sb(f"{name}_power", [P, 1])
        self.scale = s.sb(f"{name}_scale", [P, 1])
        self.unscale = s.sb(f"{name}_unscale", [P, 1])
        self.loaded = after.loaded if after else s.sem(f"{name}_loaded")
        self.found = after.found if after else s.sem(f"{name}_found")
        self.turned = after.turned if after else s.sem(f"{name}_turned")

    def vector(self, nc, dve, turn, spread, loads=1):
        dve.wait_ge(self.loaded, 16 * loads)
        nc.vector.tensor_reduce(self.top[:, :], self.w[:, :], AX.X, ALU.max,
                                apply_absolute_value=True).then_inc(self.found, 1)
        dve.wait_ge(self.turned, self.first_turn + 1)
        nc.vector.tensor_reduce(self.top_all[:, :], turn, AX.X, ALU.max).then_inc(self.found, 1)
        dve.wait_ge(self.turned, self.first_turn + 2)
        nc.vector.tensor_scalar(self.power[:, :], spread, 1e-30, None, ALU.max).then_inc(self.found, 1)
        dve.wait_ge(self.found, self.first_step + 3)
        nc.vector.tensor_scalar(self.unscale[:, :].bitcast(I32), self.power[:, :].bitcast(I32), 0x7F800000,
                                None, ALU.bitwise_and).then_inc(self.found, 1)
        dve.wait_ge(self.found, self.first_step + 4)
        nc.vector.tensor_scalar(self.scale[:, :].bitcast(I32), self.unscale[:, :].bitcast(I32), 0x7F800000,
                                None, ALU.bitwise_xor).then_inc(self.found, 1)
        dve.wait_ge(self.found, self.first_step + 5)
        nc.vector.tensor_scalar(self.scale[:, :], self.scale[:, :], 2.0 ** 12, None, ALU.mult).then_inc(self.found, 1)
        nc.vector.tensor_scalar(self.unscale[:, :], self.unscale[:, :], 2.0 ** -13, None, ALU.mult)\
            .then_inc(self.found, 1)
        dve.wait_ge(self.found, self.first_step + 7)
        nc.vector.tensor_scalar(self.w[:, :], self.w[:, :], self.scale[:, 0:1], None, ALU.mult)\
            .then_inc(self.found, 1)
        dve.wait_ge(self.found, self.first_step + 8)
        nc.vector.tensor_copy(self.hi[:, :], self.w[:, :]).then_inc(self.found, 1)
        dve.wait_ge(self.found, self.first_step + 9)
        nc.vector.tensor_tensor(self.lo[:, :], self.w[:, :], self.hi[:, :], ALU.subtract).then_inc(self.found, 1)

    def tensor(self, nc, pe, turn, spread, ident, ones):
        pe.wait_ge(self.found, self.first_step + 1)
        nc.tensor.matmul(turn, self.top[:, :], ident, start=True, stop=True).then_inc(self.turned, 1)
        pe.wait_ge(self.found, self.first_step + 2)
        nc.tensor.matmul(spread, ones, self.top_all[:, :], start=True, stop=True).then_inc(self.turned, 1)


def layernorm_phase(nc, phase, x_d, xnT_d, parts_d, ident_d):
    with ExitStack() as ctx:
        s = Space(nc, ctx, phase)
        ident = s.sb("ident", [P, P])
        xin = s.sb("xin", [P, 2, TG, C])
        stats = s.sb("stats", [P, 2, TG, 6])
        mv = s.sb("mv", [P, 2, TG, 2])
        ve = s.sb("ve", [P, 2, TG])
        sd = s.sb("sd", [P, 2, TG])
        r0 = s.sb("r0", [P, 2, TG])
        nt = s.sb("nt", [P, 2, TG])
        rstd = s.sb("rstd", [P, 2, TG])
        xn = s.sb("xn", [P, 2, TG, C])
        hi = s.sb("hi", [P, 2, KC, GT], F16)
        lo = s.sb("lo", [P, 2, KC, GT], F16)
        full = s.sb("full", [P, 2, KC, GT])
        turned = s.ps("turned", [P, 2, KC, GT])

        ident_in = s.sem("ident_in")
        x_in = [s.sem(f"x_in{p}") for p in range(2)]
        x_read = s.step("x_read", credit=2)
        stats_done = s.step("stats_done")
        mv_done = s.step("mv_done")
        ve_done = s.step("ve_done")
        sd_done = s.step("sd_done")
        past_stats = s.sem("past_stats")
        newton = s.sem("newton")
        turn_done = s.step("turn_done", credit=2)
        hi_done = s.step("hi_done", credit=2)
        lo_done = s.step("lo_done", credit=2)
        zero = s.sb("zero", [P, KC])
        zero_set = s.sem("zero_set")
        zero_stored = s.sem("zero_stored")
        stored = [s.sem(f"stored{p}") for p in range(2)]
        per_store = 2 if xnT_d is None else 3
        block = ctx.enter_context(nc.Block())

        @block.sync
        def _(sp):
            sp.dma_start(ident[:, :], ident_d).then_inc(ident_in, 16)

            def load(g, slot):
                sp.wait_ge(x_read.sem, x_read.freed(g, 2))
                src = x_d[bass.ds(g * GT, GT), :].rearrange("(j p) c -> p j c", p=P)
                sp.dma_start(xin[:, slot], src).then_inc(x_in[slot], 16)

            def store(g, slot):
                sp.wait_ge(hi_done.sem, hi_done.done(g))
                sp.wait_ge(lo_done.sem, lo_done.done(g))
                cols = bass.ds(g * GT, GT)
                for part, buf in enumerate((hi, lo)):
                    sp.dma_start(parts_d[part, :, :, cols], buf[:, slot]).then_inc(stored[slot], 16)
                if xnT_d is not None:
                    dst = xnT_d[:, :, bass.ds(g // (T // GT), 1), bass.ds(g % (T // GT) * GT + 1, GT)]
                    sp.dma_start(dst.rearrange("p k b t -> p k (b t)"), full[:, slot]).then_inc(stored[slot], 16)

            if xnT_d is not None:
                sp.wait_ge(zero_set, 1)
                with nc.allow_non_contiguous_dma(reason="a column of zeros"):
                    for b in range(B):
                        sp.dma_start(xnT_d[:, :, b, 0], zero[:, :]).then_inc(zero_stored, 16)
                sp.wait_ge(zero_stored, 16 * B)
            for slot in range(2):
                sp.sem_inc(stored[slot], 16 * per_store)
                load(slot, slot)
            with sp.Fori(0, G // 2 - 1) as i:
                for slot in range(2):
                    load(i * 2 + (slot + 2), slot)
                    store(i * 2 + slot, slot)
            for slot in range(2):
                store(G - 2 + slot, slot)
            for slot in range(2):
                sp.wait_ge(stored[slot], 16 * per_store * (G // 2 + 1))

        @block.gpsimd
        def _(pool):
            nc.gpsimd.memset(zero[:, :], 0.0).then_inc(zero_set, 1)

        @block.vector
        def _(dve):
            x_read.open(dve)
            lo_done.open(dve)

            def normalise(g, slot, use):
                dve.wait_ge(x_in[slot], use * 16 + 16)
                for j in range(TG):
                    op = nc.vector.bn_stats(stats[:, slot, j], xin[:, slot, j])
                op.then_inc(stats_done.sem, 1)
                dve.wait_ge(stats_done.sem, stats_done.done(g))
                dve.sem_inc(past_stats, 1)
                for j in range(TG):
                    op = nc.vector.bn_aggr(mv[:, slot, j], stats[:, slot, j])
                op.then_inc(mv_done.sem, 1)
                dve.wait_ge(mv_done.sem, mv_done.done(g))
                nc.vector.tensor_scalar(ve[:, slot], mv[:, slot, :, 1], LN_EPS, None, ALU.add)\
                    .then_inc(ve_done.sem, 1)
                dve.wait_ge(sd_done.sem, sd_done.done(g))
                nc.vector.reciprocal(r0[:, slot], sd[:, slot]).then_inc(newton, 1)
                dve.wait_ge(newton, g * 5 + 1)
                nc.vector.tensor_tensor(nt[:, slot], r0[:, slot], r0[:, slot], ALU.mult).then_inc(newton, 1)
                dve.wait_ge(newton, g * 5 + 2)
                nc.vector.tensor_tensor(nt[:, slot], nt[:, slot], ve[:, slot], ALU.mult).then_inc(newton, 1)
                dve.wait_ge(newton, g * 5 + 3)
                nc.vector.tensor_scalar(nt[:, slot], nt[:, slot], -0.5, 1.5, ALU.mult, ALU.add)\
                    .then_inc(newton, 1)
                dve.wait_ge(newton, g * 5 + 4)
                nc.vector.tensor_tensor(rstd[:, slot], r0[:, slot], nt[:, slot], ALU.mult).then_inc(newton, 1)
                dve.wait_ge(newton, g * 5 + 5)
                dve.wait_ge(turn_done.sem, turn_done.freed(g, 2))
                for j in range(TG):
                    op = nc.vector.tensor_scalar(xn[:, slot, j], xin[:, slot, j], mv[:, slot, j, 0:1],
                                                 rstd[:, slot, j:j + 1], ALU.subtract, ALU.mult)
                op.then_inc(x_read.sem, 1)

            def low_parts(g, slot, use):
                dve.wait_ge(hi_done.sem, hi_done.done(g))
                dve.wait_ge(stored[slot], use * (16 * per_store) + 16 * per_store)
                for k in range(KC):
                    op = nc.vector.tensor_tensor(lo[:, slot, k], turned[:, slot, k], hi[:, slot, k], ALU.subtract)
                op.then_inc(lo_done.sem, 1)

            normalise(0, 0, 0)
            with dve.Fori(0, G // 2 - 1) as i:
                normalise(i * 2 + 1, 1, i)
                low_parts(i * 2, 0, i)
                normalise(i * 2 + 2, 0, i + 1)
                low_parts(i * 2 + 1, 1, i)
            normalise(G - 1, 1, G // 2 - 1)
            low_parts(G - 2, 0, G // 2 - 1)
            low_parts(G - 1, 1, G // 2 - 1)

        @block.scalar
        def _(act):
            hi_done.open(act)
            with act.Fori(0, G // 2) as i:
                for slot in range(2):
                    g = i * 2 + slot
                    act.wait_ge(ve_done.sem, ve_done.done(g))
                    nc.scalar.activation(sd[:, slot], ve[:, slot], ACT.Sqrt).then_inc(sd_done.sem, 1)
                    act.wait_ge(turn_done.sem, turn_done.done(g))
                    act.wait_ge(stored[slot], i * (16 * per_store) + 16 * per_store)
                    if xnT_d is not None:
                        for k in range(KC):
                            nc.scalar.copy(full[:, slot, k], turned[:, slot, k])
                    for k in range(KC):
                        op = nc.scalar.copy(hi[:, slot, k], turned[:, slot, k])
                    op.then_inc(hi_done.sem, 1)

        @block.tensor
        def _(pe):
            turn_done.open(pe)
            pe.wait_ge(ident_in, 16)
            with pe.Fori(0, G // 2) as i:
                for slot in range(2):
                    g = i * 2 + slot
                    pe.wait_ge(x_read.sem, x_read.done(g))
                    pe.wait_ge(lo_done.sem, lo_done.freed(g, 2))
                    for k in range(KC):
                        for j in range(TG):
                            op = nc.tensor.transpose(turned[:, slot, k, j * P:(j + 1) * P],
                                                     xn[:, slot, j, k * P:(k + 1) * P], ident[:, :])
                    op.then_inc(turn_done.sem, 1)


def qkv_phase(nc, parts_d, w_qkv_d, cos_d, sin_d, ident_d, qk_d, va_d):
    W3 = 3 * C
    CH = 4
    QG = T // GT
    swap = [j ^ 1 for j in range(32)]
    with ExitStack() as ctx:
        s = Space(nc, ctx, "qkv")
        w = WeightSplit(s, "w_qkv", KC * W3)
        ident = s.sb("ident", [P, P])
        ones = s.sb("ones", [1, P])
        cos = s.sb("cos", [P, T])
        sin = s.sb("sin", [P, T])
        x = s.sb("x", [P, 2, 2, KC, GT], F16)
        raw = s.sb("raw", [P, 2, GT])
        swapped = s.sb("swapped", [P, 2, GT])
        by_cos = s.sb("by_cos", [P, 2, GT])
        by_sin = s.sb("by_sin", [P, 2, GT])
        rot = s.sb("rot", [P, 2, GT])
        rest = s.sb("rest", [P, 2, GT])
        parts = s.sb("parts", [P, 2, 3, GT], BF16)
        v = s.sb("v", [P, 2, TG, HEADS, 2 * D])
        qk_ps = s.ps("qk_ps", [P, CH, GT])
        v_ps = s.ps("v_ps", [P, TG, C])
        cells = s.ps("cells", [P, GT])

        const_in = s.sem("const_in")
        set_done = s.sem("set_done")
        x_in = [s.sem(f"x_in{p}") for p in range(2)]
        qk_done = s.step("qk_done")
        v_done = s.step("v_done", credit=2)
        raw_done = s.step("raw_done", credit=CH)
        v_copied = s.step("v_copied", credit=1)
        swap_done = s.step("swap_done", credit=2)
        passed = s.sem("passed")
        past_raw = s.sem("past_raw")
        cos_done = s.step("cos_done", credit=2)
        sin_done = s.step("sin_done", credit=2)
        rot_done = s.step("rot_done", credit=2)
        hi_done = s.step("hi_done")
        rest_done = s.step("rest_done")
        mid_done = s.step("mid_done")
        parts_done = s.step("parts_done")
        qk_stored = [s.sem(f"qk_stored{p}") for p in range(2)]
        v_stored = [s.sem(f"v_stored{p}") for p in range(2)]
        QK_STORE, V_STORE = 16, 16 * (HEADS // HG)
        block = ctx.enter_context(nc.Block())

        @block.sync
        def _(sp):
            sp.dma_start(w.w[:, :].rearrange("p (k n) -> p k n", k=KC),
                         w_qkv_d.rearrange("(k p) n -> p k n", p=P)).then_inc(w.loaded, 16)
            for dst, src in ((ident, ident_d), (cos, cos_d), (sin, sin_d)):
                sp.dma_start(dst[:, :], src).then_inc(const_in, 16)

            def load(g, slot):
                sp.wait_ge(v_done.sem, v_done.freed(g, 2))
                for part in range(2):
                    sp.dma_start(x[:, slot, part], parts_d[part, :, :, bass.ds(g * GT, GT)]).then_inc(x_in[slot], 16)

            def store(b, q):
                g = b * QG + q
                for m in range(CH):
                    sp.wait_ge(parts_done.sem, parts_done.done(g * CH + m))
                    dst = qk_d[m // 2, m % 2 * P:(m % 2 + 1) * P, :, bass.ds(g * GT, GT)]
                    sp.dma_start(dst, parts[:, m % 2]).then_inc(qk_stored[m % 2], 16)
                sp.wait_ge(v_copied.sem, v_copied.done(g))
                for hg in range(HEADS // HG):
                    dst = va_d[bass.ds(b * (HEADS // HG) + hg, 1), :, q * TG:(q + 1) * TG, :]
                    sp.dma_start(dst.rearrange("o p j n -> (o p) j n"),
                                 v[:, q % 2, :, hg * HG:(hg + 1) * HG, :].rearrange("p j h n -> p j (h n)"))\
                        .then_inc(v_stored[q % 2], 16)

            for slot in range(2):
                sp.sem_inc(qk_stored[slot], QK_STORE)
                sp.sem_inc(v_stored[slot], V_STORE)
                load(slot, slot)
            with sp.Fori(0, B - 1) as b:
                for q in range(QG):
                    store(b, q)
                    load(b * QG + (q + 2), q % 2)
            for q in range(QG):
                store(B - 1, q)
                if q + 2 < QG:
                    load((B - 1) * QG + q + 2, q % 2)
            for slot in range(2):
                sp.wait_ge(qk_stored[slot], QK_STORE * (1 + G * CH // 2))
                sp.wait_ge(v_stored[slot], V_STORE * (1 + G // 2))

        @block.gpsimd
        def _(pool):
            cos_done.open(pool)
            sin_done.open(pool)
            nc.gpsimd.memset(ones[:, :], 1.0)
            nc.gpsimd.memset(v[:, :, :, :, D:], 1.0).then_inc(set_done, 1)
            pool.wait_ge(const_in, 48)
            with pool.Fori(0, B) as b:
                for q in range(QG):
                    at = slice(q * GT, (q + 1) * GT)
                    for m in range(CH):
                        n = b * (QG * CH) + (q * CH + m)
                        pool.wait_ge(raw_done.sem, raw_done.done(n))
                        pool.wait_ge(rot_done.sem, rot_done.freed(n, 2))
                        pool.sem_inc(passed, 1)
                        nc.gpsimd.tensor_tensor(by_cos[:, m % 2], raw[:, m % 2], cos[:, at], ALU.mult).then_inc(cos_done.sem, 1)
                        pool.wait_ge(swap_done.sem, swap_done.done(n))
                        pool.sem_inc(passed, 1)
                        nc.gpsimd.tensor_tensor(by_sin[:, m % 2], swapped[:, m % 2], sin[:, at], ALU.mult).then_inc(sin_done.sem, 1)

        @block.vector
        def _(dve):
            swap_done.open(dve)
            rot_done.open(dve)
            w.vector(nc, dve, cells[0:1, 0:P], cells[:, P:P + 1])

            def exchange(n, m):
                dve.wait_ge(raw_done.sem, raw_done.done(n))
                dve.wait_ge(sin_done.sem, sin_done.freed(n, 2))
                dve.sem_inc(past_raw, 1)
                nc.vector.stream_shuffle(swapped[:, m % 2], raw[:, m % 2], swap).then_inc(swap_done.sem, 1)

            def finish(n, m, use):
                c = m % 2
                dve.wait_ge(cos_done.sem, cos_done.done(n))
                dve.wait_ge(sin_done.sem, sin_done.done(n))
                nc.vector.tensor_tensor(rot[:, c], by_cos[:, c], by_sin[:, c], ALU.add).then_inc(rot_done.sem, 1)
                dve.wait_ge(rot_done.sem, rot_done.done(n))
                dve.wait_ge(qk_stored[c], use * QK_STORE + QK_STORE)
                nc.vector.tensor_copy(parts[:, c, 0], rot[:, c]).then_inc(hi_done.sem, 1)
                dve.wait_ge(hi_done.sem, hi_done.done(n))
                nc.vector.tensor_tensor(rest[:, c], rot[:, c], parts[:, c, 0], ALU.subtract).then_inc(rest_done.sem, 1)
                dve.wait_ge(rest_done.sem, rest_done.done(n))
                nc.vector.tensor_copy(parts[:, c, 1], rest[:, c]).then_inc(mid_done.sem, 1)
                dve.wait_ge(mid_done.sem, mid_done.done(n))
                nc.vector.tensor_tensor(parts[:, c, 2], rest[:, c], parts[:, c, 1], ALU.subtract)\
                    .then_inc(parts_done.sem, 1)

            with dve.Fori(0, B) as b:
                for q in range(QG):
                    for m in range(CH + 1):
                        n = b * (QG * CH) + (q * CH + m)
                        if m < CH:
                            exchange(n, m)
                        if m > 0:
                            finish(n - 1, m - 1, b * (QG * CH // 2) + (q * CH + m - 1) // 2)

        @block.scalar
        def _(act):
            raw_done.open(act)
            v_copied.open(act)
            act.wait_ge(w.found, w.ready)
            act.wait_ge(set_done, 1)
            with act.Fori(0, B) as b:
                for q in range(QG):
                    g = b * QG + q
                    for m in range(CH):
                        n = g * CH + m
                        act.wait_ge(qk_done.sem, qk_done.done(n))
                        act.wait_ge(swap_done.sem, swap_done.freed(n, 2))
                        act.wait_ge(cos_done.sem, cos_done.freed(n, 2))
                        nc.scalar.activation(raw[:, m % 2], qk_ps[:, m], ACT.Identity, scale=w.unscale[:, 0:1])\
                            .then_inc(raw_done.sem, 1)
                    act.wait_ge(v_done.sem, v_done.done(g))
                    act.wait_ge(v_stored[q % 2], (b * (QG // 2) + q // 2) * V_STORE + V_STORE)
                    nc.scalar.activation(v[:, q % 2, :, :, 0:D].rearrange("p j h d -> p (j h) d"),
                                         v_ps[:, :, :].rearrange("p j (h d) -> p (j h) d", d=D),
                                         ACT.Identity, scale=w.unscale[:, 0:1]).then_inc(v_copied.sem, 1)

        @block.tensor
        def _(pe):
            v_done.open(pe)
            pe.wait_ge(const_in, 48)
            pe.wait_ge(set_done, 1)
            w.tensor(nc, pe, cells[0:1, 0:P], cells[:, P:P + 1], ident[:, :], ones[:, :])
            pe.wait_ge(w.found, w.ready)

            def weight(k, cols):
                at = slice(k * W3 + cols.start, k * W3 + cols.stop)
                return w.hi[:, at], w.lo[:, at]

            with pe.Fori(0, B) as b:
                for q in range(QG):
                    g = b * QG + q
                    pe.wait_ge(x_in[q % 2], (b * (QG // 2) + q // 2) * 32 + 32)
                    for m in range(CH):
                        n = g * CH + m
                        pe.wait_ge(raw_done.sem, raw_done.freed(n, CH))
                        parts_matmul(nc, qk_ps[:, m], [weight(k, slice(m * P, (m + 1) * P)) for k in range(KC)],
                                     [(x[:, q % 2, 0, k], x[:, q % 2, 1, k]) for k in range(KC)])\
                            .then_inc(qk_done.sem, 1)
                    pe.wait_ge(v_copied.sem, v_copied.freed(g, 1))
                    for j in range(TG):
                        at = slice(j * P, (j + 1) * P)
                        op = parts_matmul(nc, v_ps[:, j], [weight(k, slice(2 * C, 3 * C)) for k in range(KC)],
                                          [(x[:, q % 2, 0, k, at], x[:, q % 2, 1, k, at]) for k in range(KC)],
                                          weights_stationary=False)
                    op.then_inc(v_done.sem, 1)


def attention_phase(nc, qk_d, va_d, ident_d, tri_d, o_d, den_d):
    ROWS = 6 * D
    MROWS = 2
    QB, KB = T // GT, T // P
    HP = HG // 2
    steps = [(t, j) for t in range(QB) for j in range(TG * (t + 1))]
    NS, NP = len(steps), len(steps) * HP
    last_step = [max(i for i, (t, _) in enumerate(steps) if t == u) for u in range(QB)]
    diagonal = [i for i, (t, j) in enumerate(steps) if j >= TG * t]
    MXR, SCR = 3, 4
    LATE = QB - 1
    LATE_TO = 18

    def chunks(t):
        return [("chunk", t, tt, h, c) for tt in range(TG * t, TG * (t + 1)) for h in range(HG) for c in range(t + 1)]

    def with_turn(t, turned):
        own = chunks(t)
        return own[:MXR] + [("turn", turned)] + own[MXR:]

    late = with_turn(LATE, LATE - 1)
    early = [e for t in range(LATE) for e in with_turn(t, (t - 1) % QB)]
    period = late + early
    ahead = [e for e in early if e != ("turn", LATE)]
    NA, NE = len(ahead), len(period)
    bank_of = {e: i % MXR for i, e in enumerate(period)}

    def entry_done(it, i):
        return it * NE + (NA + i + 1)

    def bank_freed(it, i):
        before = [k for k in range(i) if bank_of[period[k]] == bank_of[period[i]]]
        if before:
            return entry_done(it, before[-1])
        return it * NE + (NA - NE) + 1 + max(k for k in range(NE) if bank_of[period[k]] == bank_of[period[i]])

    def spread_entries():
        def pace(pairs, entries):
            work = np.cumsum([GT - max(0, steps[r // HP][1] - TG * steps[r // HP][0]) * P for r in pairs])
            cost = np.cumsum([1.0 if e[0] == "turn" or e[4] < e[2] // TG else 0.2 + 0.2 * (e[2] % TG + 1)
                              for e in entries])
            place = np.searchsorted(work / work[-1], cost / cost[-1] - 1e-9)
            return [pairs[k] for k in place]

        at = pace(range(LATE_TO * HP), late) + pace(range(LATE_TO * HP, NP), early)
        return [[i for i, r in enumerate(at) if r == k] for k in range(NP)]

    spots = spread_entries()
    SCALE = float(D) ** -0.5
    with ExitStack() as ctx:
        s = Space(nc, ctx, "att")
        qop = s.sb("qop", [P, 2, QB, HG, GT], BF16)
        kop = s.sb("kop", [P, 2, HG, T], BF16)
        v = s.sb("v", [P, 2, KB, HG * 2 * D])
        prob = s.sb("prob", [P, 4, 2, GT])
        o = s.sb("o", [P, 2, GT])
        ident = s.sb("ident", [P, P])
        tri = s.sb("tri", [P, GT])
        scratch = s.sb("scratch", [P, SCR, GT], BF16)
        m_part = s.sb("m_part", [P, HG, KB, QB])
        neg_m = s.sb("neg_m", [P, 2, P])
        m_row = s.sb("m_row", [HG * TG, 2, MROWS, P], BF16)
        score = s.ps("score", [P, 2, 2, GT])
        mx = s.ps("mx", [P, MXR, GT])
        pv = s.ps("pv", [P, GT])

        const_in = s.sem("const_in")
        ones_set = s.sem("ones_set")
        qkv_in = [s.sem(f"qkv_in{p}") for p in range(2)]
        m_in = [s.sem(f"m_in{t}") for t in range(QB)]
        score_done = s.step("score_done")
        exp_done = s.step("exp_done", credit=2)
        masked = s.step("masked")
        passed = s.sem("passed")
        passed_pe = s.sem("passed_pe")
        pv_done = s.step("pv_done", credit=2)
        o_copied = s.step("o_copied", credit=1)
        mx_done = s.sem("mx_done")
        m_found = s.sem("m_found")
        past_mx = s.sem("past_mx")
        m_reduced = s.step("m_reduced", credit=QB)
        m_high = s.step("m_high")
        o_stored = [s.sem(f"o_stored{p}") for p in range(2)]
        LOADS = 16 * (6 * (1 + QB) + 1)
        O_STORE = 16 * (HG + 1)
        block = ctx.enter_context(nc.Block())

        def schedule(eng, iteration, first):
            first()
            with eng.Fori(0, NIT // 2 - 1) as i:
                iteration(i * 2, 0, i, True, True)
                iteration(i * 2 + 1, 1, i, True, True)
            iteration(NIT - 2, 0, NIT // 2 - 1, True, False)
            iteration(NIT - 1, 1, NIT // 2 - 1, False, False)

        def walk(eng, entry):
            def first():
                for i, e in enumerate(ahead):
                    entry(0, e, i + 1)

            def iteration(it, slot, use, with_next, with_load):
                for i, e in enumerate(period):
                    own = i < len(late) or e == ("turn", LATE)
                    if own or with_next:
                        count = entry_done(it, i if i < len(late) or with_next else len(late))
                        entry(it if own else it + 1, e, count)

            schedule(eng, iteration, first)

        @block.sync
        def _(sp):
            for dst, src in ((ident, ident_d), (tri, tri_d)):
                sp.dma_start(dst[:, :], src).then_inc(const_in, 16)

            def load(b, hg, slot):
                toks, rows = bass.ds(b * T, T), bass.ds(hg * (HG * D), HG * D)
                for row, (kp, qp) in enumerate((i, j) for i in range(3) for j in range(3 - i)):
                    at = slice(row * D, (row + 1) * D)
                    sp.dma_start(kop[at, slot], qk_d[1, rows, kp, toks].rearrange("(h d) t -> d h t", d=D))\
                        .then_inc(qkv_in[slot], 16)
                    for t in range(QB):
                        toks_t = bass.ds(b * T + t * GT, GT)
                        sp.dma_start(qop[at, slot, t], qk_d[0, rows, qp, toks_t].rearrange("(h d) t -> d h t", d=D))\
                            .then_inc(qkv_in[slot], 16)
                sp.dma_start(v[:, slot].rearrange("p j n -> p (j n)"),
                              va_d[bass.ds(b * (HEADS // HG) + hg, 1)].rearrange("o p j n -> (o p) (j n)"))\
                    .then_inc(qkv_in[slot], 16)

            def send_m(it, slot, t, own, with_next=True):
                i = period.index(("turn", t)) if with_next else len(late)
                sp.wait_ge(m_found, entry_done(it, i if own else i - NE))
                for part in range(MROWS):
                    row = qop[ROWS + part:ROWS + part + 1, slot, t]
                    sp.dma_start(row.rearrange("o h (j t) -> o (h j) t", t=P),
                                 m_row[:, t % 2, part, :]).then_inc(m_in[t], 16)

            def store(it, t):
                b, hg = it // (HEADS // HG), it % (HEADS // HG)
                sp.wait_ge(o_copied.sem, o_copied.done(it * QB + t))
                toks = bass.ds(b * T + t * GT, GT)
                for h in range(HG):
                    sp.dma_start(o_d[bass.ds((hg * HG + h) * D, D), toks], o[2 * D * h:2 * D * h + D, t % 2])\
                        .then_inc(o_stored[t % 2], 16)
                sp.dma_start(den_d[bass.ds(hg * HG, HG), toks], o[D:P:2 * D, t % 2]).then_inc(o_stored[t % 2], 16)

            def first():
                for slot in range(2):
                    sp.sem_inc(o_stored[slot], O_STORE)
                    load(0, slot, slot)
                for t in range(QB):
                    sp.sem_inc(m_in[t], 16 * MROWS)
                for t in range(LATE - 1):
                    send_m(0, 0, t, False)

            def iteration(it, slot, use, with_next, with_load):
                send_m(it, slot, LATE - 1, True)
                store(it, 0)
                store(it, 1)
                send_m(it, slot, LATE, True, with_next)
                store(it, 2)
                if with_next:
                    for t in range(LATE - 1):
                        send_m(it + 1, 1 - slot, t, False)
                store(it, 3)
                if with_load:
                    sp.wait_ge(pv_done.sem, pv_done.done(it * NS + (NS - 1)))
                    nxt = it + 2
                    load(nxt // (HEADS // HG), nxt % (HEADS // HG), slot)

            schedule(sp, iteration, first)
            for slot in range(2):
                sp.wait_ge(o_stored[slot], O_STORE * (1 + NIT * QB // 2))

        @block.gpsimd
        def _(pool):
            nc.gpsimd.memset(kop[ROWS:ROWS + MROWS], 1.0).then_inc(ones_set, 1)

            def iteration(it, slot, use, with_next, with_load):
                for i, st in enumerate(diagonal):
                    t, j = steps[st]
                    n0 = (j - TG * t) * P
                    for hp in range(HP):
                        r = st * HP + hp
                        pool.wait_ge(exp_done.sem, exp_done.done(it * NP + r))
                        pool.sem_inc(passed, 1)
                        at = prob[:, r % 4, :, n0:n0 + P]
                        nc.gpsimd.affine_select(out=at, in_=at, compare_op=ALU.is_ge, fill=0.0, base=0,
                                                pattern=[[0, 2], [1, P]], channel_multiplier=-1)\
                            .then_inc(masked.sem, 1)

            schedule(pool, iteration, lambda: None)

        @block.vector
        def _(dve):
            m_reduced.open(dve)
            nc.vector.memset(m_part[:], LOWEST)
            nc.vector.memset(neg_m[:], 0.0).then_inc(ones_set, 1)
            dve.wait_ge(const_in, 32)
            dve.wait_ge(ones_set, 2)

            def entry(it, e, count):
                dve.wait_ge(mx_done, count)
                if e[0] == "turn":
                    t = e[1]
                    rows = mx[0:HG * TG, bank_of[e], 0:P]
                    dve.wait_ge(m_in[(t - 2) % QB], (it + (t // 2 + 1)) * (16 * MROWS))
                    nc.vector.tensor_copy(m_row[:, t % 2, 0, :], rows).then_inc(m_high.sem, 1)
                    dve.wait_ge(m_high.sem, m_high.done(it * QB + t))
                    nc.vector.tensor_tensor(m_row[:, t % 2, 1, :], rows, m_row[:, t % 2, 0, :], ALU.subtract)\
                        .then_inc(m_found, 1)
                    return
                _, t, tt, h, c = e
                first, last = chunks(t)[0], chunks(t)[-1]
                cell = m_part[:, h, tt, c:c + 1]
                bank = mx[:, bank_of[e]]
                if e == first:
                    dve.wait_ge(m_reduced.sem, m_reduced.freed(it * QB + t, QB))
                if c < tt // TG:
                    nc.vector.tensor_reduce(cell, bank, AX.X, ALU.max).then_inc(m_found, 1)
                else:
                    w = (tt % TG + 1) * P
                    dve.wait_ge(m_found, count - SCR) if not isinstance(count, int) or count > SCR else None
                    dve.sem_inc(past_mx, 1)
                    nc.vector.tensor_tensor_reduce(scratch[:, period.index(e) % SCR, 0:w], bank[:, 0:w], tri[:, GT - w:GT],
                                                   1.0, LOWEST, ALU.add, ALU.max, cell).then_inc(m_found, 1)
                if e == last:
                    dve.wait_ge(m_found, count)
                    nc.vector.tensor_reduce(
                        neg_m[:, t % 2, 0:HG * TG].rearrange("p (h j) -> p h j", h=HG),
                        m_part[:, :, TG * t:TG * (t + 1), :], AX.X, ALU.max, negate=True).then_inc(m_reduced.sem, 1)

            walk(dve, entry)

        @block.scalar
        def _(act):
            exp_done.open(act)
            o_copied.open(act)

            def iteration(it, slot, use, with_next, with_load):
                def copy_out(t):
                    act.wait_ge(pv_done.sem, pv_done.done(it * NS + last_step[t]))
                    act.wait_ge(o_stored[t % 2], it * (O_STORE * QB // 2) + (t // 2 + 1) * O_STORE)
                    nc.scalar.copy(o[:, t % 2], pv[:, :]).then_inc(o_copied.sem, 1)

                for st, (t, j) in enumerate(steps):
                    n0 = max(0, j - TG * t) * P
                    act.wait_ge(pv_done.sem, pv_done.freed(it * NS + st, 2))
                    for hp in range(HP):
                        r = st * HP + hp
                        act.wait_ge(score_done.sem, score_done.done(it * NP + r))
                        nc.scalar.activation(prob[:, r % 4, :, n0:], score[:, r % 2, :, n0:], ACT.Exp, scale=SCALE)\
                            .then_inc(exp_done.sem, 1)
                    if st - 1 in last_step:
                        copy_out(t - 1)
                copy_out(QB - 1)

            schedule(act, iteration, lambda: None)

        @block.tensor
        def _(pe):
            pv_done.open(pe)

            def entry(it, slot, e, freed):
                if freed is not None:
                    pe.wait_ge(m_found, freed)
                if e[0] == "turn":
                    t = e[1]
                    pe.wait_ge(m_reduced.sem, m_reduced.done(it * QB + t))
                    pe.sem_inc(passed_pe, 1)
                    nc.tensor.transpose(mx[:, bank_of[e], 0:P], neg_m[:, t % 2], ident[:, :]).then_inc(mx_done, 1)
                    return
                _, t, tt, h, c = e
                w = GT if c < tt // TG else (tt % TG + 1) * P
                nc.tensor.matmul(mx[:, bank_of[e], 0:w], qop[0:ROWS, slot, t, h, (tt - TG * t) * P:(tt - TG * t + 1) * P],
                                 kop[0:ROWS, slot, h, c * GT:c * GT + w], start=True, stop=True).then_inc(mx_done, 1)

            def first():
                pe.wait_ge(const_in, 32)
                pe.wait_ge(ones_set, 2)
                pe.wait_ge(qkv_in[0], LOADS)
                for i, e in enumerate(ahead):
                    before = [k for k in range(i) if bank_of[ahead[k]] == bank_of[e]]
                    entry(0, 0, e, before[-1] + 1 if before else None)

            def iteration(it, slot, use, with_next, with_load):
                pe.wait_ge(qkv_in[slot], use * LOADS + LOADS)
                def products(st):
                    t, j = steps[st]
                    n0 = max(0, j - TG * t) * P
                    if j == 0:
                        pe.wait_ge(o_copied.sem, o_copied.freed(it * QB + t, 1))
                    if st in diagonal:
                        pe.wait_ge(masked.sem, masked.done(it * (len(diagonal) * HP) + (diagonal.index(st) * HP + HP - 1)))
                    else:
                        pe.wait_ge(exp_done.sem, exp_done.done(it * NP + (st * HP + HP - 1)))
                    for h in range(HG):
                        at = slice(2 * D * h, 2 * D * (h + 1))
                        op = nc.tensor.matmul(pv[at, n0:], v[:, slot, j, at], prob[:, (st * HP + h // 2) % 4, h % 2, n0:],
                                              start=(j == 0), stop=(j == TG * (t + 1) - 1))
                    op.then_inc(pv_done.sem, 1)

                for st, (t, j) in enumerate(steps):
                    n0 = max(0, j - TG * t) * P
                    if j == 0:
                        pe.wait_ge(m_in[t], it * (16 * MROWS) + 2 * (16 * MROWS))
                    for hp in range(HP):
                        r = st * HP + hp
                        pe.wait_ge(exp_done.sem, exp_done.freed(it * NP + r, 2))
                        for hh in range(2):
                            op = nc.tensor.matmul(score[:, r % 2, hh, n0:],
                                                  kop[0:ROWS + MROWS, slot, hp * 2 + hh, j * P:(j + 1) * P],
                                                  qop[0:ROWS + MROWS, slot, t, hp * 2 + hh, n0:],
                                                  start=True, stop=True)
                        op.then_inc(score_done.sem, 1)
                        if r == LATE_TO * HP:
                            if with_next:
                                pe.wait_ge(qkv_in[1 - slot], (use + slot + 1) * LOADS)
                            else:
                                entry(it, slot, ("turn", LATE), entry_done(it, len(late) - 1))
                        for i in spots[r]:
                            e = period[i]
                            own = i < len(late) or e == ("turn", LATE)
                            if i < len(late) or with_next:
                                entry(it if own else it + 1, slot if own else 1 - slot, e, bank_freed(it, i))
                    if st > 0:
                        products(st - 1)
                products(NS - 1)

            schedule(pe, iteration, first)


def rolling(eng, step, depth=2, n=G):
    lead = depth - 1
    pairs = (n - lead) // 2

    def peeled(m):
        step([(m - k, (m - k) % 2, (m - k) // 2) if 0 <= m - k < n else None for k in range(depth)])

    for m in range(lead):
        peeled(m)
    with eng.Fori(0, pairs) as i:
        for r in range(2):
            at = [lead + r - k for k in range(depth)]
            step([(i * 2 + a, a % 2, i + a // 2) for a in at])
    for m in range(lead + 2 * pairs, n + lead):
        peeled(m)


def streamed(eng, ahead, behind, n=G):
    ahead(0, 0, 0)
    with eng.Fori(0, n // 2 - 1) as i:
        ahead(i * 2 + 1, 1, i)
        behind(i * 2, 0, i)
        ahead(i * 2 + 2, 0, i + 1)
        behind(i * 2 + 1, 1, i)
    ahead(n - 1, 1, n // 2 - 1)
    behind(n - 2, 0, n // 2 - 1)
    behind(n - 1, 1, n // 2 - 1)


def in_groups(eng, each, n=G):
    with eng.Fori(0, n // 2) as i:
        for slot in range(2):
            each(i * 2 + slot, slot, i)


def prefetched(sp, load, store, n=G):
    load(0, 0)
    load(1, 1)
    with sp.Fori(0, n // 2 - 1) as i:
        for slot in range(2):
            load(i * 2 + (slot + 2), slot)
            store(i * 2 + slot, slot)
    store(n - 2, 0)
    store(n - 1, 1)


def ffn_phase(nc, x_d, parts_d, o_d, den_d, rden_d, w1_d, b1_d, w2_d, b2_d, w_out_d, ident_d, x1_d):
    HB = 2
    with ExitStack() as ctx:
        s = Space(nc, ctx, "ffn")
        ident = s.sb("ident", [P, P])
        den = s.sb("den", [P, HEADS * N // P])
        rden = s.sb("rden", [P, HEADS * N // P])
        w1 = s.sb("w1", [P, FC, C])
        w2 = s.sb("w2", [P, KC, FF])
        sign1 = s.sb("sign1", [P, FC, C])
        sign2 = s.sb("sign2", [P, KC, FF])
        a1 = s.sb("a1", [P, FC])
        a2 = s.sb("a2", [P, KC])
        b1 = s.sb("b1", [P, FC])
        b2 = s.sb("b2", [P, C])
        w1T = s.sb("w1T", [P, KC, FF], F16)
        w2T = s.sb("w2T", [P, FC, C])
        wo = s.sb("wo", [P, KC, C])
        xp = s.sb("xp", [P, 2, 2, KC, GT], F16)
        o = s.sb("o", [P, 2, KC, GT])
        rd = s.sb("rd", [P, 2, KC, GT])
        att = s.sb("att", [P, 2, KC, GT])
        xin = s.sb("xin", [P, 2, TG, C])
        xb = s.sb("xb", [P, 2, TG, C])
        hid = s.sb("hid", [P, 2, FC, GT])
        x1 = s.sb("x1", [P, 2, TG, C])
        hid_ps = s.ps("hid_ps", [P, HB, GT])
        out_ps = s.ps("out_ps", [P, 2, TG, C])
        turn_ps = s.ps("turn_ps", [P, GT])

        den_in, rden_done, rden_out = s.sem("den_in"), s.sem("rden_done"), s.sem("rden_out")
        w_in = s.sem("w_in")
        mean_done = s.sem("mean_done")
        sign_done = s.sem("sign_done")
        scaled = s.sem("scaled")
        w_turned = s.step("w_turned")
        w_copied = s.step("w_copied", credit=1)
        g_in = [s.sem(f"g_in{p}") for p in range(2)]
        att_done = s.step("att_done", credit=2)
        xb_done = s.step("xb_done", credit=2)
        past_wait = s.sem("past_wait")
        past_in = s.sem("past_in")
        hid_done = s.step("hid_done", credit=2 * FC)
        gelu_done = s.step("gelu_done", credit=2)
        out_done = s.step("out_done", credit=2)
        x1_done = s.step("x1_done", credit=2)
        x1_out = [s.sem(f"x1_out{p}") for p in range(2)]
        LOADS = 16 * (2 + 1 + KC + 1)
        WLOADS = 16 * 6
        turns = [(0, m) for m in range(0, FC * KC, 4)] + [(1, m) for m in range(0, FC * KC, 4)]
        block = ctx.enter_context(nc.Block())

        @block.sync
        def _(sp):
            rows = den_d.rearrange("h (q t) -> (h q) t", q=P // HEADS)
            sp.dma_start(den[:, :], rows).then_inc(den_in, 16)
            sp.dma_start(ident[:, :], ident_d).then_inc(w_in, 16)
            sp.dma_start(w1[:, :, :], w1_d.rearrange("(m p) c -> p m c", p=P)).then_inc(w_in, 16)
            sp.dma_start(w2[:, :, :], w2_d.rearrange("(k p) n -> p k n", p=P)).then_inc(w_in, 16)
            sp.dma_start(wo[:, :, :], w_out_d.rearrange("(k p) n -> p k n", p=P)).then_inc(w_in, 16)
            with nc.allow_non_contiguous_dma(reason="one value per partition"):
                sp.dma_start(b1[:, :], b1_d.rearrange("(m p) -> p m", p=P)).then_inc(w_in, 16)
            sp.dma_start(b2[:, :], b2_d.rearrange("(o c) -> o c", o=1).broadcast_to([P, C])).then_inc(w_in, 16)
            sp.wait_ge(rden_done, 1)
            sp.dma_start(rden_d.rearrange("h (q t) -> (h q) t", q=P // HEADS), rden[:, :]).then_inc(rden_out, 16)
            sp.wait_ge(rden_out, 16)

            def load(g, slot):
                sp.wait_ge(hid_done.sem, hid_done.freed(g * FC + (FC - 1), 2 * FC))
                sp.sem_inc(past_wait, 1)
                sp.wait_ge(att_done.sem, att_done.freed(g, 2))
                sp.wait_ge(xb_done.sem, xb_done.freed(g, 2))
                toks = bass.ds(g * GT, GT)
                for part in range(2):
                    sp.dma_start(xp[:, slot, part], parts_d[part, :, :, toks]).then_inc(g_in[slot], 16)
                sp.dma_start(o[:, slot], o_d[:, toks].rearrange("(k p) t -> p k t", p=P)).then_inc(g_in[slot], 16)
                for k in range(KC):
                    heads = rden_d[k * P // D:(k + 1) * P // D, toks]
                    sp.dma_start(rd[:, slot, k], heads.unsqueeze(1).broadcast_to([P // D, D, GT]))\
                        .then_inc(g_in[slot], 16)
                sp.dma_start(xin[:, slot], x_d[toks, :].rearrange("(j p) c -> p j c", p=P)).then_inc(g_in[slot], 16)

            def store(g, slot):
                sp.wait_ge(x1_done.sem, x1_done.done(g))
                sp.dma_start(x1_d[bass.ds(g * GT, GT), :].rearrange("(j p) c -> p j c", p=P), x1[:, slot])\
                    .then_inc(x1_out[slot], 16)

            for slot in range(2):
                sp.sem_inc(x1_out[slot], 16)
            prefetched(sp, load, store)
            for slot in range(2):
                sp.wait_ge(x1_out[slot], 16 * (1 + G // 2))

        @block.gpsimd
        def _(pool):
            att_done.open(pool)
            xb_done.open(pool)
            pool.wait_ge(w_in, WLOADS)

            def each(g, slot, use):
                pool.wait_ge(g_in[slot], use * LOADS + LOADS)
                pool.wait_ge(out_done.sem, out_done.freed(g, 2))
                pool.wait_ge(x1_done.sem, x1_done.freed(g, 2))
                pool.sem_inc(past_in, 1)
                nc.gpsimd.tensor_tensor(att[:, slot], o[:, slot], rd[:, slot], ALU.mult)\
                    .then_inc(att_done.sem, 1)
                for j in range(TG):
                    op = nc.gpsimd.tensor_tensor(xb[:, slot, j], xin[:, slot, j], b2[:, :], ALU.add)
                op.then_inc(xb_done.sem, 1)

            in_groups(pool, each)

        @block.vector
        def _(dve):
            w_copied.open(dve)
            x1_done.open(dve)
            dve.wait_ge(den_in, 16)
            nc.vector.reciprocal(rden[:, :], den[:, :]).then_inc(rden_done, 1)
            dve.wait_ge(w_in, WLOADS)
            nc.vector.tensor_reduce(a1[:, :], w1[:, :, :], AX.X, ALU.add, apply_absolute_value=True)
            nc.vector.tensor_reduce(a2[:, :], w2[:, :, :], AX.X, ALU.add, apply_absolute_value=True)\
                .then_inc(mean_done, 1)
            dve.wait_ge(mean_done, 1)
            nc.vector.tensor_scalar(a1[:, :], a1[:, :], 1.0 / C, None, ALU.mult).then_inc(mean_done, 1)
            nc.vector.tensor_scalar(a2[:, :], a2[:, :], 1.0 / FF, None, ALU.mult).then_inc(mean_done, 1)
            dve.wait_ge(mean_done, 3)
            dve.wait_ge(sign_done, 2)
            for k in range(KC):
                nc.vector.tensor_scalar(w2[:, k], sign2[:, k], a2[:, k:k + 1], None, ALU.mult).then_inc(scaled, 1)
            for n, (which, m0) in enumerate(turns):
                dve.wait_ge(w_turned.sem, w_turned.done(n))
                if which == 0:
                    k, m = m0 // FC, m0 % FC
                    op = nc.vector.tensor_copy(w1T[:, k, m * P:(m + 4) * P], turn_ps[:, :])
                else:
                    op = nc.vector.tensor_copy(w2T[:, m0 // KC:m0 // KC + 2].rearrange("p m c -> p (m c)"), turn_ps[:, :])
                op.then_inc(w_copied.sem, 1)

            def each(g, slot, use):
                dve.wait_ge(out_done.sem, out_done.done(g))
                dve.wait_ge(xb_done.sem, xb_done.done(g))
                dve.wait_ge(x1_out[slot], use * 16 + 16)
                nc.vector.tensor_tensor(x1[:, slot], out_ps[:, slot], xb[:, slot], ALU.add).then_inc(x1_done.sem, 1)

            in_groups(dve, each)

        @block.scalar
        def _(act):
            gelu_done.open(act)
            act.wait_ge(w_in, WLOADS)
            nc.scalar.activation(sign1[:, :, :], w1[:, :, :], ACT.Sign).then_inc(sign_done, 1)
            nc.scalar.activation(sign2[:, :, :], w2[:, :, :], ACT.Sign).then_inc(sign_done, 1)
            act.wait_ge(mean_done, 3)

            def each(g, slot, use):
                act.wait_ge(out_done.sem, out_done.freed(g, 2))
                for m in range(FC):
                    act.wait_ge(hid_done.sem, hid_done.done(g * FC + m))
                    nc.scalar.activation(hid[:, slot, m], hid_ps[:, m % HB], ACT.Gelu, scale=a1[:, m:m + 1],
                                         bias=b1[:, m:m + 1]).then_inc(gelu_done.sem, 1)

            in_groups(act, each)

        @block.tensor
        def _(pe):
            out_done.open(pe)
            hid_done.open(pe)
            pe.wait_ge(w_in, WLOADS)
            for n, (which, m0) in enumerate(turns):
                if n == 0:
                    pe.wait_ge(sign_done, 1)
                if which == 1:
                    pe.wait_ge(scaled, KC)
                pe.wait_ge(w_copied.sem, w_copied.freed(n, 1))
                for i in range(4):
                    if which == 0:
                        k, m = (m0 + i) // FC, (m0 + i) % FC
                        src = sign1[:, m, k * P:(k + 1) * P]
                    else:
                        m, k = (m0 + i) // KC, (m0 + i) % KC
                        src = w2[:, k, m * P:(m + 1) * P]
                    op = nc.tensor.transpose(turn_ps[:, i * P:(i + 1) * P], src, ident[:, :])
                op.then_inc(w_turned.sem, 1)
            pe.wait_ge(w_copied.sem, w_copied.done(len(turns) - 1))

            def hidden(g, slot, use):
                pe.wait_ge(g_in[slot], use * LOADS + LOADS)
                for m in range(FC):
                    pe.wait_ge(gelu_done.sem, gelu_done.freed(g * FC + m, 2))
                    for k in range(KC):
                        for part in range(2):
                            op = nc.tensor.matmul(hid_ps[:, m % HB], w1T[:, k, m * P:(m + 1) * P],
                                                  xp[:, slot, part, k], start=(k == 0 and part == 0),
                                                  stop=(k == KC - 1 and part == 1))
                    op.then_inc(hid_done.sem, 1)

            def output(g, slot, use):
                pe.wait_ge(att_done.sem, att_done.done(g))
                pe.wait_ge(x1_done.sem, x1_done.freed(g, 2))
                pe.wait_ge(gelu_done.sem, gelu_done.done(g * FC + FC - 1))
                for j in range(TG):
                    at = slice(j * P, (j + 1) * P)
                    for k in range(KC):
                        nc.tensor.matmul(out_ps[:, slot, j], att[:, slot, k, at], wo[:, k], start=(k == 0), stop=False)
                    for m in range(FC):
                        op = nc.tensor.matmul(out_ps[:, slot, j], hid[:, slot, m, at], w2T[:, m], start=False,
                                              stop=(m == FC - 1))
                op.then_inc(out_done.sem, 1)

            streamed(pe, hidden, output)


def rwkv_phase(nc, xnT_d, mix_ds, w_ds, decay_d, first_d, ident_d, yT_d):
    NW = 3
    NO = NW * KC
    STEPS = G
    with ExitStack() as ctx:
        s = Space(nc, ctx, "rwkv")
        ident = s.sb("ident", [P, P])
        raw_w = s.sb("raw_w", [P, NW, KC, C])
        wT = s.sb("wT", [P, NW, KC, C])
        mix = s.sb("mix", [P, NW, KC])
        unmix = s.sb("unmix", [P, NW, KC])
        decay = s.sb("decay", [P, KC])
        first = s.sb("first", [P, KC])
        x = s.sb("x", [P, B, KC, GT + 1])
        xm = s.sb("xm", [P, B, NW, KC, GT])
        kvr = s.sb("kvr", [P, B, NW, KC, GT])
        p = s.sb("p", [P, B, KC, GT + 1])
        q = s.sb("q", [P, B, KC, GT + 1])
        d_raw = s.sb("d_raw", [P, KC, GT])
        e_raw = s.sb("e_raw", [P, KC, GT])
        d = s.sb("d", [P, B, KC, GT])
        e_old = s.sb("e_old", [P, B, KC, GT])
        e_new = s.sb("e_new", [P, B, KC, GT])
        by_q = s.sb("by_q", [P, B, KC, GT])
        by_v = s.sb("by_v", [P, B, KC, GT])
        y = s.sb("y", [P, B, KC, GT])
        prod = s.ps("prod", [P, NO, GT])
        turn_ps = s.ps("turn_ps", [P, GT])

        w_in = s.sem("w_in")
        state_set = s.sem("state_set")
        unmix_done = s.sem("unmix_done")
        w_turned = s.step("w_turned")
        w_copied = s.step("w_copied", credit=1)
        x_in = [s.sem(f"x_in{b}") for b in range(B)]
        past = s.sem("past")
        prev_done = s.step("prev_done")
        xm_done = s.step("xm_done", credit=2)
        prod_done = s.step("prod_done", credit=2 * NO)
        kvr_done = s.step("kvr_done", credit=NO)
        p_carried = s.step("p_carried")
        p_done = s.step("p_done")
        raw_done = s.step("raw_done")
        arg_done = s.step("arg_done", credit=1)
        gates_done = s.step("gates_done")
        times_v = s.step("times_v")
        q_carried = s.step("q_carried")
        q_done = s.step("q_done")
        wkv_done = s.step("wkv_done")
        y_done = s.step("y_done", credit=2)
        y_out = [s.sem(f"y_out{b}") for b in range(B)]
        WLOADS = 16 * (1 + 2 * NW + 2)
        block = ctx.enter_context(nc.Block())

        @block.sync
        def _(sp):
            sp.dma_start(ident[:, :], ident_d).then_inc(w_in, 16)
            for n in range(NW):
                sp.dma_start(raw_w[:, n], w_ds[n].rearrange("(k p) n -> p k n", p=P)).then_inc(w_in, 16)
            with nc.allow_non_contiguous_dma(reason="one value per partition"):
                for n in range(NW):
                    sp.dma_start(mix[:, n], mix_ds[n].rearrange("(k p) -> p k", p=P)).then_inc(w_in, 16)
                sp.dma_start(decay[:, :], decay_d.rearrange("(k p) -> p k", p=P)).then_inc(w_in, 16)
                sp.dma_start(first[:, :], first_d.rearrange("(k p) -> p k", p=P)).then_inc(w_in, 16)

            def load(n, b, use):
                sp.wait_ge(xm_done.sem, xm_done.freed(n, 2))
                src = xnT_d[:, :, b, bass.ds(use * GT, GT + 1)]
                sp.dma_start(x[:, b], src).then_inc(x_in[b], 16)

            def store(n, b, use):
                sp.wait_ge(y_done.sem, y_done.done(n))
                sp.dma_start(yT_d[:, :, bass.ds(use * GT + b * T, GT)], y[:, b]).then_inc(y_out[b], 16)

            for b in range(B):
                sp.sem_inc(y_out[b], 16)

            def step(at):
                if at[0]:
                    load(*at[0])
                if at[3]:
                    store(*at[3])

            rolling(sp, step, 4)
            for b in range(B):
                sp.wait_ge(y_out[b], 16 * (1 + STEPS // 2))

        @block.gpsimd
        def _(pool):
            for b in range(B):
                nc.gpsimd.memset(p[:, b, :, GT:], LOWEST)
                op = nc.gpsimd.memset(q[:, b, :, GT:], 0.0)
            op.then_inc(state_set, 1)
            pool.wait_ge(unmix_done, 1)

            def step(at):
                new, _, old = at
                if new:
                    n, b, use = new
                    pool.wait_ge(x_in[b], use * 16 + 16)
                    pool.wait_ge(prod_done.sem, prod_done.freed(n * NO + (NO - 1), 2 * NO))
                    pool.sem_inc(past, 1)
                    for w in range(NW):
                        for c in range(KC):
                            op = nc.gpsimd.tensor_scalar(xm[:, b, w, c], x[:, b, c, 0:GT], unmix[:, w, c:c + 1], 0.0,
                                                         ALU.mult, ALU.add)
                    op.then_inc(prev_done.sem, 1)
                if old:
                    n, b, use = old
                    pool.wait_ge(gates_done.sem, gates_done.done(n))
                    pool.wait_ge(kvr_done.sem, kvr_done.done(n * NO + (2 * KC - 1)))
                    pool.sem_inc(past, 1)
                    nc.gpsimd.tensor_tensor(e_new[:, b], e_new[:, b], kvr[:, b, 1], ALU.mult)
                    nc.gpsimd.tensor_tensor(by_v[:, b], by_v[:, b], kvr[:, b, 1], ALU.mult)\
                        .then_inc(times_v.sem, 1)

            rolling(pool, step, 3)

        @block.vector
        def _(dve):
            xm_done.open(dve)
            y_done.open(dve)
            w_copied.open(dve)
            arg_done.open(dve)
            dve.wait_ge(w_in, WLOADS)
            nc.vector.tensor_scalar(unmix[:, :, :], mix[:, :, :], -1.0, 1.0, ALU.mult, ALU.add).then_inc(unmix_done, 1)
            for n in range(NW):
                dve.wait_ge(w_turned.sem, w_turned.done(n))
                nc.vector.tensor_copy(wT[:, n].rearrange("p k e -> p (k e)"), turn_ps[:, :]).then_inc(w_copied.sem, 1)
            dve.wait_ge(state_set, 1)

            def blend(n, b, use):
                dve.wait_ge(prev_done.sem, prev_done.done(n))
                for w in range(NW):
                    for c in range(KC):
                        op = nc.vector.scalar_tensor_tensor(xm[:, b, w, c], x[:, b, c, 1:], mix[:, w, c:c + 1],
                                                            xm[:, b, w, c], ALU.mult, ALU.add)
                op.then_inc(xm_done.sem, 1)

            def state(n, b, use):
                dve.wait_ge(kvr_done.sem, kvr_done.done(n * NO + (KC - 1)))
                dve.wait_ge(y_done.sem, y_done.freed(n, 2))
                nc.vector.tensor_copy(p[:, b, :, 0:1], p[:, b, :, GT:]).then_inc(p_carried.sem, 1)
                dve.wait_ge(p_carried.sem, p_carried.done(n))
                for c in range(KC):
                    op = nc.vector.tensor_tensor_scan(p[:, b, c, 1:], decay[:, c:c + 1].broadcast_to([P, GT]),
                                                      kvr[:, b, 0, c], p[:, b, c, 0:1], ALU.add, ALU.max)
                op.then_inc(p_done.sem, 1)
                dve.wait_ge(p_done.sem, p_done.done(n))
                dve.wait_ge(arg_done.sem, arg_done.freed(n, 1))
                for c in range(KC):
                    nc.vector.scalar_tensor_tensor(d_raw[:, c], p[:, b, c, 0:GT], first[:, c:c + 1], kvr[:, b, 0, c],
                                                   ALU.subtract, ALU.subtract)
                    op = nc.vector.scalar_tensor_tensor(e_raw[:, c], p[:, b, c, 0:GT], decay[:, c:c + 1],
                                                        kvr[:, b, 0, c], ALU.add, ALU.subtract)
                op.then_inc(raw_done.sem, 1)
                dve.wait_ge(raw_done.sem, raw_done.done(n))
                nc.vector.tensor_scalar(d[:, b], d_raw[:, :, :], CLAMP, -CLAMP, ALU.min, ALU.max)
                nc.vector.tensor_scalar(e_old[:, b], e_raw[:, :, :], 0.0, -CLAMP, ALU.min, ALU.max)
                nc.vector.tensor_scalar(e_new[:, b], e_raw[:, :, :], CLAMP, 0.0, ALU.min, ALU.max)\
                    .then_inc(arg_done.sem, 1)

            def outcome(n, b, use):
                nc.vector.tensor_copy(q[:, b, :, 0:1], q[:, b, :, GT:]).then_inc(q_carried.sem, 1)
                dve.wait_ge(times_v.sem, times_v.done(n))
                dve.wait_ge(q_carried.sem, q_carried.done(n))
                for c in range(KC):
                    op = nc.vector.tensor_tensor_scan(q[:, b, c, 1:], e_old[:, b, c], e_new[:, b, c], q[:, b, c, 0:1],
                                                      ALU.mult, ALU.add)
                op.then_inc(q_done.sem, 1)
                dve.wait_ge(q_done.sem, q_done.done(n))
                nc.vector.tensor_tensor(by_q[:, b], by_q[:, b], q[:, b, :, 0:GT], ALU.mult).then_inc(wkv_done.sem, 1)
                dve.wait_ge(wkv_done.sem, wkv_done.done(n * 2))
                nc.vector.tensor_tensor(by_q[:, b], by_q[:, b], by_v[:, b], ALU.add).then_inc(wkv_done.sem, 1)
                dve.wait_ge(wkv_done.sem, wkv_done.done(n * 2 + 1))
                dve.wait_ge(kvr_done.sem, kvr_done.done(n * NO + (NO - 1)))
                dve.wait_ge(y_out[b], use * 16 + 16)
                nc.vector.tensor_tensor(y[:, b], by_q[:, b], kvr[:, b, 2], ALU.mult).then_inc(y_done.sem, 1)

            def step(at):
                for stage, group in zip((blend, state, outcome), at):
                    if group:
                        stage(*group)

            rolling(dve, step, 3)

        @block.scalar
        def _(act):
            kvr_done.open(act)

            def step(at):
                new, old = at
                if old:
                    n, b, use = old
                    act.wait_ge(arg_done.sem, arg_done.done(n))
                    nc.scalar.activation(by_q[:, b], d[:, b], ACT.Sigmoid)
                    nc.scalar.activation(by_v[:, b], d[:, b], ACT.Sigmoid, scale=-1.0)
                    nc.scalar.activation(e_old[:, b], e_old[:, b], ACT.Exp)
                    nc.scalar.activation(e_new[:, b], e_new[:, b], ACT.Exp, scale=-1.0).then_inc(gates_done.sem, 1)
                if new:
                    n, b, use = new
                    act.wait_ge(y_done.sem, y_done.freed(n, 2))
                    for o in range(NO):
                        w, c = o // KC, o % KC
                        act.wait_ge(prod_done.sem, prod_done.done(n * NO + o))
                        nc.scalar.activation(kvr[:, b, w, c], prod[:, o], ACT.Sigmoid if w == 2 else ACT.Identity)\
                            .then_inc(kvr_done.sem, 1)

            rolling(act, step, 2)

        @block.tensor
        def _(pe):
            prod_done.open(pe)
            pe.wait_ge(w_in, WLOADS)
            for n in range(NW):
                pe.wait_ge(w_copied.sem, w_copied.freed(n, 1))
                for k in range(KC):
                    for c in range(KC):
                        at = (k * KC + c) * P
                        op = nc.tensor.transpose(turn_ps[:, at:at + P], raw_w[:, n, c, k * P:(k + 1) * P], ident[:, :])
                op.then_inc(w_turned.sem, 1)
            pe.wait_ge(w_copied.sem, w_copied.done(NW - 1))

            def each(n, b, use):
                pe.wait_ge(xm_done.sem, xm_done.done(n))
                for o in range(NO):
                    w, c = o // KC, o % KC
                    pe.wait_ge(kvr_done.sem, kvr_done.freed(n * NO + o, NO))
                    for k in range(KC):
                        op = nc.tensor.matmul(prod[:, o], wT[:, w, k, c * P:(c + 1) * P], xm[:, b, w, k],
                                              start=(k == 0), stop=(k == KC - 1))
                    op.then_inc(prod_done.sem, 1)

            in_groups(pe, each)


def moe_phase(nc, x1_d, parts_d, yT_d, wo_d, router_d, gate_d, up_d, down_d, sgate_d, sup_d, sdown_d,
              lower_d, ident_d, coef_d, out_d):
    UNITS = E + ES // P
    SHARED = ES // P
    with ExitStack() as ctx:
        s = Space(nc, ctx, "moe")
        router = WeightSplit(s, "router", KC * E)
        sgate = WeightSplit(s, "sgate", KC * ES, after=router)
        sup = WeightSplit(s, "sup", KC * ES, after=sgate)
        gate = WeightSplit(s, "gate", KC * E * ED, after=sup)
        up = WeightSplit(s, "up", KC * E * ED, after=gate)
        splits = (router, sgate, sup, gate, up)
        ident = s.sb("ident", [P, P])
        ones = s.sb("ones", [1, P])
        lower = s.sb("lower", [P, E, E])
        raw_wo = s.sb("raw_wo", [P, KC, C])
        woT = s.sb("woT", [P, KC, C])
        down = s.sb("down", [P, UNITS, C])
        xp = s.sb("xp", [P, 2, 2, KC, GT], F16)
        yT = s.sb("yT", [P, 2, KC, GT])
        x1 = s.sb("x1", [P, 2, TG, C])
        top = s.sb("top", [P, TG])
        z = s.sb("z", [P, TG, E])
        ex = s.sb("ex", [P, TG, E])
        total = s.sb("total", [P, TG])
        inv = s.sb("inv", [P, TG])
        prob = s.sb("prob", [P, TG, E])
        above = s.sb("above", [P, TG, E, E])
        equal = s.sb("equal", [P, TG, E, E])
        rank = s.sb("rank", [P, TG, E])
        coef = s.sb("coef", [P, TG, E])
        coefT = s.sb("coefT", [TG * E, P])
        spread = s.sb("spread", [P, 2, TG, E, P])
        silu = s.sb("silu", [P, 2, GT])
        weighted = s.sb("weighted", [P, 2, GT])
        hid = s.sb("hid", [P, UNITS, GT])
        out = s.sb("out", [P, 2, TG, C])
        gate_ps = s.ps("gate_ps", [P, 2, GT])
        up_ps = s.ps("up_ps", [P, 2, GT])
        out_ps = s.ps("out_ps", [P, TG, C])
        logit_ps = s.ps("logit_ps", [P, GT])
        turn_ps = s.ps("turn_ps", [P, GT])

        w_in = s.sem("w_in")
        ones_set = s.sem("ones_set")
        wo_turned = s.sem("wo_turned")
        wo_copied = s.sem("wo_copied")
        xp_in = [s.sem(f"xp_in{p}") for p in range(2)]
        late_in = [s.sem(f"late_in{p}") for p in range(2)]
        spread_in = [s.sem(f"spread_in{p}") for p in range(2)]
        logit_done = s.step("logit_done")
        route = s.sem("route")
        exp_done = s.step("exp_done")
        past = s.sem("past")
        past_wait = s.sem("past_wait")
        coef_turned = s.step("coef_turned", credit=1)
        coefT_done = s.step("coefT_done")
        coef_out = s.step("coef_out", credit=1, unit=16)
        gate_done = s.step("gate_done")
        up_done = s.step("up_done", credit=2 * UNITS)
        silu_done = s.step("silu_done", credit=2)
        weighted_done = s.step("weighted_done", credit=2 * E)
        hid_done = s.step("hid_done", credit=2)
        down_done = s.step("down_done", credit=2)
        out_done = s.step("out_done", credit=2)
        stored = [s.sem(f"stored{p}") for p in range(2)]
        ROUTE = 11
        SPLIT_LOADS = 3 + 2 * KC
        WLOADS = 16 * 5
        block = ctx.enter_context(nc.Block())

        @block.sync
        def _(sp):
            sp.dma_start(ident[:, :], ident_d).then_inc(w_in, 16)
            sp.dma_start(router.w[:, :].rearrange("p (k e) -> p k e", k=KC),
                         router_d.rearrange("(k p) e -> p k e", p=P)).then_inc(router.loaded, 16)
            for w, src in ((sgate, sgate_d), (sup, sup_d)):
                sp.dma_start(w.w[:, :].rearrange("p (k n) -> p k n", k=KC),
                             src.rearrange("(k p) n -> p k n", p=P)).then_inc(w.loaded, 16)
            for w, src in ((gate, gate_d), (up, up_d)):
                for k in range(KC):
                    sp.dma_start(w.w[:, k * E * ED:(k + 1) * E * ED].rearrange("p (e d) -> p e d", e=E),
                                 src[:, k * P:(k + 1) * P, :].rearrange("e p d -> p e d")).then_inc(w.loaded, 16)
            sp.dma_start(lower[:, :, :], lower_d).then_inc(w_in, 16)
            sp.dma_start(raw_wo[:, :, :], wo_d.rearrange("(k p) n -> p k n", p=P)).then_inc(w_in, 16)
            sp.dma_start(down[:, 0:SHARED], sdown_d.rearrange("(k p) n -> p k n", p=P)).then_inc(w_in, 16)
            sp.dma_start(down[:, SHARED:], down_d.rearrange("e p n -> p e n")).then_inc(w_in, 16)

            def load(g, slot):
                toks = bass.ds(g * GT, GT)
                sp.wait_ge(up_done.sem, up_done.freed(g * UNITS + (UNITS - 1), 2 * UNITS))
                for part in range(2):
                    sp.dma_start(xp[:, slot, part], parts_d[part, :, :, toks]).then_inc(xp_in[slot], 16)

            def load_late(g, slot):
                toks = bass.ds(g * GT, GT)
                sp.wait_ge(out_done.sem, out_done.freed(g, 2))
                sp.sem_inc(past_wait, 1)
                sp.dma_start(yT[:, slot], yT_d[:, :, toks]).then_inc(late_in[slot], 16)
                sp.dma_start(x1[:, slot], x1_d[toks, :].rearrange("(j p) c -> p j c", p=P)).then_inc(late_in[slot], 16)

            def coefficients(g, slot):
                sp.wait_ge(coefT_done.sem, coefT_done.done(g))
                sp.dma_start(coef_d[bass.ds(g, 1), :, :].rearrange("o r t -> (o r) t"), coefT[:, :])\
                    .then_inc(coef_out.sem, 16)
                sp.wait_ge(coef_out.sem, coef_out.done(g))
                sp.wait_ge(weighted_done.sem, weighted_done.freed(g * E + (E - 1), 2 * E))
                row = coef_d[bass.ds(g, 1), :, :].rearrange("o r t -> o (r t)")
                sp.dma_start(spread[:, slot].rearrange("p j e t -> p (j e t)"), row.broadcast_to([P, TG * E * P]))\
                    .then_inc(spread_in[slot], 16)

            def store(g, slot):
                sp.wait_ge(out_done.sem, out_done.done(g))
                dst = out_d[bass.ds(g * GT, GT), :].rearrange("(j p) c -> p j c", p=P)
                sp.dma_start(dst, out[:, slot]).then_inc(stored[slot], 16)

            sp.sem_inc(coef_out.sem, 16)
            for slot in range(2):
                sp.sem_inc(stored[slot], 16)

            def step(at):
                new, old = at
                if new:
                    g, slot, use = new
                    load(g, slot)
                    load_late(g, slot)
                    coefficients(g, slot)
                if old:
                    store(old[0], old[1])

            rolling(sp, step, 2)
            for slot in range(2):
                sp.wait_ge(stored[slot], 16 * (1 + G // 2))

        @block.gpsimd
        def _(pool):
            weighted_done.open(pool)
            nc.gpsimd.memset(ones[:, :], 1.0).then_inc(ones_set, 1)

            def each(g, slot, use):
                pool.wait_ge(spread_in[slot], use * 16 + 16)
                for e in range(E):
                    u = SHARED + e
                    pool.wait_ge(silu_done.sem, silu_done.done(g * UNITS + u))
                    pool.wait_ge(hid_done.sem, hid_done.freed(g * UNITS + u, 2))
                    pool.sem_inc(past, 1)
                    nc.gpsimd.tensor_tensor(weighted[:, u % 2].rearrange("p (j t) -> p j t", j=TG), silu[:, u % 2].rearrange("p (j t) -> p j t", j=TG), spread[:, slot, :, e, :], ALU.mult)\
                        .then_inc(weighted_done.sem, 1)

            in_groups(pool, each)

        @block.vector
        def _(dve):
            hid_done.open(dve)
            out_done.open(dve)
            for w in splits:
                w.vector(nc, dve, logit_ps[0:1, 0:P], logit_ps[:, P:P + 1], SPLIT_LOADS)
            dve.wait_ge(wo_turned, 1)
            nc.vector.tensor_copy(woT[:, :, :].rearrange("p k e -> p (k e)"), turn_ps[:, :]).then_inc(wo_copied, 1)

            def over_e(t):
                return t.unsqueeze(2).broadcast_to([P, TG, E])

            def routing(g, slot, use):
                logits = logit_ps[:, 0:TG * E].rearrange("p (j e) -> p j e", j=TG)
                others = prob[:, :, :].unsqueeze(2).broadcast_to([P, TG, E, E])
                own = prob[:, :, :].unsqueeze(3).broadcast_to([P, TG, E, E])
                masks = lower[:, :, :].unsqueeze(1).broadcast_to([P, TG, E, E])
                at = g * ROUTE
                dve.wait_ge(logit_done.sem, logit_done.done(g))
                nc.vector.tensor_reduce(top[:, :], logits, AX.X, ALU.max).then_inc(route, 1)
                dve.wait_ge(route, at + 1)
                nc.vector.tensor_tensor(z[:, :, :], logits, over_e(top[:, :]), ALU.subtract).then_inc(route, 1)
                dve.wait_ge(exp_done.sem, exp_done.done(g))
                nc.vector.tensor_reduce(total[:, :], ex[:, :, :], AX.X, ALU.add).then_inc(route, 1)
                dve.wait_ge(route, at + 3)
                nc.vector.reciprocal(inv[:, :], total[:, :]).then_inc(route, 1)
                dve.wait_ge(route, at + 4)
                nc.vector.tensor_tensor(prob[:, :, :], ex[:, :, :], over_e(inv[:, :]), ALU.mult).then_inc(route, 1)
                dve.wait_ge(route, at + 5)
                nc.vector.tensor_tensor(above[:, :, :, :], others, own, ALU.is_gt).then_inc(route, 1)
                nc.vector.tensor_tensor(equal[:, :, :, :], others, own, ALU.is_equal).then_inc(route, 1)
                dve.wait_ge(route, at + 7)
                nc.vector.tensor_tensor(equal[:, :, :, :], equal[:, :, :, :], masks, ALU.mult).then_inc(route, 1)
                dve.wait_ge(route, at + 8)
                nc.vector.tensor_tensor(above[:, :, :, :], above[:, :, :, :], equal[:, :, :, :], ALU.add)\
                    .then_inc(route, 1)
                dve.wait_ge(route, at + 9)
                nc.vector.tensor_reduce(rank[:, :, :], above[:, :, :, :], AX.X, ALU.add).then_inc(route, 1)
                dve.wait_ge(route, at + 10)
                dve.wait_ge(coef_turned.sem, coef_turned.freed(g, 1))
                nc.vector.scalar_tensor_tensor(coef[:, :, :], rank[:, :, :], 1.5, prob[:, :, :], ALU.is_lt, ALU.mult)\
                    .then_inc(route, 1)
                dve.wait_ge(coef_turned.sem, coef_turned.done(g))
                dve.wait_ge(coef_out.sem, coef_out.freed(g, 1))
                nc.vector.tensor_copy(coefT[:, :], turn_ps[0:TG * E, 0:P]).then_inc(coefT_done.sem, 1)

            def hidden(g, slot, use):
                dve.wait_ge(down_done.sem, down_done.freed(g, 1))
                for u in range(UNITS):
                    n = g * UNITS + u
                    dve.wait_ge(up_done.sem, up_done.done(n))
                    if u < SHARED:
                        dve.wait_ge(silu_done.sem, silu_done.done(n))
                    else:
                        dve.wait_ge(weighted_done.sem, weighted_done.done(g * E + (u - SHARED)))
                    act = (silu if u < SHARED else weighted)[:, u % 2]
                    w = sup if u < SHARED else up
                    nc.vector.scalar_tensor_tensor(hid[:, u], up_ps[:, u % 2], w.unscale[:, 0:1], act,
                                                   ALU.mult, ALU.mult).then_inc(hid_done.sem, 1)

            def output(g, slot, use):
                dve.wait_ge(down_done.sem, down_done.done(g))
                dve.wait_ge(late_in[slot], use * 32 + 32)
                dve.wait_ge(stored[slot], use * 16 + 16)
                nc.vector.tensor_tensor(out[:, slot], out_ps[:, :, :], x1[:, slot], ALU.add).then_inc(out_done.sem, 1)

            def step(at):
                new, old = at
                if old:
                    hidden(*old)
                if new:
                    routing(*new)
                if old:
                    output(*old)

            rolling(dve, step, 2)

        @block.scalar
        def _(act):
            silu_done.open(act)
            for w in splits:
                act.wait_ge(w.found, w.ready)

            def step(at):
                new, old = at
                if old:
                    g, slot, use = old
                    for u in range(UNITS):
                        n = g * UNITS + u
                        act.wait_ge(gate_done.sem, gate_done.done(n))
                        act.wait_ge(hid_done.sem, hid_done.freed(n, 2))
                        w = sgate if u < SHARED else gate
                        nc.scalar.activation(silu[:, u % 2], gate_ps[:, u % 2], ACT.Silu, scale=w.unscale[:, 0:1])\
                            .then_inc(silu_done.sem, 1)
                if new:
                    g, slot, use = new
                    act.wait_ge(route, g * ROUTE + 2)
                    nc.scalar.activation(ex[:, :, :], z[:, :, :], ACT.Exp, scale=router.unscale[:, 0:1])\
                        .then_inc(exp_done.sem, 1)

            rolling(act, step, 2)

        @block.tensor
        def _(pe):
            up_done.open(pe)
            down_done.open(pe)
            coef_turned.open(pe)
            pe.wait_ge(w_in, WLOADS)
            pe.wait_ge(ones_set, 1)
            for k in range(KC):
                for c in range(KC):
                    at = (k * KC + c) * P
                    op = nc.tensor.transpose(turn_ps[:, at:at + P], raw_wo[:, c, k * P:(k + 1) * P], ident[:, :])
            op.then_inc(wo_turned, 1)
            for w in splits:
                w.tensor(nc, pe, logit_ps[0:1, 0:P], logit_ps[:, P:P + 1], ident[:, :], ones[:, :])
            for w in splits:
                pe.wait_ge(w.found, w.ready)
            pe.wait_ge(wo_copied, 1)

            def columns(w, start, k, width, total):
                at = slice(k * total + start, k * total + start + width)
                return w.hi[:, at], w.lo[:, at]

            def routing(g, slot, use):
                pe.wait_ge(xp_in[slot], use * 32 + 32)
                pe.sem_inc(past, 1)
                for j in range(TG):
                    at = slice(j * P, (j + 1) * P)
                    op = parts_matmul(nc, logit_ps[:, j * E:(j + 1) * E],
                                      [columns(router, 0, k, E, E) for k in range(KC)],
                                      [(xp[:, slot, 0, k, at], xp[:, slot, 1, k, at]) for k in range(KC)],
                                      weights_stationary=False)
                op.then_inc(logit_done.sem, 1)

            def turn(g, slot, use):
                pe.wait_ge(route, g * ROUTE + ROUTE)
                pe.sem_inc(past, 1)
                nc.tensor.transpose(turn_ps[0:TG * E, 0:P], coef[:, :, :].rearrange("p j e -> p (j e)"), ident[:, :])\
                    .then_inc(coef_turned.sem, 1)

            def hidden(g, slot, use):
                acts = [(xp[:, slot, 0, k], xp[:, slot, 1, k]) for k in range(KC)]
                for u in range(UNITS):
                    n = g * UNITS + u
                    a, b, at, width = ((sgate, sup, u * P, ES) if u < SHARED else
                                       (gate, up, (u - SHARED) * ED, E * ED))
                    pe.wait_ge(silu_done.sem, silu_done.freed(n, 2))
                    parts_matmul(nc, gate_ps[:, u % 2], [columns(a, at, k, P, width) for k in range(KC)], acts)\
                        .then_inc(gate_done.sem, 1)
                    pe.wait_ge(hid_done.sem, hid_done.freed(n, 2))
                    parts_matmul(nc, up_ps[:, u % 2], [columns(b, at, k, P, width) for k in range(KC)], acts)\
                        .then_inc(up_done.sem, 1)

            def output(g, slot, tiles):
                for j in tiles:
                    at = slice(j * P, (j + 1) * P)
                    for k in range(KC):
                        nc.tensor.matmul(out_ps[:, j], yT[:, slot, k, at], woT[:, k], start=(k == 0), stop=False)
                    for u in range(UNITS):
                        op = nc.tensor.matmul(out_ps[:, j], hid[:, u, at], down[:, u], start=False,
                                              stop=(u == UNITS - 1))
                return op

            def step(at):
                new, old = at
                if old:
                    hidden(*old)
                if new:
                    routing(*new)
                if old:
                    g, slot, use = old
                    pe.wait_ge(late_in[slot], use * 32 + 32)
                    pe.wait_ge(hid_done.sem, hid_done.done(g * UNITS + (UNITS - 1)))
                    pe.wait_ge(out_done.sem, out_done.freed(g, 1))
                    output(g, slot, range(0, TG // 2))
                if new:
                    turn(*new)
                if old:
                    output(g, slot, range(TG // 2, TG)).then_inc(down_done.sem, 1)

            rolling(pe, step, 2)


def program(nc, x, w_qkv, w_out, w1, b1, w2, b2, mix_k, mix_v, mix_r, w_k, w_v, w_r, w_o, decay, first,
            router, gate, up, down, sgate, sup, sdown, ident, cos, sin, tri, lower, out):

    def scratch(name, shape, dt=F32):
        return nc.dram_tensor(name, shape, dt, kind="Internal").ap()

    x = x.rearrange("b t c -> (b t) c")
    out = out.rearrange("b t c -> (b t) c")
    parts0 = scratch("parts0", [2, P, KC, N], F16)
    qk = scratch("qk", [2, C, 3, N], BF16)
    va = scratch("va", [NIT, P, T // P, HG * 2 * D])
    heads_out = scratch("heads_out", [C, N])
    den = scratch("den", [HEADS, N])
    rden = scratch("rden", [HEADS, N])
    x1 = scratch("x1", [N, C])
    xn1T = scratch("xn1T", [P, KC, B, T + 1])
    parts1 = scratch("parts1", [2, P, KC, N], F16)
    yT = scratch("yT", [P, KC, N])
    coef = scratch("coef", [G, TG * E, P])

    layernorm_phase(nc, "ln1", x, None, parts0, ident)
    qkv_phase(nc, parts0, w_qkv, cos, sin, ident, qk, va)
    attention_phase(nc, qk, va, ident, tri, heads_out, den)
    ffn_phase(nc, x, parts0, heads_out, den, rden, w1, b1, w2, b2, w_out, ident, x1)
    layernorm_phase(nc, "ln2", x1, xn1T, parts1, ident)
    rwkv_phase(nc, xn1T, (mix_k, mix_v, mix_r), (w_k, w_v, w_r), decay, first, ident, yT)
    moe_phase(nc, x1, parts1, yT, w_o, router, gate, up, down, sgate, sup, sdown, lower, ident, coef, out)


def shape_tables():
    row = np.arange(P)
    freqs = np.arange(T, dtype=np.float32)[None] * (
        1.0 / np.float32(10000.0) ** (np.arange(0, D, 2, dtype=np.float32) / np.float32(D))
    ).astype(np.float32)[row % D // 2][:, None]
    sign = np.where(row % 2 == 0, -1.0, 1.0)[:, None]
    tri = np.zeros((P, GT), np.float32)
    tri[:, GT - P:] = np.where(row[None] > row[:, None], -1e37, 0.0)
    lower = np.broadcast_to(np.tril(np.ones((E, E), np.float32), -1), (P, E, E))
    return {
        "ident": np.eye(P, dtype=np.float32),
        "cos": np.cos(freqs).astype(np.float32),
        "sin": (np.sin(freqs) * sign).astype(np.float32),
        "tri": tri,
        "lower": np.ascontiguousarray(lower),
    }


INPUTS = (
    "L0_attn_x", "L0_attn_w_qkv", "L0_attn_w_out", "L0_ffn_w1", "L0_ffn_b1", "L0_ffn_w2", "L0_ffn_b2",
    "L1_attn_time_mix_k", "L1_attn_time_mix_v", "L1_attn_time_mix_r", "L1_attn_W_k", "L1_attn_W_v", "L1_attn_W_r",
    "L1_attn_W_o", "L1_attn_time_decay", "L1_attn_time_first", "L1_ffn_router", "L1_ffn_experts_gate",
    "L1_ffn_experts_up", "L1_ffn_experts_down", "L1_ffn_shared_gate", "L1_ffn_shared_up", "L1_ffn_shared_down",
)


def kernel(**inputs):
    import concourse.bacc as bacc
    from concourse.bass_utils import run_bass_kernel_spmd

    nc = bacc.Bacc("TRN2", target_bir_lowering=False, num_devices=1)
    arrays = {name: np.ascontiguousarray(inputs[name]) for name in INPUTS}
    arrays.update(shape_tables())
    args = [nc.dram_tensor(f"in_{name}", a.shape, mybir.dt.from_np(a.dtype), kind="ExternalInput").ap()
            for name, a in arrays.items()]
    out = nc.dram_tensor("out", (B, T, C), F32, kind="ExternalOutput").ap()
    program(nc, *args, out)
    result = run_bass_kernel_spmd(nc, [{f"in_{name}": a for name, a in arrays.items()}], core_ids=[0])
    return result.results[0]["out"]
```

```python
from contextlib import ExitStack

import numpy as np

import concourse.bass as bass
from concourse import mybir

F32 = mybir.dt.float32
BF16 = mybir.dt.bfloat16
F16 = mybir.dt.float16
I32 = mybir.dt.int32
ALU = mybir.AluOpType
ACT = mybir.ActivationFunctionType
AX = mybir.AxisListType

P = 128
B, T, C = 2, 2048, 256
N = B * T
KC = C // P
GT = 512
G = N // GT
TG = GT // P
HEADS, D = 16, C // 16
HG = 4
NIT = B * HEADS // HG
FF = 1024
FC = FF // P
E, ED, ES = 8, 128, 256
LN_EPS = 1e-5
LOWEST = -3.0e38
CLAMP = 30.0


class Step:

    def __init__(self, sem, credit=0, unit=1):
        self.sem, self.credit, self.unit = sem, credit, unit

    def open(self, eng):
        eng.sem_inc(self.sem, self.credit * self.unit)

    def done(self, n):
        return (n + (self.credit + 1)) * self.unit

    def freed(self, n, ring):
        return (n + (self.credit + 1 - ring)) * self.unit


class Space:

    def __init__(self, nc, ctx, phase):
        self.nc, self.ctx, self.phase = nc, ctx, phase

    def sb(self, name, shape, dt=F32):
        return self.ctx.enter_context(self.nc.sbuf_tensor(f"{self.phase}_{name}", shape, dt))

    def ps(self, name, shape, dt=F32):
        return self.ctx.enter_context(self.nc.psum_tensor(f"{self.phase}_{name}", shape, dt))

    def sem(self, name):
        return self.ctx.enter_context(self.nc.semaphore(f"{self.phase}_{name}"))

    def step(self, name, credit=0, unit=1):
        return Step(self.sem(name), credit, unit)


def parts_matmul(nc, out, weights, acts, weights_stationary=True):
    n = len(weights)
    last = None
    for k in range(n):
        (wh, wl), (xh, xl) = weights[k], acts[k]
        for m, (w, x) in enumerate(((wh, xh), (wl, xh), (wh, xl))):
            lhsT, rhs = (w, x) if weights_stationary else (x, w)
            last = nc.tensor.matmul(out, lhsT, rhs, start=(k == 0 and m == 0), stop=(k == n - 1 and m == 2))
    return last


class PowerScale:

    STEPS, TURNS = 7, 2

    def __init__(self, s, name, after=None):
        self.first_step = after.ready if after else 0
        self.first_turn = after.first_turn + after.TURNS if after else 0
        self.ready = self.first_step + self.STEPS
        self.top = s.sb(f"{name}_top", [P, 1])
        self.top_all = s.sb(f"{name}_top_all", [1, 1])
        self.power = s.sb(f"{name}_power", [P, 1])
        self.scale = s.sb(f"{name}_scale", [P, 1])
        self.unscale = s.sb(f"{name}_unscale", [P, 1])
        self.found = after.found if after else s.sem(f"{name}_found")
        self.turned = after.turned if after else s.sem(f"{name}_turned")

    def vector(self, nc, dve, turn, spread):
        dve.wait_ge(self.turned, self.first_turn + 1)
        nc.vector.tensor_reduce(self.top_all[:, :], turn, AX.X, ALU.max).then_inc(self.found, 1)
        dve.wait_ge(self.turned, self.first_turn + 2)
        nc.vector.tensor_scalar(self.power[:, :], spread, 1e-30, None, ALU.max).then_inc(self.found, 1)
        dve.wait_ge(self.found, self.first_step + 3)
        nc.vector.tensor_scalar(self.unscale[:, :].bitcast(I32), self.power[:, :].bitcast(I32), 0x7F800000,
                                None, ALU.bitwise_and).then_inc(self.found, 1)
        dve.wait_ge(self.found, self.first_step + 4)
        nc.vector.tensor_scalar(self.scale[:, :].bitcast(I32), self.unscale[:, :].bitcast(I32), 0x7F800000,
                                None, ALU.bitwise_xor).then_inc(self.found, 1)
        dve.wait_ge(self.found, self.first_step + 5)
        nc.vector.tensor_scalar(self.scale[:, :], self.scale[:, :], 2.0 ** 12, None, ALU.mult).then_inc(self.found, 1)
        nc.vector.tensor_scalar(self.unscale[:, :], self.unscale[:, :], 2.0 ** -13, None, ALU.mult)\
            .then_inc(self.found, 1)

    def tensor(self, nc, pe, turn, spread, ident, ones):
        pe.wait_ge(self.found, self.first_step + 1)
        nc.tensor.matmul(turn, self.top[:, :], ident, start=True, stop=True).then_inc(self.turned, 1)
        pe.wait_ge(self.found, self.first_step + 2)
        nc.tensor.matmul(spread, ones, self.top_all[:, :], start=True, stop=True).then_inc(self.turned, 1)


class WeightSplit(PowerScale):

    STEPS = 10

    def __init__(self, s, name, width, after=None):
        super().__init__(s, name, after)
        self.w = s.sb(f"{name}_w", [P, width])
        self.hi = s.sb(f"{name}_hi", [P, width], F16)
        self.lo = s.sb(f"{name}_lo", [P, width], F16)
        self.loaded = after.loaded if after else s.sem(f"{name}_loaded")

    def vector(self, nc, dve, turn, spread, loads=1):
        dve.wait_ge(self.loaded, 16 * loads)
        nc.vector.tensor_reduce(self.top[:, :], self.w[:, :], AX.X, ALU.max,
                                apply_absolute_value=True).then_inc(self.found, 1)
        super().vector(nc, dve, turn, spread)
        dve.wait_ge(self.found, self.first_step + 7)
        nc.vector.tensor_scalar(self.w[:, :], self.w[:, :], self.scale[:, 0:1], None, ALU.mult)\
            .then_inc(self.found, 1)
        dve.wait_ge(self.found, self.first_step + 8)
        nc.vector.tensor_copy(self.hi[:, :], self.w[:, :]).then_inc(self.found, 1)
        dve.wait_ge(self.found, self.first_step + 9)
        nc.vector.tensor_tensor(self.lo[:, :], self.w[:, :], self.hi[:, :], ALU.subtract).then_inc(self.found, 1)


class LayerNorm:

    NEWTON = 3
    SMALL = 5 + 3 * NEWTON
    GUESS = 2.0 ** -((0x7FFFFFFF - 0x5F3759DF) / 2 ** 23)

    def __init__(self, s, turned, full=False):
        self.turned = turned
        self.stats = s.sb("ln_stats", [P, TG, 6])
        self.mv = s.sb("ln_mv", [P, TG, 2])
        self.ve = s.sb("ln_ve", [P, TG])
        self.guess = s.sb("ln_guess", [P, TG])
        self.nt = s.sb("ln_nt", [P, TG])
        self.r = s.sb("ln_r", [P, TG])
        self.xn = s.sb("ln_xn", [P, 2, TG, C])
        self.hi = s.sb("ln_hi", [P, 2, KC, GT], F16)
        self.lo = s.sb("ln_lo", [P, 2, KC, GT], F16)
        self.full = s.sb("ln_full", [P, 2, KC, GT]) if full else None
        self.found = s.sem("ln_found")
        self.past = s.sem("ln_past")
        self.xn_done = s.step("ln_xn_done", credit=2)
        self.turn_done = s.step("ln_turn_done", credit=2)
        self.hi_done = s.step("ln_hi_done", credit=2)
        self.lo_done = s.step("ln_lo_done", credit=2)

    def statistics(self, nc, dve, n, x):
        at = n * self.SMALL
        dve.wait_ge(self.xn_done.sem, self.xn_done.freed(n, 1))
        dve.sem_inc(self.past, 1)
        for j in range(TG):
            op = nc.vector.bn_stats(self.stats[:, j], x[:, j])
        op.then_inc(self.found, 1)
        dve.wait_ge(self.found, at + 1)
        dve.sem_inc(self.past, 1)
        for j in range(TG):
            op = nc.vector.bn_aggr(self.mv[:, j], self.stats[:, j])
        op.then_inc(self.found, 1)
        dve.wait_ge(self.found, at + 2)
        nc.vector.tensor_scalar(self.ve[:, :], self.mv[:, :, 1], LN_EPS, None, ALU.add).then_inc(self.found, 1)

    def normalise(self, nc, dve, n, slot, x):
        at = n * self.SMALL
        dve.wait_ge(self.found, at + 3)
        nc.vector.tensor_scalar(self.guess[:, :].bitcast(I32), self.ve[:, :].bitcast(I32), 1, 0x7FFFFFFF,
                                ALU.logical_shift_right, ALU.bitwise_xor).then_inc(self.found, 1)
        dve.wait_ge(self.found, at + 4)
        nc.vector.tensor_scalar(self.r[:, :], self.guess[:, :], self.GUESS, None, ALU.mult).then_inc(self.found, 1)
        for i in range(self.NEWTON):
            dve.wait_ge(self.found, at + 5 + 3 * i)
            nc.vector.scalar_tensor_tensor(self.nt[:, :], self.r[:, :], -0.5, self.r[:, :], ALU.mult, ALU.mult)\
                .then_inc(self.found, 1)
            dve.wait_ge(self.found, at + 6 + 3 * i)
            nc.vector.tensor_tensor(self.nt[:, :], self.nt[:, :], self.ve[:, :], ALU.mult).then_inc(self.found, 1)
            dve.wait_ge(self.found, at + 7 + 3 * i)
            nc.vector.scalar_tensor_tensor(self.r[:, :], self.nt[:, :], 1.5, self.r[:, :], ALU.add, ALU.mult)\
                .then_inc(self.found, 1)
        dve.wait_ge(self.found, at + self.SMALL)
        dve.wait_ge(self.turn_done.sem, self.turn_done.freed(n, 2))
        for j in range(TG):
            op = nc.vector.tensor_scalar(self.xn[:, slot, j], x[:, j], self.mv[:, j, 0:1], self.r[:, j:j + 1],
                                         ALU.subtract, ALU.mult)
        op.then_inc(self.xn_done.sem, 1)

    def turn(self, nc, pe, n, slot, ident):
        pe.wait_ge(self.xn_done.sem, self.xn_done.done(n))
        pe.wait_ge(self.hi_done.sem, self.hi_done.freed(n, 1))
        pe.wait_ge(self.lo_done.sem, self.lo_done.freed(n, 1))
        for k in range(KC):
            for j in range(TG):
                op = nc.tensor.transpose(self.turned[:, k, j * P:(j + 1) * P], self.xn[:, slot, j, k * P:(k + 1) * P],
                                         ident)
        op.then_inc(self.turn_done.sem, 1)

    def high(self, nc, act, n, slot):
        act.wait_ge(self.turn_done.sem, self.turn_done.done(n))
        if self.full is not None:
            nc.scalar.copy(self.full[:, slot], self.turned[:, :, :])
        nc.scalar.copy(self.hi[:, slot], self.turned[:, :, :]).then_inc(self.hi_done.sem, 1)

    def low(self, nc, dve, n, slot):
        dve.wait_ge(self.hi_done.sem, self.hi_done.done(n))
        nc.vector.tensor_tensor(self.lo[:, slot], self.turned[:, :, :], self.hi[:, slot], ALU.subtract)\
            .then_inc(self.lo_done.sem, 1)


def rolling(eng, step, depth=2, n=G):
    lead = depth - 1
    pairs = (n - lead) // 2

    def peeled(m):
        step([(m - k, (m - k) % 2, (m - k) // 2) if 0 <= m - k < n else None for k in range(depth)])

    for m in range(lead):
        peeled(m)
    with eng.Fori(0, pairs) as i:
        for r in range(2):
            at = [lead + r - k for k in range(depth)]
            step([(i * 2 + a, a % 2, i + a // 2) for a in at])
    for m in range(lead + 2 * pairs, n + lead):
        peeled(m)


def qkv_phase(nc, x_d, w_qkv_d, cos_d, sin_d, ident_d, parts_d, qk_d, va_d):
    W3 = 3 * C
    CH = 2 * KC
    with ExitStack() as ctx:
        s = Space(nc, ctx, "qkv")
        w = WeightSplit(s, "w_qkv", KC * W3)
        w_swap = s.sb("w_swap", [P, 2, KC, 2 * C], F16)
        ident = s.sb("ident", [P, P])
        ones = s.sb("ones", [1, P])
        cos = s.sb("cos", [P, 2, GT])
        sin = s.sb("sin", [P, 2, GT])
        xin = s.sb("xin", [P, 2, TG, C])
        raw = s.sb("raw", [P, CH, GT])
        swapped = s.sb("swapped", [P, CH, GT])
        by_cos = s.sb("by_cos", [P, CH, GT])
        by_sin = s.sb("by_sin", [P, CH, GT])
        rot = s.sb("rot", [P, CH, GT])
        rest = s.sb("rest", [P, CH, GT])
        parts = s.sb("parts", [P, 2, CH, 3, GT], BF16)
        v = s.sb("v", [P, 2, HEADS // HG, TG, HG, 2 * D])
        turned = s.ps("turned", [P, KC, GT])
        qk_ps = s.ps("qk_ps", [P, 2, 2, GT])
        v_ps = s.ps("v_ps", [P, TG, C])
        ln = LayerNorm(s, turned)

        const_in = s.sem("const_in")
        set_done = s.sem("set_done")
        swap_done = s.sem("swap_done")
        x_in = [s.sem(f"x_in{p}") for p in range(2)]
        rope_in = [s.sem(f"rope_in{p}") for p in range(2)]
        qk_done = s.step("qk_done")
        v_done = s.step("v_done", credit=2)
        raw_done = s.step("raw_done", credit=2)
        v_copied = s.step("v_copied", credit=1)
        passed = s.sem("passed")
        past_wait = s.sem("past_wait")
        turns_done = s.step("turns_done", credit=2 * CH)
        rot_done = s.step("rot_done", credit=CH)
        hi_done = s.step("hi_done")
        rest_done = s.step("rest_done")
        mid_done = s.step("mid_done")
        parts_done = s.step("parts_done")
        xn_stored = [s.sem(f"xn_stored{p}") for p in range(2)]
        qk_stored = [s.sem(f"qk_stored{p}") for p in range(2)]
        v_stored = [s.sem(f"v_stored{p}") for p in range(2)]
        block = ctx.enter_context(nc.Block())

        def tokens(b, q):
            return bass.ds(q * GT + b * T, GT)

        @block.sync
        def _(sp):
            def load(n, b, q):
                sp.wait_ge(ln.xn_done.sem, ln.xn_done.freed(n, 2))
                sp.dma_start(xin[:, b], x_d[tokens(b, q), :].rearrange("(j p) c -> p j c", p=P)).then_inc(x_in[b], 16)

            def load_weights():
                sp.dma_start(w.w[:, :].rearrange("p (k n) -> p k n", k=KC),
                             w_qkv_d.rearrange("(k p) n -> p k n", p=P)).then_inc(w.loaded, 16)
                sp.dma_start(ident[:, :], ident_d).then_inc(const_in, 16)

            def load_rope(n, b, q):
                sp.wait_ge(turns_done.sem, turns_done.freed(n * CH + (CH - 1), 2 * CH))
                sp.sem_inc(past_wait, 1)
                for dst, src in ((cos, cos_d), (sin, sin_d)):
                    sp.dma_start(dst[:, b], src[:, bass.ds(q * GT, GT)]).then_inc(rope_in[b], 16)

            def store_xn(n, b, q):
                sp.wait_ge(ln.lo_done.sem, ln.lo_done.done(n))
                sp.sem_inc(past_wait, 1)
                for part, buf in enumerate((ln.hi, ln.lo)):
                    sp.dma_start(parts_d[part, :, :, tokens(b, q)], buf[:, b]).then_inc(xn_stored[b], 16)

            def store_heads(n, b, q):
                for m in range(CH):
                    sp.wait_ge(parts_done.sem, parts_done.done(n * CH + m))
                    sp.dma_start(qk_d[m // KC, m % KC * P:(m % KC + 1) * P, :, tokens(b, q)], parts[:, b, m])\
                        .then_inc(qk_stored[b], 16)
                sp.wait_ge(v_copied.sem, v_copied.done(n))
                dst = va_d[b * (HEADS // HG):(b + 1) * (HEADS // HG), :, bass.ds(q * TG, TG), :]
                sp.dma_start(dst.rearrange("i p j n -> p i (j n)"), v[:, b].rearrange("p i j h d -> p i (j h d)"))\
                    .then_inc(v_stored[b], 16)

            for b in range(2):
                sp.sem_inc(xn_stored[b], 32)
                sp.sem_inc(v_stored[b], 16)
                sp.sem_inc(qk_stored[b], 16 * CH)

            def step(at):
                if at[0]:
                    load(*at[0])
                    if not at[1]:
                        load_weights()
                    load_rope(*at[0])
                if at[1]:
                    store_xn(*at[1])
                if at[3]:
                    store_heads(*at[3])

            rolling(sp, step, 4)
            for b in range(2):
                sp.wait_ge(qk_stored[b], 16 * CH * (1 + G // 2))
                sp.wait_ge(xn_stored[b], 32 * (1 + G // 2))
                sp.wait_ge(v_stored[b], 16 * (1 + G // 2))

        @block.gpsimd
        def _(pool):
            turns_done.open(pool)
            nc.gpsimd.memset(ones[:, :], 1.0)
            nc.gpsimd.memset(v[:, :, :, :, :, D:], 1.0).then_inc(set_done, 1)

            def each(n, b, q):
                for m in range(CH):
                    c = n * CH + m
                    if m == 0:
                        pool.wait_ge(rope_in[b], q * 32 + 32)
                    pool.wait_ge(raw_done.sem, raw_done.done(c))
                    pool.wait_ge(rot_done.sem, rot_done.freed(c, CH))
                    pool.sem_inc(passed, 1)
                    nc.gpsimd.tensor_tensor(by_cos[:, m], raw[:, m], cos[:, b], ALU.mult)
                    nc.gpsimd.tensor_tensor(by_sin[:, m], swapped[:, m], sin[:, b], ALU.mult)\
                        .then_inc(turns_done.sem, 1)

            in_groups(pool, each)

        @block.vector
        def _(dve):
            ln.xn_done.open(dve)
            ln.lo_done.open(dve)
            rot_done.open(dve)

            def weights():
                w.vector(nc, dve, qk_ps[0:1, 0, 0, 0:P], qk_ps[:, 0, 0, P:P + 1])
                dve.wait_ge(w.found, w.ready)
                for part, src in enumerate((w.hi, w.lo)):
                    for k in range(KC):
                        pairs = src[:, k * W3:k * W3 + 2 * C].rearrange("p (i two) -> p i two", two=2)
                        exchanged = w_swap[:, part, k].rearrange("p (i two) -> p i two", two=2)
                        for one in range(2):
                            op = nc.vector.tensor_copy(exchanged[:, :, one], pairs[:, :, 1 - one])
                op.then_inc(swap_done, 1)

            def rotated(c, m, b):
                dve.wait_ge(turns_done.sem, turns_done.done(c))
                nc.vector.tensor_tensor(rot[:, m], by_cos[:, m], by_sin[:, m], ALU.add).then_inc(rot_done.sem, 1)

            def middle(c, m, b):
                dve.wait_ge(hi_done.sem, hi_done.done(c))
                nc.vector.tensor_tensor(rest[:, m], rot[:, m], parts[:, b, m, 0], ALU.subtract).then_inc(rest_done.sem, 1)

            def last(c, m, b):
                dve.wait_ge(mid_done.sem, mid_done.done(c))
                nc.vector.tensor_tensor(parts[:, b, m, 2], rest[:, m], parts[:, b, m, 1], ALU.subtract)\
                    .then_inc(parts_done.sem, 1)

            def step(at):
                new, mid, old = at

                def parts_of(*todo):
                    for stage, m in todo if old else ():
                        stage(old[0] * CH + m, m, old[1])

                if new:
                    n, b, q = new
                    dve.wait_ge(x_in[b], q * 16 + 16)
                    ln.statistics(nc, dve, n, xin[:, b])
                parts_of((rotated, 0), (rotated, 1))
                if new:
                    ln.normalise(nc, dve, n, b, xin[:, b])
                    if not mid:
                        weights()
                parts_of((middle, 0), (rotated, 2), (middle, 1), (last, 0), (rotated, 3), (middle, 2), (last, 1),
                         (middle, 3), (last, 2))
                if new:
                    dve.wait_ge(v_done.sem, v_done.freed(n, 2))
                    dve.wait_ge(xn_stored[b], q * 32 + 32)
                    ln.low(nc, dve, n, b)
                parts_of((last, 3))

            rolling(dve, step, 3)

        @block.scalar
        def _(act):
            ln.hi_done.open(act)
            raw_done.open(act)
            v_copied.open(act)
            act.wait_ge(set_done, 1)

            def own(n, b, q, m):
                c = n * CH + m
                act.wait_ge(qk_done.sem, qk_done.done(c))
                act.wait_ge(turns_done.sem, turns_done.freed(c, CH))
                nc.scalar.activation(raw[:, m], qk_ps[:, m % 2, 0], ACT.Identity, scale=w.unscale[:, 0:1])
                nc.scalar.activation(swapped[:, m], qk_ps[:, m % 2, 1], ACT.Identity, scale=w.unscale[:, 0:1])\
                    .then_inc(raw_done.sem, 1)

            def values(n, b, q):
                act.wait_ge(v_done.sem, v_done.done(n))
                act.wait_ge(v_stored[b], q * 16 + 16)
                for j in range(TG):
                    op = nc.scalar.activation(v[:, b, :, j, :, 0:D],
                                              v_ps[:, j].rearrange("p (i h d) -> p i h d", h=HG, d=D),
                                              ACT.Identity, scale=w.unscale[:, 0:1])
                op.then_inc(v_copied.sem, 1)

            def first_part(n, b, q, m):
                c = n * CH + m
                act.wait_ge(rot_done.sem, rot_done.done(c))
                act.wait_ge(qk_stored[b], q * (16 * CH) + 16 * CH)
                nc.scalar.copy(parts[:, b, m, 0], rot[:, m]).then_inc(hi_done.sem, 1)

            def second_part(n, b, q, m):
                c = n * CH + m
                act.wait_ge(rest_done.sem, rest_done.done(c))
                nc.scalar.copy(parts[:, b, m, 1], rest[:, m]).then_inc(mid_done.sem, 1)

            def step(at):
                new, mid, old = at

                def pieces(*todo):
                    for stage, m in todo:
                        group = mid if stage is own else old
                        if group:
                            stage(*group, m)

                pieces((own, 0), (first_part, 0), (first_part, 1), (own, 1), (second_part, 0), (first_part, 2),
                       (second_part, 1), (own, 2), (first_part, 3), (second_part, 2))
                if new:
                    n, b, q = new
                    act.wait_ge(v_done.sem, v_done.freed(n, 2))
                    act.wait_ge(xn_stored[b], q * 32 + 32)
                    ln.high(nc, act, n, b)
                pieces((second_part, 3), (own, 3))
                if mid:
                    values(*mid)

            rolling(act, step, 3)

        @block.tensor
        def _(pe):
            ln.turn_done.open(pe)
            v_done.open(pe)
            pe.wait_ge(const_in, 16)
            pe.wait_ge(set_done, 1)
            def weight(k, cols):
                at = slice(k * W3 + cols.start, k * W3 + cols.stop)
                return w.hi[:, at], w.lo[:, at]

            def heads(n, b, q, m):
                acts = [(ln.hi[:, b, k], ln.lo[:, b, k]) for k in range(KC)]
                cols = slice(m * P, (m + 1) * P)
                pe.wait_ge(raw_done.sem, raw_done.freed(n * CH + m, 2))
                parts_matmul(nc, qk_ps[:, m % 2, 0], [weight(k, cols) for k in range(KC)], acts)
                parts_matmul(nc, qk_ps[:, m % 2, 1], [(w_swap[:, 0, k, cols], w_swap[:, 1, k, cols]) for k in range(KC)],
                             acts).then_inc(qk_done.sem, 1)

            def values(n, b, q):
                pe.wait_ge(v_copied.sem, v_copied.freed(n, 1))
                for j in range(TG):
                    at = slice(j * P, (j + 1) * P)
                    op = parts_matmul(nc, v_ps[:, j], [weight(k, slice(2 * C, 3 * C)) for k in range(KC)],
                                      [(ln.hi[:, b, k, at], ln.lo[:, b, k, at]) for k in range(KC)],
                                      weights_stationary=False)
                op.then_inc(v_done.sem, 1)

            def step(at):
                new, mid = at
                if mid:
                    n, b, q = mid
                    pe.wait_ge(ln.lo_done.sem, ln.lo_done.done(n))
                    for m in range(CH - 1):
                        heads(*mid, m)
                if new:
                    ln.turn(nc, pe, new[0], new[1], ident[:, :])
                    if not mid:
                        w.tensor(nc, pe, qk_ps[0:1, 0, 0, 0:P], qk_ps[:, 0, 0, P:P + 1], ident[:, :], ones[:, :])
                        pe.wait_ge(swap_done, 1)
                if mid:
                    heads(*mid, CH - 1)
                    values(*mid)

            rolling(pe, step, 2)


def attention_phase(nc, qk_d, va_d, ident_d, tri_d, o_d, den_d):
    ROWS = 6 * D
    MROWS = 2
    QB, KB = T // GT, T // P
    HP = HG // 2
    steps = [(t, j) for t in range(QB) for j in range(TG * (t + 1))]
    NS, NP = len(steps), len(steps) * HP
    last_step = [max(i for i, (t, _) in enumerate(steps) if t == u) for u in range(QB)]
    diagonal = [i for i, (t, j) in enumerate(steps) if j >= TG * t]
    MXR, SCR = 3, 4
    LATE = QB - 1
    LATE_TO = 18

    def chunks(t):
        return [("chunk", t, tt, h, c) for tt in range(TG * t, TG * (t + 1)) for h in range(HG) for c in range(t + 1)]

    def with_turn(t, turned):
        own = chunks(t)
        return own[:MXR] + [("turn", turned)] + own[MXR:]

    late = with_turn(LATE, LATE - 1)
    early = [e for t in range(LATE) for e in with_turn(t, (t - 1) % QB)]
    period = late + early
    ahead = [e for e in early if e != ("turn", LATE)]
    NA, NE = len(ahead), len(period)
    bank_of = {e: i % MXR for i, e in enumerate(period)}

    def entry_done(it, i):
        return it * NE + (NA + i + 1)

    def bank_freed(it, i):
        before = [k for k in range(i) if bank_of[period[k]] == bank_of[period[i]]]
        if before:
            return entry_done(it, before[-1])
        return it * NE + (NA - NE) + 1 + max(k for k in range(NE) if bank_of[period[k]] == bank_of[period[i]])

    def spread_entries():
        def pace(pairs, entries):
            work = np.cumsum([GT - max(0, steps[r // HP][1] - TG * steps[r // HP][0]) * P for r in pairs])
            cost = np.cumsum([1.0 if e[0] == "turn" or e[4] < e[2] // TG else 0.2 + 0.2 * (e[2] % TG + 1)
                              for e in entries])
            place = np.searchsorted(work / work[-1], cost / cost[-1] - 1e-9)
            return [pairs[k] for k in place]

        at = pace(range(LATE_TO * HP), late) + pace(range(LATE_TO * HP, NP), early)
        return [[i for i, r in enumerate(at) if r == k] for k in range(NP)]

    spots = spread_entries()
    SCALE = float(D) ** -0.5
    with ExitStack() as ctx:
        s = Space(nc, ctx, "att")
        qop = s.sb("qop", [P, 2, QB, HG, GT], BF16)
        kop = s.sb("kop", [P, 2, HG, T], BF16)
        v = s.sb("v", [P, 2, KB, HG * 2 * D])
        prob = s.sb("prob", [P, 4, 2, GT])
        o = s.sb("o", [P, 2, GT])
        ident = s.sb("ident", [P, P])
        tri = s.sb("tri", [P, GT])
        scratch = s.sb("scratch", [P, SCR, GT], BF16)
        m_part = s.sb("m_part", [P, HG, KB, QB])
        neg_m = s.sb("neg_m", [P, 2, P])
        m_row = s.sb("m_row", [HG * TG, 2, MROWS, P], BF16)
        score = s.ps("score", [P, 2, 2, GT])
        mx = s.ps("mx", [P, MXR, GT])
        pv = s.ps("pv", [P, GT])

        const_in = s.sem("const_in")
        ones_set = s.sem("ones_set")
        qkv_in = [s.sem(f"qkv_in{p}") for p in range(2)]
        m_in = [s.sem(f"m_in{t}") for t in range(QB)]
        score_done = s.step("score_done")
        exp_done = s.step("exp_done", credit=2)
        masked = s.step("masked")
        passed = s.sem("passed")
        passed_pe = s.sem("passed_pe")
        pv_done = s.step("pv_done", credit=2)
        o_copied = s.step("o_copied", credit=1)
        mx_done = s.sem("mx_done")
        m_found = s.sem("m_found")
        past_mx = s.sem("past_mx")
        m_reduced = s.step("m_reduced", credit=QB)
        m_high = s.step("m_high")
        o_stored = [s.sem(f"o_stored{p}") for p in range(2)]
        LOADS = 16 * (6 * (1 + QB) + 1)
        O_STORE = 16 * (HG + 1)
        block = ctx.enter_context(nc.Block())

        def schedule(eng, iteration, first):
            first()
            with eng.Fori(0, NIT // 2 - 1) as i:
                iteration(i * 2, 0, i, True, True)
                iteration(i * 2 + 1, 1, i, True, True)
            iteration(NIT - 2, 0, NIT // 2 - 1, True, False)
            iteration(NIT - 1, 1, NIT // 2 - 1, False, False)

        def walk(eng, entry):
            def first():
                for i, e in enumerate(ahead):
                    entry(0, e, i + 1)

            def iteration(it, slot, use, with_next, with_load):
                for i, e in enumerate(period):
                    own = i < len(late) or e == ("turn", LATE)
                    if own or with_next:
                        count = entry_done(it, i if i < len(late) or with_next else len(late))
                        entry(it if own else it + 1, e, count)

            schedule(eng, iteration, first)

        @block.sync
        def _(sp):
            for dst, src in ((ident, ident_d), (tri, tri_d)):
                sp.dma_start(dst[:, :], src).then_inc(const_in, 16)

            def load(b, hg, slot):
                toks, rows = bass.ds(b * T, T), bass.ds(hg * (HG * D), HG * D)
                for row, (kp, qp) in enumerate((i, j) for i in range(3) for j in range(3 - i)):
                    at = slice(row * D, (row + 1) * D)
                    sp.dma_start(kop[at, slot], qk_d[1, rows, kp, toks].rearrange("(h d) t -> d h t", d=D))\
                        .then_inc(qkv_in[slot], 16)
                    for t in range(QB):
                        toks_t = bass.ds(b * T + t * GT, GT)
                        sp.dma_start(qop[at, slot, t], qk_d[0, rows, qp, toks_t].rearrange("(h d) t -> d h t", d=D))\
                            .then_inc(qkv_in[slot], 16)
                sp.dma_start(v[:, slot].rearrange("p j n -> p (j n)"),
                              va_d[bass.ds(b * (HEADS // HG) + hg, 1)].rearrange("o p j n -> (o p) (j n)"))\
                    .then_inc(qkv_in[slot], 16)

            def send_m(it, slot, t, own, with_next=True):
                i = period.index(("turn", t)) if with_next else len(late)
                sp.wait_ge(m_found, entry_done(it, i if own else i - NE))
                for part in range(MROWS):
                    row = qop[ROWS + part:ROWS + part + 1, slot, t]
                    sp.dma_start(row.rearrange("o h (j t) -> o (h j) t", t=P),
                                 m_row[:, t % 2, part, :]).then_inc(m_in[t], 16)

            def store(it, t):
                b, hg = it // (HEADS // HG), it % (HEADS // HG)
                sp.wait_ge(o_copied.sem, o_copied.done(it * QB + t))
                toks = bass.ds(b * T + t * GT, GT)
                for h in range(HG):
                    sp.dma_start(o_d[bass.ds((hg * HG + h) * D, D), toks], o[2 * D * h:2 * D * h + D, t % 2])\
                        .then_inc(o_stored[t % 2], 16)
                sp.dma_start(den_d[bass.ds(hg * HG, HG), toks], o[D:P:2 * D, t % 2]).then_inc(o_stored[t % 2], 16)

            def first():
                for slot in range(2):
                    sp.sem_inc(o_stored[slot], O_STORE)
                    load(0, slot, slot)
                for t in range(QB):
                    sp.sem_inc(m_in[t], 16 * MROWS)
                for t in range(LATE - 1):
                    send_m(0, 0, t, False)

            def iteration(it, slot, use, with_next, with_load):
                send_m(it, slot, LATE - 1, True)
                store(it, 0)
                store(it, 1)
                send_m(it, slot, LATE, True, with_next)
                store(it, 2)
                if with_next:
                    for t in range(LATE - 1):
                        send_m(it + 1, 1 - slot, t, False)
                store(it, 3)
                if with_load:
                    sp.wait_ge(pv_done.sem, pv_done.done(it * NS + (NS - 1)))
                    nxt = it + 2
                    load(nxt // (HEADS // HG), nxt % (HEADS // HG), slot)

            schedule(sp, iteration, first)
            for slot in range(2):
                sp.wait_ge(o_stored[slot], O_STORE * (1 + NIT * QB // 2))

        @block.gpsimd
        def _(pool):
            nc.gpsimd.memset(kop[ROWS:ROWS + MROWS], 1.0).then_inc(ones_set, 1)

            def iteration(it, slot, use, with_next, with_load):
                for i, st in enumerate(diagonal):
                    t, j = steps[st]
                    n0 = (j - TG * t) * P
                    for hp in range(HP):
                        r = st * HP + hp
                        pool.wait_ge(exp_done.sem, exp_done.done(it * NP + r))
                        pool.sem_inc(passed, 1)
                        at = prob[:, r % 4, :, n0:n0 + P]
                        nc.gpsimd.affine_select(out=at, in_=at, compare_op=ALU.is_ge, fill=0.0, base=0,
                                                pattern=[[0, 2], [1, P]], channel_multiplier=-1)\
                            .then_inc(masked.sem, 1)

            schedule(pool, iteration, lambda: None)

        @block.vector
        def _(dve):
            m_reduced.open(dve)
            nc.vector.memset(m_part[:], LOWEST)
            nc.vector.memset(neg_m[:], 0.0).then_inc(ones_set, 1)
            dve.wait_ge(const_in, 32)
            dve.wait_ge(ones_set, 2)

            def entry(it, e, count):
                dve.wait_ge(mx_done, count)
                if e[0] == "turn":
                    t = e[1]
                    rows = mx[0:HG * TG, bank_of[e], 0:P]
                    dve.wait_ge(m_in[(t - 2) % QB], (it + (t // 2 + 1)) * (16 * MROWS))
                    nc.vector.tensor_copy(m_row[:, t % 2, 0, :], rows).then_inc(m_high.sem, 1)
                    dve.wait_ge(m_high.sem, m_high.done(it * QB + t))
                    nc.vector.tensor_tensor(m_row[:, t % 2, 1, :], rows, m_row[:, t % 2, 0, :], ALU.subtract)\
                        .then_inc(m_found, 1)
                    return
                _, t, tt, h, c = e
                first, last = chunks(t)[0], chunks(t)[-1]
                cell = m_part[:, h, tt, c:c + 1]
                bank = mx[:, bank_of[e]]
                if e == first:
                    dve.wait_ge(m_reduced.sem, m_reduced.freed(it * QB + t, QB))
                if c < tt // TG:
                    nc.vector.tensor_reduce(cell, bank, AX.X, ALU.max).then_inc(m_found, 1)
                else:
                    w = (tt % TG + 1) * P
                    dve.wait_ge(m_found, count - SCR) if not isinstance(count, int) or count > SCR else None
                    dve.sem_inc(past_mx, 1)
                    nc.vector.tensor_tensor_reduce(scratch[:, period.index(e) % SCR, 0:w], bank[:, 0:w], tri[:, GT - w:GT],
                                                   1.0, LOWEST, ALU.add, ALU.max, cell).then_inc(m_found, 1)
                if e == last:
                    dve.wait_ge(m_found, count)
                    nc.vector.tensor_reduce(
                        neg_m[:, t % 2, 0:HG * TG].rearrange("p (h j) -> p h j", h=HG),
                        m_part[:, :, TG * t:TG * (t + 1), :], AX.X, ALU.max, negate=True).then_inc(m_reduced.sem, 1)

            walk(dve, entry)

        @block.scalar
        def _(act):
            exp_done.open(act)
            o_copied.open(act)

            def iteration(it, slot, use, with_next, with_load):
                def copy_out(t):
                    act.wait_ge(pv_done.sem, pv_done.done(it * NS + last_step[t]))
                    act.wait_ge(o_stored[t % 2], it * (O_STORE * QB // 2) + (t // 2 + 1) * O_STORE)
                    nc.scalar.copy(o[:, t % 2], pv[:, :]).then_inc(o_copied.sem, 1)

                for st, (t, j) in enumerate(steps):
                    n0 = max(0, j - TG * t) * P
                    act.wait_ge(pv_done.sem, pv_done.freed(it * NS + st, 2))
                    for hp in range(HP):
                        r = st * HP + hp
                        act.wait_ge(score_done.sem, score_done.done(it * NP + r))
                        nc.scalar.activation(prob[:, r % 4, :, n0:], score[:, r % 2, :, n0:], ACT.Exp, scale=SCALE)\
                            .then_inc(exp_done.sem, 1)
                    if st - 1 in last_step:
                        copy_out(t - 1)
                copy_out(QB - 1)

            schedule(act, iteration, lambda: None)

        @block.tensor
        def _(pe):
            pv_done.open(pe)

            def entry(it, slot, e, freed):
                if freed is not None:
                    pe.wait_ge(m_found, freed)
                if e[0] == "turn":
                    t = e[1]
                    pe.wait_ge(m_reduced.sem, m_reduced.done(it * QB + t))
                    pe.sem_inc(passed_pe, 1)
                    nc.tensor.transpose(mx[:, bank_of[e], 0:P], neg_m[:, t % 2], ident[:, :]).then_inc(mx_done, 1)
                    return
                _, t, tt, h, c = e
                w = GT if c < tt // TG else (tt % TG + 1) * P
                nc.tensor.matmul(mx[:, bank_of[e], 0:w], qop[0:ROWS, slot, t, h, (tt - TG * t) * P:(tt - TG * t + 1) * P],
                                 kop[0:ROWS, slot, h, c * GT:c * GT + w], start=True, stop=True).then_inc(mx_done, 1)

            def first():
                pe.wait_ge(const_in, 32)
                pe.wait_ge(ones_set, 2)
                pe.wait_ge(qkv_in[0], LOADS)
                for i, e in enumerate(ahead):
                    before = [k for k in range(i) if bank_of[ahead[k]] == bank_of[e]]
                    entry(0, 0, e, before[-1] + 1 if before else None)

            def iteration(it, slot, use, with_next, with_load):
                pe.wait_ge(qkv_in[slot], use * LOADS + LOADS)
                def products(st):
                    t, j = steps[st]
                    n0 = max(0, j - TG * t) * P
                    if j == 0:
                        pe.wait_ge(o_copied.sem, o_copied.freed(it * QB + t, 1))
                    if st in diagonal:
                        pe.wait_ge(masked.sem, masked.done(it * (len(diagonal) * HP) + (diagonal.index(st) * HP + HP - 1)))
                    else:
                        pe.wait_ge(exp_done.sem, exp_done.done(it * NP + (st * HP + HP - 1)))
                    for h in range(HG):
                        at = slice(2 * D * h, 2 * D * (h + 1))
                        op = nc.tensor.matmul(pv[at, n0:], v[:, slot, j, at], prob[:, (st * HP + h // 2) % 4, h % 2, n0:],
                                              start=(j == 0), stop=(j == TG * (t + 1) - 1))
                    op.then_inc(pv_done.sem, 1)

                for st, (t, j) in enumerate(steps):
                    n0 = max(0, j - TG * t) * P
                    if j == 0:
                        pe.wait_ge(m_in[t], it * (16 * MROWS) + 2 * (16 * MROWS))
                    for hp in range(HP):
                        r = st * HP + hp
                        pe.wait_ge(exp_done.sem, exp_done.freed(it * NP + r, 2))
                        for hh in range(2):
                            op = nc.tensor.matmul(score[:, r % 2, hh, n0:],
                                                  kop[0:ROWS + MROWS, slot, hp * 2 + hh, j * P:(j + 1) * P],
                                                  qop[0:ROWS + MROWS, slot, t, hp * 2 + hh, n0:],
                                                  start=True, stop=True)
                        op.then_inc(score_done.sem, 1)
                        if r == LATE_TO * HP:
                            if with_next:
                                pe.wait_ge(qkv_in[1 - slot], (use + slot + 1) * LOADS)
                            else:
                                entry(it, slot, ("turn", LATE), entry_done(it, len(late) - 1))
                        for i in spots[r]:
                            e = period[i]
                            own = i < len(late) or e == ("turn", LATE)
                            if i < len(late) or with_next:
                                entry(it if own else it + 1, slot if own else 1 - slot, e, bank_freed(it, i))
                    if st > 0:
                        products(st - 1)
                products(NS - 1)

            schedule(pe, iteration, first)


def in_groups(eng, each, n=G):
    with eng.Fori(0, n // 2) as i:
        for slot in range(2):
            each(i * 2 + slot, slot, i)


def prefetched(sp, load, store, n=G):
    load(0, 0)
    load(1, 1)
    with sp.Fori(0, n // 2 - 1) as i:
        for slot in range(2):
            load(i * 2 + (slot + 2), slot)
            store(i * 2 + slot, slot)
    store(n - 2, 0)
    store(n - 1, 1)


def ffn_phase(nc, x_d, parts_d, o_d, den_d, rden_d, w1_d, b1_d, w2_d, b2_d, w_out_d, ident_d, x1_d, xn1T_d, parts1_d):
    GELUS = 4
    with ExitStack() as ctx:
        s = Space(nc, ctx, "ffn")
        ident = s.sb("ident", [P, P])
        ones = s.sb("ones", [1, P])
        zero = s.sb("zero", [P, KC])
        den = s.sb("den", [P, HEADS * N // P])
        rden = s.sb("rden", [P, HEADS * N // P])
        w1 = s.sb("w1", [P, FC, C])
        w2 = s.sb("w2", [P, KC, FF])
        sign = s.sb("sign", [P, FC * C])
        a1 = s.sb("a1", [P, FC])
        a2 = s.sb("a2", [P, KC])
        a2_wide = s.sb("a2_wide", [P, KC, P])
        a2_row = s.sb("a2_row", [P, C])
        bound = s.sb("bound", [P, FC])
        hid_scale = PowerScale(s, "hid_scale")
        b1 = s.sb("b1", [P, FC])
        b2 = s.sb("b2", [P, C])
        w1T = s.sb("w1T", [P, KC, FF], F16)
        w2T = s.sb("w2T", [P, FC, C], F16)
        wo = s.sb("wo", [P, KC, C])
        xp = s.sb("xp", [P, 2, 2, KC, GT], F16)
        o = s.sb("o", [P, 2, KC, GT])
        rd = s.sb("rd", [P, 2, KC, GT])
        att = s.sb("att", [P, 2, KC, GT])
        xin = s.sb("xin", [P, 2, TG, C])
        xb = s.sb("xb", [P, 2, TG, C])
        gelu = s.sb("gelu", [P, GELUS, GT])
        hid = s.sb("hid", [P, 2, 2, FC, GT], F16)
        scaled = s.sb("scaled", [P, TG, C])
        x1 = s.sb("x1", [P, 2, TG, C])
        hid_ps = s.ps("hid_ps", [P, 2, GT])
        out_ps = s.ps("out_ps", [P, TG, C])
        att_ps = s.ps("att_ps", [P, TG, C])
        turned = s.ps("turned", [P, KC, GT])
        ln = LayerNorm(s, turned, full=True)

        den_in, rden_done, rden_out = s.sem("den_in"), s.sem("rden_done"), s.sem("rden_out")
        w_in = s.sem("w_in")
        set_done = s.sem("set_done")
        zero_stored = s.sem("zero_stored")
        mean_done = s.sem("mean_done")
        a2_done = s.sem("a2_done")
        a2_kept = s.sem("a2_kept")
        sign_done = s.sem("sign_done")
        w_turned = s.step("w_turned")
        w_copied = s.step("w_copied", credit=1)
        xp_in = [s.sem(f"xp_in{p}") for p in range(2)]
        g_in = [s.sem(f"g_in{p}") for p in range(2)]
        att_done = s.step("att_done", credit=2)
        xb_done = s.step("xb_done", credit=2)
        past_wait = s.sem("past_wait")
        hid_done = s.step("hid_done", credit=2 * FC)
        gelu_done = s.step("gelu_done", credit=2)
        high_done = s.step("high_done")
        low_done = s.step("low_done", credit=GELUS)
        out_done = s.step("out_done", credit=2)
        sum_done = s.step("sum_done", credit=1)
        x1_done = s.step("x1_done", credit=2)
        x1_out = [s.sem(f"x1_out{p}") for p in range(2)]
        xn_out = [s.sem(f"xn_out{p}") for p in range(2)]
        G_LOADS = 16 * (1 + KC + 1)
        WLOADS = 16 * 6
        w1_turns = [(k, m) for k in range(KC) for m in range(0, FC, TG)]
        w2_turns = [m for m in range(0, FC, 2)]
        block = ctx.enter_context(nc.Block())

        @block.sync
        def _(sp):
            rows = den_d.rearrange("h (q t) -> (h q) t", q=P // HEADS)
            sp.dma_start(w1[:, :, :], w1_d.rearrange("(m p) c -> p m c", p=P)).then_inc(w_in, 16)
            sp.dma_start(w2[:, :, :], w2_d.rearrange("(k p) n -> p k n", p=P)).then_inc(w_in, 16)
            with nc.allow_non_contiguous_dma(reason="one value per partition"):
                sp.dma_start(b1[:, :], b1_d.rearrange("(m p) -> p m", p=P)).then_inc(w_in, 16)
            sp.dma_start(ident[:, :], ident_d).then_inc(w_in, 16)
            sp.dma_start(wo[:, :, :], w_out_d.rearrange("(k p) n -> p k n", p=P)).then_inc(w_in, 16)
            sp.dma_start(b2[:, :], b2_d.rearrange("(o c) -> o c", o=1).broadcast_to([P, C])).then_inc(w_in, 16)
            sp.dma_start(den[:, :], rows).then_inc(den_in, 16)

            def load_xn(g, slot, use):
                sp.wait_ge(hid_done.sem, hid_done.freed(g * FC + (FC - 1), 2 * FC))
                sp.sem_inc(past_wait, 1)
                for part in range(2):
                    sp.dma_start(xp[:, slot, part], parts_d[part, :, :, bass.ds(g * GT, GT)]).then_inc(xp_in[slot], 16)

            def load(g, slot, use):
                sp.wait_ge(att_done.sem, att_done.freed(g, 2))
                sp.wait_ge(xb_done.sem, xb_done.freed(g, 2))
                sp.sem_inc(past_wait, 1)
                toks = bass.ds(g * GT, GT)
                sp.dma_start(o[:, slot], o_d[:, toks].rearrange("(k p) t -> p k t", p=P)).then_inc(g_in[slot], 16)
                for k in range(KC):
                    heads = rden_d[k * P // D:(k + 1) * P // D, toks]
                    sp.dma_start(rd[:, slot, k], heads.unsqueeze(1).broadcast_to([P // D, D, GT]))\
                        .then_inc(g_in[slot], 16)
                sp.dma_start(xin[:, slot], x_d[toks, :].rearrange("(j p) c -> p j c", p=P)).then_inc(g_in[slot], 16)

            def store(g, slot, use):
                sp.wait_ge(x1_done.sem, x1_done.done(g))
                sp.sem_inc(past_wait, 1)
                sp.dma_start(x1_d[bass.ds(g * GT, GT), :].rearrange("(j p) c -> p j c", p=P), x1[:, slot])\
                    .then_inc(x1_out[slot], 16)

            def store_xn(g, slot, use):
                sp.wait_ge(ln.lo_done.sem, ln.lo_done.done(g))
                sp.sem_inc(past_wait, 1)
                cols = bass.ds(g * GT, GT)
                for part, buf in enumerate((ln.hi, ln.lo)):
                    sp.dma_start(parts1_d[part, :, :, cols], buf[:, slot]).then_inc(xn_out[slot], 16)
                dst = xn1T_d[:, :, bass.ds(g // (T // GT), 1), bass.ds(g % (T // GT) * GT + 1, GT)]
                sp.dma_start(dst.rearrange("p k b t -> p k (b t)"), ln.full[:, slot]).then_inc(xn_out[slot], 16)

            for slot in range(2):
                sp.sem_inc(x1_out[slot], 16)
                sp.sem_inc(xn_out[slot], 48)
                load_xn(slot, slot, 0)
            sp.wait_ge(rden_done, 1)
            sp.dma_start(rden_d.rearrange("h (q t) -> (h q) t", q=P // HEADS), rden[:, :]).then_inc(rden_out, 16)
            sp.wait_ge(rden_out, 16)
            for slot in range(2):
                load(slot, slot, 0)
            sp.wait_ge(set_done, 1)
            with nc.allow_non_contiguous_dma(reason="a column of zeros"):
                for b in range(B):
                    sp.dma_start(xn1T_d[:, :, b, 0], zero[:, :]).then_inc(zero_stored, 16)

            def body(m, with_load, with_x1, with_xn):
                g, slot, use = m
                if with_load:
                    load_xn(g + 2, slot, use)
                    load(g + 2, slot, use)
                if with_x1:
                    store(g - 1, 1 - slot, use)
                if with_xn:
                    store_xn(g - 2, slot, use)

            body((0, 0, 0), True, False, False)
            body((1, 1, 0), True, True, False)
            with sp.Fori(0, (G - 4) // 2) as i:
                for r in range(2):
                    body((i * 2 + (2 + r), r, i), True, True, True)
            for g in range(G - 2, G + 2):
                body((g, g % 2, 0), False, g - 1 < G, True)
            for slot in range(2):
                sp.wait_ge(x1_out[slot], 16 * (1 + G // 2))
                sp.wait_ge(xn_out[slot], 48 * (1 + G // 2))
            sp.wait_ge(zero_stored, 16 * B)

        @block.gpsimd
        def _(pool):
            att_done.open(pool)
            xb_done.open(pool)
            nc.gpsimd.memset(ones[:, :], 1.0)
            nc.gpsimd.memset(zero[:, :], 0.0).then_inc(set_done, 1)
            pool.wait_ge(w_in, WLOADS)

            def each(g, slot, use):
                pool.wait_ge(g_in[slot], use * G_LOADS + G_LOADS)
                pool.wait_ge(out_done.sem, out_done.freed(g, 2))
                pool.wait_ge(x1_done.sem, x1_done.freed(g, 2))
                pool.sem_inc(past_wait, 1)
                nc.gpsimd.tensor_tensor(att[:, slot], o[:, slot], rd[:, slot], ALU.mult).then_inc(att_done.sem, 1)
                for j in range(TG):
                    op = nc.gpsimd.tensor_tensor(xb[:, slot, j], xin[:, slot, j], b2[:, :], ALU.add)
                op.then_inc(xb_done.sem, 1)

            in_groups(pool, each)

        @block.vector
        def _(dve):
            w_copied.open(dve)
            x1_done.open(dve)
            sum_done.open(dve)
            low_done.open(dve)
            ln.xn_done.open(dve)
            ln.lo_done.open(dve)
            dve.wait_ge(w_in, WLOADS)
            nc.vector.tensor_reduce(a1[:, :], w1[:, :, :], AX.X, ALU.add, apply_absolute_value=True)
            nc.vector.tensor_reduce(a2[:, :], w2[:, :, :], AX.X, ALU.add, apply_absolute_value=True)
            nc.vector.scalar_tensor_tensor(bound[:, :], b1[:, :], -1.0, b1[:, :], ALU.mult, ALU.max).then_inc(mean_done, 1)
            dve.wait_ge(mean_done, 1)
            nc.vector.scalar_tensor_tensor(bound[:, :], bound[:, :], 1.0, a1[:, :], ALU.add, ALU.add)
            nc.vector.tensor_scalar(a2[:, :], a2[:, :], 1.0 / FF, None, ALU.mult).then_inc(mean_done, 1)
            dve.wait_ge(den_in, 16)
            nc.vector.reciprocal(rden[:, :], den[:, :]).then_inc(rden_done, 1)
            dve.wait_ge(mean_done, 2)
            nc.vector.tensor_scalar(a1[:, :], a1[:, :], 1.0 / C, None, ALU.mult)
            nc.vector.tensor_copy(a2_wide[:, :, :], a2[:, :].unsqueeze(2).broadcast_to([P, KC, P])).then_inc(mean_done, 1)
            nc.vector.tensor_reduce(hid_scale.top[:, :], bound[:, :], AX.X, ALU.max).then_inc(hid_scale.found, 1)
            n = 0
            for k, m in w1_turns:
                dve.wait_ge(w_turned.sem, w_turned.done(n))
                nc.vector.tensor_copy(w1T[:, k, m * P:(m + TG) * P], turned[:, n % 2]).then_inc(w_copied.sem, 1)
                n += 1
            hid_scale.vector(nc, dve, out_ps[0:1, 0, 0:P], out_ps[:, 0, P:P + 1])
            dve.wait_ge(a2_done, 1)
            dve.wait_ge(hid_scale.found, hid_scale.ready)
            nc.vector.tensor_scalar(a2_row[:, :], att_ps[:, 0, :], hid_scale.unscale[:, 0:1], None, ALU.mult)\
                .then_inc(a2_kept, 1)
            for m in w2_turns:
                dve.wait_ge(w_turned.sem, w_turned.done(n))
                nc.vector.tensor_copy(w2T[:, m:m + 2].rearrange("p m c -> p (m c)"), turned[:, n % 2])\
                    .then_inc(w_copied.sem, 1)
                n += 1
            dve.wait_ge(a2_kept, 1)

            def low(g, slot, use, chunks):
                for m in chunks:
                    c = g * FC + m
                    dve.wait_ge(high_done.sem, high_done.done(c))
                    nc.vector.scalar_tensor_tensor(hid[:, slot, 1, m], gelu[:, m % GELUS], hid_scale.scale[:, 0:1],
                                                   hid[:, slot, 0, m], ALU.mult, ALU.subtract).then_inc(low_done.sem, 1)

            def output(g, slot, use):
                dve.wait_ge(out_done.sem, out_done.done(g))
                dve.wait_ge(xb_done.sem, xb_done.done(g))
                dve.wait_ge(x1_out[slot], use * 16 + 16)
                dve.wait_ge(ln.xn_done.sem, ln.xn_done.freed(g, 2))
                dve.wait_ge(x1_done.sem, x1_done.freed(g, 1))
                nc.vector.tensor_tensor(scaled[:, :, :], out_ps[:, :, :],
                                        a2_row[:, :].unsqueeze(1).broadcast_to([P, TG, C]), ALU.mult)
                nc.vector.tensor_tensor(x1[:, slot], att_ps[:, :, :], xb[:, slot], ALU.add).then_inc(sum_done.sem, 1)
                dve.wait_ge(sum_done.sem, sum_done.done(g))
                nc.vector.tensor_tensor(x1[:, slot], x1[:, slot], scaled[:, :, :], ALU.add).then_inc(x1_done.sem, 1)

            def step(at):
                new, _, old = at
                if old:
                    output(*old)
                    dve.wait_ge(x1_done.sem, x1_done.done(old[0]))
                    ln.statistics(nc, dve, old[0], x1[:, old[1]])
                if new:
                    low(*new, range(0, 2))
                if old:
                    ln.normalise(nc, dve, old[0], old[1], x1[:, old[1]])
                if new:
                    low(*new, range(2, FC))
                if old:
                    g, slot, use = old
                    dve.wait_ge(xn_out[slot], use * 48 + 48)
                    ln.low(nc, dve, g, slot)

            rolling(dve, step, 3)

        @block.scalar
        def _(act):
            gelu_done.open(act)
            ln.hi_done.open(act)
            act.wait_ge(w_in, WLOADS)
            nc.scalar.activation(sign[:, :], w1[:, :, :].rearrange("p m c -> p (m c)"), ACT.Sign).then_inc(sign_done, 1)
            act.wait_ge(w_turned.sem, w_turned.done(len(w1_turns) - 1))
            nc.scalar.activation(sign[:, :], w2[:, :, :].rearrange("p k n -> p (k n)"), ACT.Sign).then_inc(sign_done, 1)
            act.wait_ge(mean_done, 3)
            act.wait_ge(hid_scale.found, hid_scale.ready)

            def hidden(g, slot, use):
                act.wait_ge(out_done.sem, out_done.freed(g, 2))
                for m in range(FC):
                    c = g * FC + m
                    act.wait_ge(hid_done.sem, hid_done.done(c))
                    act.wait_ge(low_done.sem, low_done.freed(c, GELUS))
                    nc.scalar.activation(gelu[:, m % GELUS], hid_ps[:, m % 2], ACT.Gelu, scale=a1[:, m:m + 1],
                                         bias=b1[:, m:m + 1]).then_inc(gelu_done.sem, 1)
                    if m > 0:
                        high(g, slot, m - 1)
                high(g, slot, FC - 1)

            def high(g, slot, m):
                act.wait_ge(gelu_done.sem, gelu_done.done(g * FC + m))
                nc.scalar.activation(hid[:, slot, 0, m], gelu[:, m % GELUS], ACT.Identity,
                                     scale=hid_scale.scale[:, 0:1]).then_inc(high_done.sem, 1)

            def step(at):
                new, _, old = at
                if new:
                    hidden(*new)
                if old:
                    g, slot, use = old
                    act.wait_ge(xn_out[slot], use * 48 + 48)
                    ln.high(nc, act, g, slot)

            rolling(act, step, 3)

        @block.tensor
        def _(pe):
            out_done.open(pe)
            hid_done.open(pe)
            ln.turn_done.open(pe)
            pe.wait_ge(w_in, WLOADS)
            pe.wait_ge(set_done, 1)
            pe.wait_ge(sign_done, 1)
            n = 0
            for k, m in w1_turns:
                if n >= 2:
                    pe.wait_ge(w_copied.sem, w_copied.done(n - 2))
                for i in range(TG):
                    src = sign[:, (m + i) * C + k * P:(m + i) * C + (k + 1) * P]
                    op = nc.tensor.transpose(turned[:, n % 2, i * P:(i + 1) * P], src, ident[:, :])
                op.then_inc(w_turned.sem, 1)
                n += 1
            hid_scale.tensor(nc, pe, out_ps[0:1, 0, 0:P], out_ps[:, 0, P:P + 1], ident[:, :], ones[:, :])
            pe.wait_ge(mean_done, 3)
            for k in range(KC):
                op = nc.tensor.matmul(att_ps[:, 0, k * P:(k + 1) * P], a2_wide[:, k], ident[:, :], start=True, stop=True)
            op.then_inc(a2_done, 1)
            pe.wait_ge(sign_done, 2)
            for m in w2_turns:
                pe.wait_ge(w_copied.sem, w_copied.done(n - 2))
                for i in range(2):
                    for k in range(KC):
                        src = sign[:, k * FF + (m + i) * P:k * FF + (m + i + 1) * P]
                        op = nc.tensor.transpose(turned[:, n % 2, (i * KC + k) * P:(i * KC + k + 1) * P], src, ident[:, :])
                op.then_inc(w_turned.sem, 1)
                n += 1
            pe.wait_ge(w_copied.sem, w_copied.done(n - 1))
            pe.wait_ge(a2_kept, 1)

            def hidden(g, slot, use, chunks):
                for m in chunks:
                    if m == 0:
                        pe.wait_ge(xp_in[slot], use * 32 + 32)
                    pe.wait_ge(gelu_done.sem, gelu_done.freed(g * FC + m, 2))
                    for k in range(KC):
                        for part in range(2):
                            op = nc.tensor.matmul(hid_ps[:, m % 2], w1T[:, k, m * P:(m + 1) * P],
                                                  xp[:, slot, part, k], start=(k == 0 and part == 0),
                                                  stop=(k == KC - 1 and part == 1))
                    op.then_inc(hid_done.sem, 1)

            def output(g, slot, use, j):
                if j == 0:
                    pe.wait_ge(att_done.sem, att_done.done(g))
                    pe.wait_ge(sum_done.sem, sum_done.freed(g, 1))
                    pe.wait_ge(low_done.sem, low_done.done(g * FC + FC - 1))
                at = slice(j * P, (j + 1) * P)
                for k in range(KC):
                    nc.tensor.matmul(att_ps[:, j], att[:, slot, k, at], wo[:, k], start=(k == 0), stop=(k == KC - 1))
                for m in range(FC):
                    for part in range(2):
                        op = nc.tensor.matmul(out_ps[:, j], hid[:, slot, part, m, at], w2T[:, m],
                                              start=(m == 0 and part == 0), stop=(m == FC - 1 and part == 1))
                if j == TG - 1:
                    op.then_inc(out_done.sem, 1)

            def step(at):
                new, mid, old = at
                for chunks, tile in (((0, 1, 2), 0), ((3, 4), 1), ((5, 6), 2), ((7,), 3)):
                    if new:
                        hidden(*new, chunks)
                    if old and tile == 2:
                        ln.turn(nc, pe, old[0], old[1], ident[:, :])
                    if mid:
                        output(*mid, tile)

            rolling(pe, step, 3)


def rwkv_phase(nc, xnT_d, mix_ds, w_ds, decay_d, first_d, ident_d, yT_d):
    NW = 3
    NO = NW * KC
    STEPS = G
    with ExitStack() as ctx:
        s = Space(nc, ctx, "rwkv")
        ident = s.sb("ident", [P, P])
        raw_w = s.sb("raw_w", [P, NW, KC, C])
        wT = s.sb("wT", [P, NW, KC, C])
        mix = s.sb("mix", [P, NW, KC])
        unmix = s.sb("unmix", [P, NW, KC])
        decay = s.sb("decay", [P, KC])
        first = s.sb("first", [P, KC])
        x = s.sb("x", [P, B, KC, GT + 1])
        xm = s.sb("xm", [P, B, NW, KC, GT])
        kvr = s.sb("kvr", [P, B, NW, KC, GT])
        p = s.sb("p", [P, B, KC, GT + 1])
        q = s.sb("q", [P, B, KC, GT + 1])
        d_raw = s.sb("d_raw", [P, KC, GT])
        e_raw = s.sb("e_raw", [P, KC, GT])
        d = s.sb("d", [P, B, KC, GT])
        e_old = s.sb("e_old", [P, B, KC, GT])
        e_new = s.sb("e_new", [P, B, KC, GT])
        by_q = s.sb("by_q", [P, B, KC, GT])
        by_v = s.sb("by_v", [P, B, KC, GT])
        y = s.sb("y", [P, B, KC, GT])
        prod = s.ps("prod", [P, NO, GT])
        turn_ps = s.ps("turn_ps", [P, GT])

        w_in = s.sem("w_in")
        state_set = s.sem("state_set")
        unmix_done = s.sem("unmix_done")
        w_turned = s.step("w_turned")
        w_copied = s.step("w_copied", credit=1)
        x_in = [s.sem(f"x_in{b}") for b in range(B)]
        past = s.sem("past")
        prev_done = s.step("prev_done")
        xm_done = s.step("xm_done", credit=2)
        prod_done = s.step("prod_done", credit=2 * NO)
        kvr_done = s.step("kvr_done", credit=NO)
        p_carried = s.step("p_carried")
        p_done = s.step("p_done")
        raw_done = s.step("raw_done")
        arg_done = s.step("arg_done", credit=1)
        gates_done = s.step("gates_done")
        times_v = s.step("times_v")
        q_carried = s.step("q_carried")
        q_done = s.step("q_done")
        wkv_done = s.step("wkv_done")
        y_done = s.step("y_done", credit=2)
        y_out = [s.sem(f"y_out{b}") for b in range(B)]
        WLOADS = 16 * (1 + 2 * NW + 2)
        block = ctx.enter_context(nc.Block())

        @block.sync
        def _(sp):
            sp.dma_start(ident[:, :], ident_d).then_inc(w_in, 16)
            for n in range(NW):
                sp.dma_start(raw_w[:, n], w_ds[n].rearrange("(k p) n -> p k n", p=P)).then_inc(w_in, 16)
            with nc.allow_non_contiguous_dma(reason="one value per partition"):
                for n in range(NW):
                    sp.dma_start(mix[:, n], mix_ds[n].rearrange("(k p) -> p k", p=P)).then_inc(w_in, 16)
                sp.dma_start(decay[:, :], decay_d.rearrange("(k p) -> p k", p=P)).then_inc(w_in, 16)
                sp.dma_start(first[:, :], first_d.rearrange("(k p) -> p k", p=P)).then_inc(w_in, 16)

            def load(n, b, use):
                sp.wait_ge(xm_done.sem, xm_done.freed(n, 2))
                src = xnT_d[:, :, b, bass.ds(use * GT, GT + 1)]
                sp.dma_start(x[:, b], src).then_inc(x_in[b], 16)

            def store(n, b, use):
                sp.wait_ge(y_done.sem, y_done.done(n))
                sp.dma_start(yT_d[:, :, bass.ds(use * GT + b * T, GT)], y[:, b]).then_inc(y_out[b], 16)

            for b in range(B):
                sp.sem_inc(y_out[b], 16)

            def step(at):
                if at[0]:
                    load(*at[0])
                if at[3]:
                    store(*at[3])

            rolling(sp, step, 4)
            for b in range(B):
                sp.wait_ge(y_out[b], 16 * (1 + STEPS // 2))

        @block.gpsimd
        def _(pool):
            for b in range(B):
                nc.gpsimd.memset(p[:, b, :, GT:], LOWEST)
                op = nc.gpsimd.memset(q[:, b, :, GT:], 0.0)
            op.then_inc(state_set, 1)
            pool.wait_ge(unmix_done, 1)

            def step(at):
                new, _, old = at
                if new:
                    n, b, use = new
                    pool.wait_ge(x_in[b], use * 16 + 16)
                    pool.wait_ge(prod_done.sem, prod_done.freed(n * NO + (NO - 1), 2 * NO))
                    pool.sem_inc(past, 1)
                    for w in range(NW):
                        for c in range(KC):
                            op = nc.gpsimd.tensor_scalar(xm[:, b, w, c], x[:, b, c, 0:GT], unmix[:, w, c:c + 1], 0.0,
                                                         ALU.mult, ALU.add)
                    op.then_inc(prev_done.sem, 1)
                if old:
                    n, b, use = old
                    pool.wait_ge(gates_done.sem, gates_done.done(n))
                    pool.wait_ge(kvr_done.sem, kvr_done.done(n * NO + (2 * KC - 1)))
                    pool.sem_inc(past, 1)
                    nc.gpsimd.tensor_tensor(e_new[:, b], e_new[:, b], kvr[:, b, 1], ALU.mult)
                    nc.gpsimd.tensor_tensor(by_v[:, b], by_v[:, b], kvr[:, b, 1], ALU.mult)\
                        .then_inc(times_v.sem, 1)

            rolling(pool, step, 3)

        @block.vector
        def _(dve):
            xm_done.open(dve)
            y_done.open(dve)
            w_copied.open(dve)
            arg_done.open(dve)
            dve.wait_ge(w_in, WLOADS)
            nc.vector.tensor_scalar(unmix[:, :, :], mix[:, :, :], -1.0, 1.0, ALU.mult, ALU.add).then_inc(unmix_done, 1)
            for n in range(NW):
                dve.wait_ge(w_turned.sem, w_turned.done(n))
                nc.vector.tensor_copy(wT[:, n].rearrange("p k e -> p (k e)"), turn_ps[:, :]).then_inc(w_copied.sem, 1)
            dve.wait_ge(state_set, 1)

            def blend(n, b, use):
                dve.wait_ge(prev_done.sem, prev_done.done(n))
                for w in range(NW):
                    for c in range(KC):
                        op = nc.vector.scalar_tensor_tensor(xm[:, b, w, c], x[:, b, c, 1:], mix[:, w, c:c + 1],
                                                            xm[:, b, w, c], ALU.mult, ALU.add)
                op.then_inc(xm_done.sem, 1)

            def state(n, b, use):
                dve.wait_ge(kvr_done.sem, kvr_done.done(n * NO + (KC - 1)))
                dve.wait_ge(y_done.sem, y_done.freed(n, 2))
                nc.vector.tensor_copy(p[:, b, :, 0:1], p[:, b, :, GT:]).then_inc(p_carried.sem, 1)
                dve.wait_ge(p_carried.sem, p_carried.done(n))
                for c in range(KC):
                    op = nc.vector.tensor_tensor_scan(p[:, b, c, 1:], decay[:, c:c + 1].broadcast_to([P, GT]),
                                                      kvr[:, b, 0, c], p[:, b, c, 0:1], ALU.add, ALU.max)
                op.then_inc(p_done.sem, 1)
                dve.wait_ge(p_done.sem, p_done.done(n))
                dve.wait_ge(arg_done.sem, arg_done.freed(n, 1))
                for c in range(KC):
                    nc.vector.scalar_tensor_tensor(d_raw[:, c], p[:, b, c, 0:GT], first[:, c:c + 1], kvr[:, b, 0, c],
                                                   ALU.subtract, ALU.subtract)
                    op = nc.vector.scalar_tensor_tensor(e_raw[:, c], p[:, b, c, 0:GT], decay[:, c:c + 1],
                                                        kvr[:, b, 0, c], ALU.add, ALU.subtract)
                op.then_inc(raw_done.sem, 1)
                dve.wait_ge(raw_done.sem, raw_done.done(n))
                nc.vector.tensor_scalar(d[:, b], d_raw[:, :, :], CLAMP, -CLAMP, ALU.min, ALU.max)
                nc.vector.tensor_scalar(e_old[:, b], e_raw[:, :, :], 0.0, -CLAMP, ALU.min, ALU.max)
                nc.vector.tensor_scalar(e_new[:, b], e_raw[:, :, :], CLAMP, 0.0, ALU.min, ALU.max)\
                    .then_inc(arg_done.sem, 1)

            def outcome(n, b, use):
                nc.vector.tensor_copy(q[:, b, :, 0:1], q[:, b, :, GT:]).then_inc(q_carried.sem, 1)
                dve.wait_ge(times_v.sem, times_v.done(n))
                dve.wait_ge(q_carried.sem, q_carried.done(n))
                for c in range(KC):
                    op = nc.vector.tensor_tensor_scan(q[:, b, c, 1:], e_old[:, b, c], e_new[:, b, c], q[:, b, c, 0:1],
                                                      ALU.mult, ALU.add)
                op.then_inc(q_done.sem, 1)
                dve.wait_ge(q_done.sem, q_done.done(n))
                nc.vector.tensor_tensor(by_q[:, b], by_q[:, b], q[:, b, :, 0:GT], ALU.mult).then_inc(wkv_done.sem, 1)
                dve.wait_ge(wkv_done.sem, wkv_done.done(n * 2))
                nc.vector.tensor_tensor(by_q[:, b], by_q[:, b], by_v[:, b], ALU.add).then_inc(wkv_done.sem, 1)
                dve.wait_ge(wkv_done.sem, wkv_done.done(n * 2 + 1))
                dve.wait_ge(kvr_done.sem, kvr_done.done(n * NO + (NO - 1)))
                dve.wait_ge(y_out[b], use * 16 + 16)
                nc.vector.tensor_tensor(y[:, b], by_q[:, b], kvr[:, b, 2], ALU.mult).then_inc(y_done.sem, 1)

            def step(at):
                for stage, group in zip((blend, state, outcome), at):
                    if group:
                        stage(*group)

            rolling(dve, step, 3)

        @block.scalar
        def _(act):
            kvr_done.open(act)

            def step(at):
                new, old = at
                if old:
                    n, b, use = old
                    act.wait_ge(arg_done.sem, arg_done.done(n))
                    nc.scalar.activation(by_q[:, b], d[:, b], ACT.Sigmoid)
                    nc.scalar.activation(by_v[:, b], d[:, b], ACT.Sigmoid, scale=-1.0)
                    nc.scalar.activation(e_old[:, b], e_old[:, b], ACT.Exp)
                    nc.scalar.activation(e_new[:, b], e_new[:, b], ACT.Exp, scale=-1.0).then_inc(gates_done.sem, 1)
                if new:
                    n, b, use = new
                    act.wait_ge(y_done.sem, y_done.freed(n, 2))
                    for o in range(NO):
                        w, c = o // KC, o % KC
                        act.wait_ge(prod_done.sem, prod_done.done(n * NO + o))
                        nc.scalar.activation(kvr[:, b, w, c], prod[:, o], ACT.Sigmoid if w == 2 else ACT.Identity)\
                            .then_inc(kvr_done.sem, 1)

            rolling(act, step, 2)

        @block.tensor
        def _(pe):
            prod_done.open(pe)
            pe.wait_ge(w_in, WLOADS)
            for n in range(NW):
                pe.wait_ge(w_copied.sem, w_copied.freed(n, 1))
                for k in range(KC):
                    for c in range(KC):
                        at = (k * KC + c) * P
                        op = nc.tensor.transpose(turn_ps[:, at:at + P], raw_w[:, n, c, k * P:(k + 1) * P], ident[:, :])
                op.then_inc(w_turned.sem, 1)
            pe.wait_ge(w_copied.sem, w_copied.done(NW - 1))

            def each(n, b, use):
                pe.wait_ge(xm_done.sem, xm_done.done(n))
                for o in range(NO):
                    w, c = o // KC, o % KC
                    pe.wait_ge(kvr_done.sem, kvr_done.freed(n * NO + o, NO))
                    for k in range(KC):
                        op = nc.tensor.matmul(prod[:, o], wT[:, w, k, c * P:(c + 1) * P], xm[:, b, w, k],
                                              start=(k == 0), stop=(k == KC - 1))
                    op.then_inc(prod_done.sem, 1)

            in_groups(pe, each)


def moe_phase(nc, x1_d, parts_d, yT_d, wo_d, router_d, gate_d, up_d, down_d, sgate_d, sup_d, sdown_d,
              lower_d, ident_d, coef_d, out_d):
    UNITS = E + ES // P
    SHARED = ES // P
    with ExitStack() as ctx:
        s = Space(nc, ctx, "moe")
        router = WeightSplit(s, "router", KC * E)
        sgate = WeightSplit(s, "sgate", KC * ES, after=router)
        sup = WeightSplit(s, "sup", KC * ES, after=sgate)
        gate = WeightSplit(s, "gate", KC * E * ED, after=sup)
        up = WeightSplit(s, "up", KC * E * ED, after=gate)
        splits = (router, sgate, sup, gate, up)
        ident = s.sb("ident", [P, P])
        ones = s.sb("ones", [1, P])
        lower = s.sb("lower", [P, E, E])
        raw_wo = s.sb("raw_wo", [P, KC, C])
        woT = s.sb("woT", [P, KC, C])
        down = s.sb("down", [P, UNITS, C])
        xp = s.sb("xp", [P, 2, 2, KC, GT], F16)
        yT = s.sb("yT", [P, 2, KC, GT])
        x1 = s.sb("x1", [P, 2, TG, C])
        top = s.sb("top", [P, TG])
        z = s.sb("z", [P, TG, E])
        ex = s.sb("ex", [P, TG, E])
        total = s.sb("total", [P, TG])
        inv = s.sb("inv", [P, TG])
        prob = s.sb("prob", [P, TG, E])
        above = s.sb("above", [P, TG, E, E])
        equal = s.sb("equal", [P, TG, E, E])
        rank = s.sb("rank", [P, TG, E])
        coef = s.sb("coef", [P, TG, E])
        coefT = s.sb("coefT", [TG * E, P])
        spread = s.sb("spread", [P, 2, TG, E, P])
        silu = s.sb("silu", [P, 2, GT])
        weighted = s.sb("weighted", [P, 2, GT])
        hid = s.sb("hid", [P, UNITS, GT])
        out = s.sb("out", [P, 2, TG, C])
        gate_ps = s.ps("gate_ps", [P, 2, GT])
        up_ps = s.ps("up_ps", [P, 2, GT])
        out_ps = s.ps("out_ps", [P, TG, C])
        logit_ps = s.ps("logit_ps", [P, GT])
        turn_ps = s.ps("turn_ps", [P, GT])

        w_in = s.sem("w_in")
        ones_set = s.sem("ones_set")
        wo_turned = s.sem("wo_turned")
        wo_copied = s.sem("wo_copied")
        xp_in = [s.sem(f"xp_in{p}") for p in range(2)]
        late_in = [s.sem(f"late_in{p}") for p in range(2)]
        spread_in = [s.sem(f"spread_in{p}") for p in range(2)]
        logit_done = s.step("logit_done")
        route = s.sem("route")
        exp_done = s.step("exp_done")
        past = s.sem("past")
        past_wait = s.sem("past_wait")
        coef_turned = s.step("coef_turned", credit=1)
        coefT_done = s.step("coefT_done")
        coef_out = s.step("coef_out", credit=1, unit=16)
        gate_done = s.step("gate_done")
        up_done = s.step("up_done", credit=2 * UNITS)
        silu_done = s.step("silu_done", credit=2)
        weighted_done = s.step("weighted_done", credit=2 * E)
        hid_done = s.step("hid_done", credit=2)
        down_done = s.step("down_done", credit=2)
        out_done = s.step("out_done", credit=2)
        stored = [s.sem(f"stored{p}") for p in range(2)]
        ROUTE = 11
        SPLIT_LOADS = 3 + 2 * KC
        WLOADS = 16 * 5
        block = ctx.enter_context(nc.Block())

        @block.sync
        def _(sp):
            sp.dma_start(ident[:, :], ident_d).then_inc(w_in, 16)
            sp.dma_start(router.w[:, :].rearrange("p (k e) -> p k e", k=KC),
                         router_d.rearrange("(k p) e -> p k e", p=P)).then_inc(router.loaded, 16)
            for w, src in ((sgate, sgate_d), (sup, sup_d)):
                sp.dma_start(w.w[:, :].rearrange("p (k n) -> p k n", k=KC),
                             src.rearrange("(k p) n -> p k n", p=P)).then_inc(w.loaded, 16)
            for w, src in ((gate, gate_d), (up, up_d)):
                for k in range(KC):
                    sp.dma_start(w.w[:, k * E * ED:(k + 1) * E * ED].rearrange("p (e d) -> p e d", e=E),
                                 src[:, k * P:(k + 1) * P, :].rearrange("e p d -> p e d")).then_inc(w.loaded, 16)
            sp.dma_start(lower[:, :, :], lower_d).then_inc(w_in, 16)
            sp.dma_start(raw_wo[:, :, :], wo_d.rearrange("(k p) n -> p k n", p=P)).then_inc(w_in, 16)
            sp.dma_start(down[:, 0:SHARED], sdown_d.rearrange("(k p) n -> p k n", p=P)).then_inc(w_in, 16)
            sp.dma_start(down[:, SHARED:], down_d.rearrange("e p n -> p e n")).then_inc(w_in, 16)

            def load(g, slot):
                toks = bass.ds(g * GT, GT)
                sp.wait_ge(up_done.sem, up_done.freed(g * UNITS + (UNITS - 1), 2 * UNITS))
                for part in range(2):
                    sp.dma_start(xp[:, slot, part], parts_d[part, :, :, toks]).then_inc(xp_in[slot], 16)

            def load_late(g, slot):
                toks = bass.ds(g * GT, GT)
                sp.wait_ge(out_done.sem, out_done.freed(g, 2))
                sp.sem_inc(past_wait, 1)
                sp.dma_start(yT[:, slot], yT_d[:, :, toks]).then_inc(late_in[slot], 16)
                sp.dma_start(x1[:, slot], x1_d[toks, :].rearrange("(j p) c -> p j c", p=P)).then_inc(late_in[slot], 16)

            def coefficients(g, slot):
                sp.wait_ge(coefT_done.sem, coefT_done.done(g))
                sp.dma_start(coef_d[bass.ds(g, 1), :, :].rearrange("o r t -> (o r) t"), coefT[:, :])\
                    .then_inc(coef_out.sem, 16)
                sp.wait_ge(coef_out.sem, coef_out.done(g))
                sp.wait_ge(weighted_done.sem, weighted_done.freed(g * E + (E - 1), 2 * E))
                row = coef_d[bass.ds(g, 1), :, :].rearrange("o r t -> o (r t)")
                sp.dma_start(spread[:, slot].rearrange("p j e t -> p (j e t)"), row.broadcast_to([P, TG * E * P]))\
                    .then_inc(spread_in[slot], 16)

            def store(g, slot):
                sp.wait_ge(out_done.sem, out_done.done(g))
                dst = out_d[bass.ds(g * GT, GT), :].rearrange("(j p) c -> p j c", p=P)
                sp.dma_start(dst, out[:, slot]).then_inc(stored[slot], 16)

            sp.sem_inc(coef_out.sem, 16)
            for slot in range(2):
                sp.sem_inc(stored[slot], 16)

            def step(at):
                new, old = at
                if new:
                    g, slot, use = new
                    load(g, slot)
                    load_late(g, slot)
                    coefficients(g, slot)
                if old:
                    store(old[0], old[1])

            rolling(sp, step, 2)
            for slot in range(2):
                sp.wait_ge(stored[slot], 16 * (1 + G // 2))

        @block.gpsimd
        def _(pool):
            weighted_done.open(pool)
            nc.gpsimd.memset(ones[:, :], 1.0).then_inc(ones_set, 1)

            def each(g, slot, use):
                pool.wait_ge(spread_in[slot], use * 16 + 16)
                for e in range(E):
                    u = SHARED + e
                    pool.wait_ge(silu_done.sem, silu_done.done(g * UNITS + u))
                    pool.wait_ge(hid_done.sem, hid_done.freed(g * UNITS + u, 2))
                    pool.sem_inc(past, 1)
                    nc.gpsimd.tensor_tensor(weighted[:, u % 2].rearrange("p (j t) -> p j t", j=TG), silu[:, u % 2].rearrange("p (j t) -> p j t", j=TG), spread[:, slot, :, e, :], ALU.mult)\
                        .then_inc(weighted_done.sem, 1)

            in_groups(pool, each)

        @block.vector
        def _(dve):
            hid_done.open(dve)
            out_done.open(dve)
            for w in splits:
                w.vector(nc, dve, logit_ps[0:1, 0:P], logit_ps[:, P:P + 1], SPLIT_LOADS)
            dve.wait_ge(wo_turned, 1)
            nc.vector.tensor_copy(woT[:, :, :].rearrange("p k e -> p (k e)"), turn_ps[:, :]).then_inc(wo_copied, 1)

            def over_e(t):
                return t.unsqueeze(2).broadcast_to([P, TG, E])

            def routing(g, slot, use):
                logits = logit_ps[:, 0:TG * E].rearrange("p (j e) -> p j e", j=TG)
                others = prob[:, :, :].unsqueeze(2).broadcast_to([P, TG, E, E])
                own = prob[:, :, :].unsqueeze(3).broadcast_to([P, TG, E, E])
                masks = lower[:, :, :].unsqueeze(1).broadcast_to([P, TG, E, E])
                at = g * ROUTE
                dve.wait_ge(logit_done.sem, logit_done.done(g))
                nc.vector.tensor_reduce(top[:, :], logits, AX.X, ALU.max).then_inc(route, 1)
                dve.wait_ge(route, at + 1)
                nc.vector.tensor_tensor(z[:, :, :], logits, over_e(top[:, :]), ALU.subtract).then_inc(route, 1)
                dve.wait_ge(exp_done.sem, exp_done.done(g))
                nc.vector.tensor_reduce(total[:, :], ex[:, :, :], AX.X, ALU.add).then_inc(route, 1)
                dve.wait_ge(route, at + 3)
                nc.vector.reciprocal(inv[:, :], total[:, :]).then_inc(route, 1)
                dve.wait_ge(route, at + 4)
                nc.vector.tensor_tensor(prob[:, :, :], ex[:, :, :], over_e(inv[:, :]), ALU.mult).then_inc(route, 1)
                dve.wait_ge(route, at + 5)
                nc.vector.tensor_tensor(above[:, :, :, :], others, own, ALU.is_gt).then_inc(route, 1)
                nc.vector.tensor_tensor(equal[:, :, :, :], others, own, ALU.is_equal).then_inc(route, 1)
                dve.wait_ge(route, at + 7)
                nc.vector.tensor_tensor(equal[:, :, :, :], equal[:, :, :, :], masks, ALU.mult).then_inc(route, 1)
                dve.wait_ge(route, at + 8)
                nc.vector.tensor_tensor(above[:, :, :, :], above[:, :, :, :], equal[:, :, :, :], ALU.add)\
                    .then_inc(route, 1)
                dve.wait_ge(route, at + 9)
                nc.vector.tensor_reduce(rank[:, :, :], above[:, :, :, :], AX.X, ALU.add).then_inc(route, 1)
                dve.wait_ge(route, at + 10)
                dve.wait_ge(coef_turned.sem, coef_turned.freed(g, 1))
                nc.vector.scalar_tensor_tensor(coef[:, :, :], rank[:, :, :], 1.5, prob[:, :, :], ALU.is_lt, ALU.mult)\
                    .then_inc(route, 1)
                dve.wait_ge(coef_turned.sem, coef_turned.done(g))
                dve.wait_ge(coef_out.sem, coef_out.freed(g, 1))
                nc.vector.tensor_copy(coefT[:, :], turn_ps[0:TG * E, 0:P]).then_inc(coefT_done.sem, 1)

            def hidden(g, slot, use):
                dve.wait_ge(down_done.sem, down_done.freed(g, 1))
                for u in range(UNITS):
                    n = g * UNITS + u
                    dve.wait_ge(up_done.sem, up_done.done(n))
                    if u < SHARED:
                        dve.wait_ge(silu_done.sem, silu_done.done(n))
                    else:
                        dve.wait_ge(weighted_done.sem, weighted_done.done(g * E + (u - SHARED)))
                    act = (silu if u < SHARED else weighted)[:, u % 2]
                    w = sup if u < SHARED else up
                    nc.vector.scalar_tensor_tensor(hid[:, u], up_ps[:, u % 2], w.unscale[:, 0:1], act,
                                                   ALU.mult, ALU.mult).then_inc(hid_done.sem, 1)

            def output(g, slot, use):
                dve.wait_ge(down_done.sem, down_done.done(g))
                dve.wait_ge(late_in[slot], use * 32 + 32)
                dve.wait_ge(stored[slot], use * 16 + 16)
                nc.vector.tensor_tensor(out[:, slot], out_ps[:, :, :], x1[:, slot], ALU.add).then_inc(out_done.sem, 1)

            def step(at):
                new, old = at
                if old:
                    hidden(*old)
                if new:
                    routing(*new)
                if old:
                    output(*old)

            rolling(dve, step, 2)

        @block.scalar
        def _(act):
            silu_done.open(act)
            for w in splits:
                act.wait_ge(w.found, w.ready)

            def step(at):
                new, old = at
                if old:
                    g, slot, use = old
                    for u in range(UNITS):
                        n = g * UNITS + u
                        act.wait_ge(gate_done.sem, gate_done.done(n))
                        act.wait_ge(hid_done.sem, hid_done.freed(n, 2))
                        w = sgate if u < SHARED else gate
                        nc.scalar.activation(silu[:, u % 2], gate_ps[:, u % 2], ACT.Silu, scale=w.unscale[:, 0:1])\
                            .then_inc(silu_done.sem, 1)
                if new:
                    g, slot, use = new
                    act.wait_ge(route, g * ROUTE + 2)
                    nc.scalar.activation(ex[:, :, :], z[:, :, :], ACT.Exp, scale=router.unscale[:, 0:1])\
                        .then_inc(exp_done.sem, 1)

            rolling(act, step, 2)

        @block.tensor
        def _(pe):
            up_done.open(pe)
            down_done.open(pe)
            coef_turned.open(pe)
            pe.wait_ge(w_in, WLOADS)
            pe.wait_ge(ones_set, 1)
            for k in range(KC):
                for c in range(KC):
                    at = (k * KC + c) * P
                    op = nc.tensor.transpose(turn_ps[:, at:at + P], raw_wo[:, c, k * P:(k + 1) * P], ident[:, :])
            op.then_inc(wo_turned, 1)
            for w in splits:
                w.tensor(nc, pe, logit_ps[0:1, 0:P], logit_ps[:, P:P + 1], ident[:, :], ones[:, :])
            for w in splits:
                pe.wait_ge(w.found, w.ready)
            pe.wait_ge(wo_copied, 1)

            def columns(w, start, k, width, total):
                at = slice(k * total + start, k * total + start + width)
                return w.hi[:, at], w.lo[:, at]

            def routing(g, slot, use):
                pe.wait_ge(xp_in[slot], use * 32 + 32)
                pe.sem_inc(past, 1)
                for j in range(TG):
                    at = slice(j * P, (j + 1) * P)
                    op = parts_matmul(nc, logit_ps[:, j * E:(j + 1) * E],
                                      [columns(router, 0, k, E, E) for k in range(KC)],
                                      [(xp[:, slot, 0, k, at], xp[:, slot, 1, k, at]) for k in range(KC)],
                                      weights_stationary=False)
                op.then_inc(logit_done.sem, 1)

            def turn(g, slot, use):
                pe.wait_ge(route, g * ROUTE + ROUTE)
                pe.sem_inc(past, 1)
                nc.tensor.transpose(turn_ps[0:TG * E, 0:P], coef[:, :, :].rearrange("p j e -> p (j e)"), ident[:, :])\
                    .then_inc(coef_turned.sem, 1)

            def hidden(g, slot, use):
                acts = [(xp[:, slot, 0, k], xp[:, slot, 1, k]) for k in range(KC)]
                for u in range(UNITS):
                    n = g * UNITS + u
                    a, b, at, width = ((sgate, sup, u * P, ES) if u < SHARED else
                                       (gate, up, (u - SHARED) * ED, E * ED))
                    pe.wait_ge(silu_done.sem, silu_done.freed(n, 2))
                    parts_matmul(nc, gate_ps[:, u % 2], [columns(a, at, k, P, width) for k in range(KC)], acts)\
                        .then_inc(gate_done.sem, 1)
                    pe.wait_ge(hid_done.sem, hid_done.freed(n, 2))
                    parts_matmul(nc, up_ps[:, u % 2], [columns(b, at, k, P, width) for k in range(KC)], acts)\
                        .then_inc(up_done.sem, 1)

            def output(g, slot, tiles):
                for j in tiles:
                    at = slice(j * P, (j + 1) * P)
                    for k in range(KC):
                        nc.tensor.matmul(out_ps[:, j], yT[:, slot, k, at], woT[:, k], start=(k == 0), stop=False)
                    for u in range(UNITS):
                        op = nc.tensor.matmul(out_ps[:, j], hid[:, u, at], down[:, u], start=False,
                                              stop=(u == UNITS - 1))
                return op

            def step(at):
                new, old = at
                if old:
                    hidden(*old)
                if new:
                    routing(*new)
                if old:
                    g, slot, use = old
                    pe.wait_ge(late_in[slot], use * 32 + 32)
                    pe.wait_ge(hid_done.sem, hid_done.done(g * UNITS + (UNITS - 1)))
                    pe.wait_ge(out_done.sem, out_done.freed(g, 1))
                    output(g, slot, range(0, TG // 2))
                if new:
                    turn(*new)
                if old:
                    output(g, slot, range(TG // 2, TG)).then_inc(down_done.sem, 1)

            rolling(pe, step, 2)


def program(nc, x, w_qkv, w_out, w1, b1, w2, b2, mix_k, mix_v, mix_r, w_k, w_v, w_r, w_o, decay, first,
            router, gate, up, down, sgate, sup, sdown, ident, cos, sin, tri, lower, out):

    def scratch(name, shape, dt=F32):
        return nc.dram_tensor(name, shape, dt, kind="Internal").ap()

    x = x.rearrange("b t c -> (b t) c")
    out = out.rearrange("b t c -> (b t) c")
    parts0 = scratch("parts0", [2, P, KC, N], F16)
    qk = scratch("qk", [2, C, 3, N], BF16)
    va = scratch("va", [NIT, P, T // P, HG * 2 * D])
    heads_out = scratch("heads_out", [C, N])
    den = scratch("den", [HEADS, N])
    rden = scratch("rden", [HEADS, N])
    x1 = scratch("x1", [N, C])
    xn1T = scratch("xn1T", [P, KC, B, T + 1])
    parts1 = scratch("parts1", [2, P, KC, N], F16)
    yT = scratch("yT", [P, KC, N])
    coef = scratch("coef", [G, TG * E, P])

    qkv_phase(nc, x, w_qkv, cos, sin, ident, parts0, qk, va)
    attention_phase(nc, qk, va, ident, tri, heads_out, den)
    ffn_phase(nc, x, parts0, heads_out, den, rden, w1, b1, w2, b2, w_out, ident, x1, xn1T,
              parts1)
    rwkv_phase(nc, xn1T, (mix_k, mix_v, mix_r), (w_k, w_v, w_r), decay, first, ident, yT)
    moe_phase(nc, x1, parts1, yT, w_o, router, gate, up, down, sgate, sup, sdown, lower, ident, coef, out)


def shape_tables():
    row = np.arange(P)
    freqs = np.arange(T, dtype=np.float32)[None] * (
        1.0 / np.float32(10000.0) ** (np.arange(0, D, 2, dtype=np.float32) / np.float32(D))
    ).astype(np.float32)[row % D // 2][:, None]
    sign = np.where(row % 2 == 0, -1.0, 1.0)[:, None]
    tri = np.zeros((P, GT), np.float32)
    tri[:, GT - P:] = np.where(row[None] > row[:, None], -1e37, 0.0)
    lower = np.broadcast_to(np.tril(np.ones((E, E), np.float32), -1), (P, E, E))
    return {
        "ident": np.eye(P, dtype=np.float32),
        "cos": np.cos(freqs).astype(np.float32),
        "sin": (np.sin(freqs) * sign).astype(np.float32),
        "tri": tri,
        "lower": np.ascontiguousarray(lower),
    }


INPUTS = (
    "L0_attn_x", "L0_attn_w_qkv", "L0_attn_w_out", "L0_ffn_w1", "L0_ffn_b1", "L0_ffn_w2", "L0_ffn_b2",
    "L1_attn_time_mix_k", "L1_attn_time_mix_v", "L1_attn_time_mix_r", "L1_attn_W_k", "L1_attn_W_v", "L1_attn_W_r",
    "L1_attn_W_o", "L1_attn_time_decay", "L1_attn_time_first", "L1_ffn_router", "L1_ffn_experts_gate",
    "L1_ffn_experts_up", "L1_ffn_experts_down", "L1_ffn_shared_gate", "L1_ffn_shared_up", "L1_ffn_shared_down",
)


def kernel(**inputs):
    import concourse.bacc as bacc
    from concourse.bass_utils import run_bass_kernel_spmd

    nc = bacc.Bacc("TRN2", target_bir_lowering=False, num_devices=1)
    arrays = {name: np.ascontiguousarray(inputs[name]) for name in INPUTS}
    arrays.update(shape_tables())
    args = [nc.dram_tensor(f"in_{name}", a.shape, mybir.dt.from_np(a.dtype), kind="ExternalInput").ap()
            for name, a in arrays.items()]
    out = nc.dram_tensor("out", (B, T, C), F32, kind="ExternalOutput").ap()
    program(nc, *args, out)
    result = run_bass_kernel_spmd(nc, [{f"in_{name}": a for name, a in arrays.items()}], core_ids=[0])
    return result.results[0]["out"]
```

```python
from contextlib import ExitStack

import numpy as np

import concourse.bass as bass
from concourse import mybir

F32 = mybir.dt.float32
BF16 = mybir.dt.bfloat16
F16 = mybir.dt.float16
I32 = mybir.dt.int32
ALU = mybir.AluOpType
ACT = mybir.ActivationFunctionType
AX = mybir.AxisListType

P = 128
B, T, C = 2, 2048, 256
N = B * T
KC = C // P
GT = 512
G = N // GT
TG = GT // P
HEADS, D = 16, C // 16
HG = 4
NIT = B * HEADS // HG
FF = 1024
FC = FF // P
E, ED, ES = 8, 128, 256
LN_EPS = 1e-5
LOWEST = -3.0e38
CLAMP = 30.0


class Step:

    def __init__(self, sem, credit=0, unit=1):
        self.sem, self.credit, self.unit = sem, credit, unit

    def open(self, eng):
        eng.sem_inc(self.sem, self.credit * self.unit)

    def done(self, n):
        return (n + (self.credit + 1)) * self.unit

    def freed(self, n, ring):
        return (n + (self.credit + 1 - ring)) * self.unit


class Space:

    def __init__(self, nc, ctx, phase):
        self.nc, self.ctx, self.phase = nc, ctx, phase

    def sb(self, name, shape, dt=F32):
        return self.ctx.enter_context(self.nc.sbuf_tensor(f"{self.phase}_{name}", shape, dt))

    def ps(self, name, shape, dt=F32):
        return self.ctx.enter_context(self.nc.psum_tensor(f"{self.phase}_{name}", shape, dt))

    def sem(self, name):
        return self.ctx.enter_context(self.nc.semaphore(f"{self.phase}_{name}"))

    def step(self, name, credit=0, unit=1):
        return Step(self.sem(name), credit, unit)


def parts_matmul(nc, out, weights, acts, weights_stationary=True):
    n = len(weights)
    last = None
    for k in range(n):
        (wh, wl), (xh, xl) = weights[k], acts[k]
        for m, (w, x) in enumerate(((wh, xh), (wl, xh), (wh, xl))):
            lhsT, rhs = (w, x) if weights_stationary else (x, w)
            last = nc.tensor.matmul(out, lhsT, rhs, start=(k == 0 and m == 0), stop=(k == n - 1 and m == 2))
    return last


class PowerScale:

    STEPS, TURNS = 8, 2
    LEAST = 2.0 ** -27

    def __init__(self, s, name, count=1, after=None):
        self.count = count
        self.first_step = after.ready if after else 0
        self.first_turn = after.first_turn + after.TURNS if after else 0
        self.ready = self.first_step + self.STEPS
        self.top = s.sb(f"{name}_top", [P, count])
        self.top_all = s.sb(f"{name}_top_all", [count, 1])
        self.apart = s.sb(f"{name}_apart", [count, count])
        self.power = s.sb(f"{name}_power", [P, count])
        self.scale = s.sb(f"{name}_scale", [P, count])
        self.unscale = s.sb(f"{name}_unscale", [P, count])
        self.found = after.found if after else s.sem(f"{name}_found")
        self.turned = after.turned if after else s.sem(f"{name}_turned")

    def vector(self, nc, dve, turn, spread, ident):
        n, at = self.count, self.first_step
        dve.wait_ge(self.turned, self.first_turn + 1)
        nc.vector.tensor_reduce(self.top_all[:, :], turn, AX.X, ALU.max).then_inc(self.found, 1)
        dve.wait_ge(self.found, at + 2)
        nc.vector.tensor_scalar(self.apart[:, :], ident[0:n, 0:n], self.top_all[:, 0:1], None, ALU.mult)\
            .then_inc(self.found, 1)
        dve.wait_ge(self.turned, self.first_turn + 2)
        nc.vector.tensor_scalar(self.power[:, :], spread, self.LEAST, None, ALU.max).then_inc(self.found, 1)
        dve.wait_ge(self.found, at + 4)
        nc.vector.tensor_scalar(self.unscale[:, :].bitcast(I32), self.power[:, :].bitcast(I32), 0x7F800000,
                                None, ALU.bitwise_and).then_inc(self.found, 1)
        dve.wait_ge(self.found, at + 5)
        nc.vector.tensor_scalar(self.scale[:, :].bitcast(I32), self.unscale[:, :].bitcast(I32), 0x7F800000,
                                None, ALU.bitwise_xor).then_inc(self.found, 1)
        dve.wait_ge(self.found, at + 6)
        nc.vector.tensor_scalar(self.scale[:, :], self.scale[:, :], 2.0 ** 12, None, ALU.mult).then_inc(self.found, 1)
        nc.vector.tensor_scalar(self.unscale[:, :], self.unscale[:, :], 2.0 ** -13, None, ALU.mult)\
            .then_inc(self.found, 1)

    def tensor(self, nc, pe, turn, spread, ident, ones):
        pe.wait_ge(self.found, self.first_step + 1)
        nc.tensor.matmul(turn, self.top[:, :], ident, start=True, stop=True).then_inc(self.turned, 1)
        pe.wait_ge(self.found, self.first_step + 3)
        nc.tensor.matmul(spread, ones[0:self.count, :], self.apart[:, :], start=True, stop=True)\
            .then_inc(self.turned, 1)


class WeightSplit(PowerScale):

    STEPS = 10

    def __init__(self, s, name, width):
        super().__init__(s, name)
        self.w = s.sb(f"{name}_w", [P, width])
        self.hi = s.sb(f"{name}_hi", [P, width], F16)
        self.lo = s.sb(f"{name}_lo", [P, width], F16)
        self.loaded = s.sem(f"{name}_loaded")

    def vector(self, nc, dve, turn, spread, ident):
        dve.wait_ge(self.loaded, 16)
        nc.vector.tensor_reduce(self.top[:, :], self.w[:, :], AX.X, ALU.max,
                                apply_absolute_value=True).then_inc(self.found, 1)
        super().vector(nc, dve, turn, spread, ident)
        dve.wait_ge(self.found, 8)
        nc.vector.tensor_scalar(self.hi[:, :], self.w[:, :], self.scale[:, 0:1], None, ALU.mult).then_inc(self.found, 1)
        dve.wait_ge(self.found, 9)
        nc.vector.scalar_tensor_tensor(self.lo[:, :], self.w[:, :], self.scale[:, 0:1], self.hi[:, :],
                                       ALU.mult, ALU.subtract).then_inc(self.found, 1)


class LayerNorm:

    NEWTON = 3
    SMALL = 5 + 3 * NEWTON
    GUESS = 2.0 ** -((0x7FFFFFFF - 0x5F3759DF) / 2 ** 23)

    def __init__(self, s, turned, full=False):
        self.turned = turned
        self.stats = s.sb("ln_stats", [P, TG, 6])
        self.mv = s.sb("ln_mv", [P, TG, 2])
        self.ve = s.sb("ln_ve", [P, TG])
        self.guess = s.sb("ln_guess", [P, TG])
        self.nt = s.sb("ln_nt", [P, TG])
        self.r = s.sb("ln_r", [P, TG])
        self.xn = s.sb("ln_xn", [P, 2, TG, C])
        self.hi = s.sb("ln_hi", [P, 2, KC, GT], F16)
        self.lo = s.sb("ln_lo", [P, 2, KC, GT], F16)
        self.full = s.sb("ln_full", [P, 2, KC, GT]) if full else None
        self.found = s.sem("ln_found")
        self.past = s.sem("ln_past")
        self.xn_done = s.step("ln_xn_done", credit=2)
        self.turn_done = s.step("ln_turn_done", credit=2)
        self.hi_done = s.step("ln_hi_done", credit=2)
        self.lo_done = s.step("ln_lo_done", credit=2)

    def statistics(self, nc, dve, n, x):
        at = n * self.SMALL
        dve.wait_ge(self.xn_done.sem, self.xn_done.freed(n, 1))
        dve.sem_inc(self.past, 1)
        for j in range(TG):
            op = nc.vector.bn_stats(self.stats[:, j], x[:, j])
        op.then_inc(self.found, 1)
        dve.wait_ge(self.found, at + 1)
        dve.sem_inc(self.past, 1)
        for j in range(TG):
            op = nc.vector.bn_aggr(self.mv[:, j], self.stats[:, j])
        op.then_inc(self.found, 1)
        dve.wait_ge(self.found, at + 2)
        nc.vector.tensor_scalar(self.ve[:, :], self.mv[:, :, 1], LN_EPS, None, ALU.add).then_inc(self.found, 1)

    def normalise(self, nc, dve, n, slot, x):
        at = n * self.SMALL
        dve.wait_ge(self.found, at + 3)
        nc.vector.tensor_scalar(self.guess[:, :].bitcast(I32), self.ve[:, :].bitcast(I32), 1, 0x7FFFFFFF,
                                ALU.logical_shift_right, ALU.bitwise_xor).then_inc(self.found, 1)
        dve.wait_ge(self.found, at + 4)
        nc.vector.tensor_scalar(self.r[:, :], self.guess[:, :], self.GUESS, None, ALU.mult).then_inc(self.found, 1)
        for i in range(self.NEWTON):
            dve.wait_ge(self.found, at + 5 + 3 * i)
            nc.vector.scalar_tensor_tensor(self.nt[:, :], self.r[:, :], -0.5, self.r[:, :], ALU.mult, ALU.mult)\
                .then_inc(self.found, 1)
            dve.wait_ge(self.found, at + 6 + 3 * i)
            nc.vector.tensor_tensor(self.nt[:, :], self.nt[:, :], self.ve[:, :], ALU.mult).then_inc(self.found, 1)
            dve.wait_ge(self.found, at + 7 + 3 * i)
            nc.vector.scalar_tensor_tensor(self.r[:, :], self.nt[:, :], 1.5, self.r[:, :], ALU.add, ALU.mult)\
                .then_inc(self.found, 1)
        dve.wait_ge(self.found, at + self.SMALL)
        dve.wait_ge(self.turn_done.sem, self.turn_done.freed(n, 2))
        for j in range(TG):
            op = nc.vector.tensor_scalar(self.xn[:, slot, j], x[:, j], self.mv[:, j, 0:1], self.r[:, j:j + 1],
                                         ALU.subtract, ALU.mult)
        op.then_inc(self.xn_done.sem, 1)

    def turn(self, nc, pe, n, slot, ident):
        pe.wait_ge(self.xn_done.sem, self.xn_done.done(n))
        pe.wait_ge(self.hi_done.sem, self.hi_done.freed(n, 1))
        pe.wait_ge(self.lo_done.sem, self.lo_done.freed(n, 1))
        for k in range(KC):
            for j in range(TG):
                op = nc.tensor.transpose(self.turned[:, k, j * P:(j + 1) * P], self.xn[:, slot, j, k * P:(k + 1) * P],
                                         ident)
        op.then_inc(self.turn_done.sem, 1)

    def high(self, nc, act, n, slot):
        act.wait_ge(self.turn_done.sem, self.turn_done.done(n))
        if self.full is not None:
            nc.scalar.copy(self.full[:, slot], self.turned[:, :, :])
        nc.scalar.copy(self.hi[:, slot], self.turned[:, :, :]).then_inc(self.hi_done.sem, 1)

    def low(self, nc, dve, n, slot):
        dve.wait_ge(self.hi_done.sem, self.hi_done.done(n))
        nc.vector.tensor_tensor(self.lo[:, slot], self.turned[:, :, :], self.hi[:, slot], ALU.subtract)\
            .then_inc(self.lo_done.sem, 1)


class LateWeights:

    NW = 4
    BANKS = 4

    def __init__(self, s, staging):
        self.w1_turns = [(k, m) for k in range(KC) for m in range(0, FC, TG)]
        self.w2_turns = list(range(0, FC, 2))
        self.GROUPS = len(self.w1_turns) + len(self.w2_turns) + self.NW
        self.b1 = s.sb("b1", [P, FC])
        self.a1 = s.sb("a1", [P, FC])
        self.a2_wide = s.sb("a2_wide", [P, KC, P])
        self.hid_scale = PowerScale(s, "hid_scale")
        self.w1T = s.sb("w1T", [P, KC, FF], F16)
        self.w2T = s.sb("w2T", [P, FC, C], F16)
        self.mixT = s.sb("mixT", [P, self.NW, KC, C])
        self.mix = s.sb("mix", [P, self.NW - 1, KC])
        self.unmix = s.sb("unmix", [P, self.NW - 1, KC])
        self.decay = s.sb("decay", [P, KC])
        self.first = s.sb("first", [P, KC])
        self.w1 = staging.sb("w1", [P, FC, C])
        self.w2 = staging.sb("w2", [P, KC, FF])
        self.raw = staging.sb("raw", [P, self.NW, KC, C])
        self.a2 = staging.sb("a2", [P, KC])
        self.bound = staging.sb("bound", [P, FC])
        self.ffn_in = s.sem("ffn_in")
        self.mixing_in = s.sem("mixing_in")
        self.MIXING = 16 * (self.NW + self.NW - 1 + 2)
        self.sign_done = s.sem("sign_done")
        self.turned = s.sem("turned")
        self.copied = s.sem("copied")
        self.mean_done = s.sem("mean_done")

    def load(self, nc, sp, w1_d, b1_d, w2_d, mixing_ds, mix_ds, decay_d, first_d):
        for n, src in enumerate(mixing_ds):
            sp.dma_start(self.raw[:, n], src.rearrange("(k p) n -> p k n", p=P)).then_inc(self.mixing_in, 16)
        sp.dma_start(self.w1[:, :, :], w1_d.rearrange("(m p) c -> p m c", p=P)).then_inc(self.ffn_in, 16)
        sp.dma_start(self.w2[:, :, :], w2_d.rearrange("(k p) n -> p k n", p=P)).then_inc(self.ffn_in, 16)
        with nc.allow_non_contiguous_dma(reason="one value per partition"):
            sp.dma_start(self.b1[:, :], b1_d.rearrange("(m p) -> p m", p=P)).then_inc(self.ffn_in, 16)
            for dst, src in [(self.mix[:, n], mix_ds[n]) for n in range(self.NW - 1)] + [
                    (self.decay[:, :], decay_d), (self.first[:, :], first_d)]:
                sp.dma_start(dst, src.rearrange("(k p) -> p k", p=P)).then_inc(self.mixing_in, 16)

    def open(self, s):
        self.sign1 = s.sb("sign1", [P, FC, C])
        self.sign2 = s.sb("sign2", [P, KC, FF])

    def turn(self, nc, pe, n, banks, ident):
        n1, n2 = self.NW, self.NW + len(self.w1_turns)
        bank = banks[n % self.BANKS]
        if n < n1:
            blocks = [self.raw[:, n, c, k * P:(k + 1) * P] for k in range(KC) for c in range(KC)]
            pe.wait_ge(self.mixing_in, self.MIXING)
        elif n < n2:
            k, m = self.w1_turns[n - n1]
            blocks = [self.sign1[:, m + i, k * P:(k + 1) * P] for i in range(TG)]
            pe.wait_ge(self.sign_done, 1)
        else:
            m = self.w2_turns[n - n2]
            blocks = [self.sign2[:, k, (m + i) * P:(m + i + 1) * P] for i in range(2) for k in range(KC)]
            pe.wait_ge(self.sign_done, 2)
        if n >= self.BANKS:
            pe.wait_ge(self.copied, n - self.BANKS + 1)
        for i, block in enumerate(blocks):
            op = nc.tensor.transpose(bank[:, i * P:(i + 1) * P], block, ident)
        op.then_inc(self.turned, 1)

    def scalar(self, nc, act, banks):
        act.wait_ge(self.ffn_in, 16 * 3)
        nc.scalar.activation(self.sign1[:, :, :], self.w1[:, :, :], ACT.Sign).then_inc(self.sign_done, 1)
        nc.scalar.activation(self.sign2[:, :, :], self.w2[:, :, :], ACT.Sign).then_inc(self.sign_done, 1)
        dst = [self.mixT[:, n].rearrange("p k e -> p (k e)") for n in range(self.NW)]
        dst += [self.w1T[:, k, m * P:(m + TG) * P] for k, m in self.w1_turns]
        dst += [self.w2T[:, m:m + 2].rearrange("p m c -> p (m c)") for m in self.w2_turns]
        for n in range(self.GROUPS):
            act.wait_ge(self.turned, n + 1)
            nc.scalar.copy(dst[n], banks[n % self.BANKS]).then_inc(self.copied, 1)

    def means(self, nc, dve):
        dve.wait_ge(self.mixing_in, self.MIXING)
        nc.vector.tensor_scalar(self.unmix[:, :, :], self.mix[:, :, :], -1.0, 1.0, ALU.mult, ALU.add)
        dve.wait_ge(self.ffn_in, 16 * 3)
        nc.vector.tensor_reduce(self.a1[:, :], self.w1[:, :, :], AX.X, ALU.add, apply_absolute_value=True)
        nc.vector.tensor_reduce(self.a2[:, :], self.w2[:, :, :], AX.X, ALU.add, apply_absolute_value=True)
        nc.vector.scalar_tensor_tensor(self.bound[:, :], self.b1[:, :], -1.0, self.b1[:, :], ALU.mult, ALU.max)\
            .then_inc(self.mean_done, 1)
        dve.wait_ge(self.mean_done, 1)
        nc.vector.scalar_tensor_tensor(self.bound[:, :], self.bound[:, :], 1.0, self.a1[:, :], ALU.add, ALU.add)
        nc.vector.tensor_scalar(self.a2[:, :], self.a2[:, :], 1.0 / FF, None, ALU.mult).then_inc(self.mean_done, 1)
        dve.wait_ge(self.mean_done, 2)
        nc.vector.tensor_scalar(self.a1[:, :], self.a1[:, :], 1.0 / C, None, ALU.mult)
        nc.vector.tensor_copy(self.a2_wide[:, :, :], self.a2[:, :].unsqueeze(2).broadcast_to([P, KC, P]))
        nc.vector.tensor_reduce(self.hid_scale.top[:, :], self.bound[:, :], AX.X, ALU.max).then_inc(self.hid_scale.found, 1)


class ExpertWeights:

    ROUTER, GATE, UP = 0, 1, 2
    EXPERTS = 3
    DOWN = EXPERTS + 2 * E
    SHARED = ES // P
    PAIRS = 1 + E
    ROUTER_SPLIT = 2

    def __init__(self, s):
        self.ident = s.sb("ident", [P, P])
        self.ones = s.sb("ones", [self.DOWN + 1, P])
        self.scales = PowerScale(s, "weights", self.DOWN + 1)
        self.router_w = s.sb("router_w", [P, KC, E])
        self.router_p = s.sb("router_p", [P, 2, KC, E], F16)
        self.shared_w = s.sb("shared_w", [P, 2, KC, ES])
        self.shared_p = s.sb("shared_p", [P, 2, 2, KC, ES], F16)
        self.expert_w = s.sb("expert_w", [P, 2, KC, E, ED])
        self.down_w = s.sb("down_w", [P, self.SHARED + E, C])
        self.pair = s.sb("pair", [P, self.PAIRS])
        self.unpair = s.sb("unpair", [P, self.PAIRS])
        self.least = s.sb("least", [P, 1])
        self.most = s.sb("most", [P, 1])
        self.up_scale = s.sb("up_scale", [P, self.PAIRS])
        self.out_unscale = s.sb("out_unscale", [P, 1])
        self.loaded = s.sem("loaded")
        self.ones_set = s.sem("ones_set")
        self.split = s.sem("split")
        self.factor = s.sem("factor")

    def unit_split(self, u):
        return self.ROUTER_SPLIT + 4 * (u + 1)

    def load(self, sp, router_d, gate_d, up_d, down_d, sgate_d, sup_d, sdown_d, ident_d):
        sp.dma_start(self.ident[:, :], ident_d).then_inc(self.loaded, 16)
        sp.dma_start(self.router_w[:, :, :], router_d.rearrange("(k p) e -> p k e", p=P)).then_inc(self.loaded, 16)
        for n, src in enumerate((sgate_d, sup_d)):
            sp.dma_start(self.shared_w[:, n], src.rearrange("(k p) n -> p k n", p=P)).then_inc(self.loaded, 16)
        for n, src in enumerate((gate_d, up_d)):
            for k in range(KC):
                sp.dma_start(self.expert_w[:, n, k], src[:, k * P:(k + 1) * P, :].rearrange("e p d -> p e d"))\
                    .then_inc(self.loaded, 16)
        sp.dma_start(self.down_w[:, 0:self.SHARED], sdown_d.rearrange("(k p) n -> p k n", p=P)).then_inc(self.loaded, 16)
        sp.dma_start(self.down_w[:, self.SHARED:], down_d.rearrange("e p n -> p e n")).then_inc(self.loaded, 16)

    LOADED = 16 * (6 + 2 * KC)

    def cells(self, bank):
        n = self.scales.count
        return bank[0:n, 0:P], bank[:, P:P + n]

    def tensor(self, nc, pe, bank):
        pe.wait_ge(self.ones_set, 1)
        turn, spread = self.cells(bank)
        self.scales.tensor(nc, pe, turn, spread, self.ident[:, :], self.ones)

    def parts_of(self, nc, dve, p, w, scale, after):
        nc.vector.tensor_scalar(p[0], w, scale, None, ALU.mult).then_inc(self.split, 1)
        dve.wait_ge(self.split, after)
        nc.vector.scalar_tensor_tensor(p[1], w, scale, p[0], ALU.mult, ALU.subtract).then_inc(self.split, 1)

    def expert_scale(self, n, e):
        return self.scales.scale[:, self.EXPERTS + n * E + e:self.EXPERTS + n * E + e + 1]

    GATES, UPS = slice(EXPERTS, EXPERTS + E), slice(EXPERTS + E, DOWN)

    def maxima(self, nc, dve):
        top = self.scales.top
        dve.wait_ge(self.loaded, self.LOADED)
        nc.vector.tensor_reduce(top[:, 0:1], self.router_w[:, :, :], AX.XY, ALU.max, apply_absolute_value=True)
        nc.vector.tensor_reduce(top[:, 1:3], self.shared_w[:, :, :, :], AX.XY, ALU.max, apply_absolute_value=True)
        for n, cols in enumerate((self.GATES, self.UPS)):
            nc.vector.tensor_reduce(top[:, cols], self.expert_w[:, n].rearrange("p k e d -> p e k d"), AX.XY,
                                    ALU.max, apply_absolute_value=True)
        nc.vector.tensor_reduce(top[:, self.DOWN:], self.down_w[:, :, :], AX.XY, ALU.max, apply_absolute_value=True)\
            .then_inc(self.scales.found, 1)

    def vector(self, nc, dve, bank):
        turn, spread = self.cells(bank)
        self.scales.vector(nc, dve, turn, spread, self.ident)

    def parts(self, nc, dve):
        scale, unscale = self.scales.scale, self.scales.unscale
        dve.wait_ge(self.scales.found, self.scales.ready)
        self.parts_of(nc, dve, [self.router_p[:, part] for part in range(2)], self.router_w[:, :, :], scale[:, 0:1], 1)
        for u in range(self.SHARED):
            cols = slice(u * P, (u + 1) * P)
            for n in range(2):
                self.parts_of(nc, dve, [self.shared_p[:, part, n, :, cols] for part in range(2)],
                              self.shared_w[:, n, :, cols], scale[:, 1 + n:2 + n], self.unit_split(u - 1) + 2 * n + 1)
        for out, src in ((self.pair, scale), (self.unpair, unscale)):
            nc.vector.tensor_tensor(out[:, 0:1], src[:, self.GATE:self.GATE + 1], src[:, self.UP:self.UP + 1], ALU.mult)
            op = nc.vector.tensor_tensor(out[:, 1:], src[:, self.GATES], src[:, self.UPS], ALU.mult)
        op.then_inc(self.factor, 1)
        dve.wait_ge(self.factor, 1)
        nc.vector.tensor_reduce(self.least[:, :], self.pair[:, :], AX.X, ALU.min)
        nc.vector.tensor_reduce(self.most[:, :], self.unpair[:, :], AX.X, ALU.max).then_inc(self.factor, 1)
        dve.wait_ge(self.factor, 2)
        nc.vector.tensor_scalar(self.least[:, :], self.least[:, :], 2.0 ** -29, None, ALU.mult)
        nc.vector.tensor_scalar(self.most[:, :], self.most[:, :], 2.0 ** 29, None, ALU.mult).then_inc(self.factor, 1)
        dve.wait_ge(self.factor, 3)
        nc.vector.tensor_scalar(self.up_scale[:, 0:1], unscale[:, self.UP:self.UP + 1], self.least[:, 0:1], None, ALU.mult)
        nc.vector.tensor_tensor(self.out_unscale[:, :], self.most[:, :], unscale[:, self.DOWN:], ALU.mult)
        nc.vector.tensor_scalar(self.up_scale[:, 1:], unscale[:, self.UPS], self.least[:, 0:1], None, ALU.mult)\
            .then_inc(self.factor, 1)


def rolling(eng, step, depth=2, n=G):
    lead = depth - 1
    pairs = (n - lead) // 2

    def peeled(m):
        step([(m - k, (m - k) % 2, (m - k) // 2) if 0 <= m - k < n else None for k in range(depth)])

    for m in range(lead):
        peeled(m)
    with eng.Fori(0, pairs) as i:
        for r in range(2):
            at = [lead + r - k for k in range(depth)]
            step([(i * 2 + a, a % 2, i + a // 2) for a in at])
    for m in range(lead + 2 * pairs, n + lead):
        peeled(m)


def qkv_phase(nc, x_d, w_qkv_d, cos_d, sin_d, ident_d, late_weights, late_ds, parts_d, qk_d, va_d):
    W3 = 3 * C
    CH = 2 * KC
    with ExitStack() as ctx:
        s = Space(nc, ctx, "qkv")
        w = WeightSplit(s, "w_qkv", KC * W3)
        exchange = s.sb("exchange", [P, P])
        ident = s.sb("ident", [P, P])
        ones = s.sb("ones", [1, P])
        cos = s.sb("cos", [P, 2, GT])
        sin = s.sb("sin", [P, 2, GT])
        xin = s.sb("xin", [P, 2, TG, C])
        raw = s.sb("raw", [P, CH, GT])
        swapped = s.sb("swapped", [P, CH, GT])
        by_cos = s.sb("by_cos", [P, CH, GT])
        by_sin = s.sb("by_sin", [P, CH, GT])
        rot = s.sb("rot", [P, CH, GT])
        rest = s.sb("rest", [P, CH, GT])
        parts = s.sb("parts", [P, 2, CH, 3, GT], BF16)
        v = s.sb("v", [P, 2, HEADS // HG, TG, HG, 2 * D])
        turned = s.ps("turned", [P, KC, GT])
        qk_ps = s.ps("qk_ps", [P, 2, 2, GT])
        v_ps = s.ps("v_ps", [P, TG, C])
        ln = LayerNorm(s, turned)

        const_in = s.sem("const_in")
        set_done = s.sem("set_done")
        exchange_set = s.sem("exchange_set")
        x_in = [s.sem(f"x_in{p}") for p in range(2)]
        rope_in = [s.sem(f"rope_in{p}") for p in range(2)]
        qk_done = s.step("qk_done")
        own_done = s.step("own_done", credit=2)
        partner_done = s.step("partner_done")
        v_done = s.step("v_done", credit=2)
        raw_done = s.step("raw_done", credit=2)
        v_copied = s.step("v_copied", credit=1)
        passed = s.sem("passed")
        turns_done = s.step("turns_done", credit=2 * CH)
        rot_done = s.step("rot_done", credit=CH)
        hi_done = s.step("hi_done")
        rest_done = s.step("rest_done")
        mid_done = s.step("mid_done")
        parts_done = s.step("parts_done")
        xn_stored = [s.sem(f"xn_stored{p}") for p in range(2)]
        qk_stored = [s.sem(f"qk_stored{p}") for p in range(2)]
        v_stored = [s.sem(f"v_stored{p}") for p in range(2)]
        block = ctx.enter_context(nc.Block())

        def tokens(b, q):
            return bass.ds(q * GT + b * T, GT)

        @block.sync
        def _(sp):
            def load(n, b, q):
                sp.wait_ge(ln.xn_done.sem, ln.xn_done.freed(n, 2))
                sp.dma_start(xin[:, b], x_d[tokens(b, q), :].rearrange("(j p) c -> p j c", p=P)).then_inc(x_in[b], 16)

            def load_weights():
                sp.dma_start(w.w[:, :].rearrange("p (k n) -> p k n", k=KC),
                             w_qkv_d.rearrange("(k p) n -> p k n", p=P)).then_inc(w.loaded, 16)
                sp.dma_start(ident[:, :], ident_d).then_inc(const_in, 16)

            def load_rope(n, b, q):
                sp.wait_ge(turns_done.sem, turns_done.freed(n * CH + (CH - 1), 2 * CH))
                sp.sem_inc(passed, 1)
                for dst, src in ((cos, cos_d), (sin, sin_d)):
                    sp.dma_start(dst[:, b], src[:, bass.ds(q * GT, GT)]).then_inc(rope_in[b], 16)

            def store_xn(n, b, q):
                sp.wait_ge(ln.lo_done.sem, ln.lo_done.done(n))
                sp.sem_inc(passed, 1)
                for part, buf in enumerate((ln.hi, ln.lo)):
                    sp.dma_start(parts_d[part, :, :, tokens(b, q)], buf[:, b]).then_inc(xn_stored[b], 16)

            def store_heads(n, b, q):
                for m in range(CH):
                    sp.wait_ge(parts_done.sem, parts_done.done(n * CH + m))
                    sp.dma_start(qk_d[m // KC, m % KC * P:(m % KC + 1) * P, :, tokens(b, q)], parts[:, b, m])\
                        .then_inc(qk_stored[b], 16)
                sp.wait_ge(v_copied.sem, v_copied.done(n))
                dst = va_d[b * (HEADS // HG):(b + 1) * (HEADS // HG), :, bass.ds(q * TG, TG), :]
                sp.dma_start(dst.rearrange("i p j n -> p i (j n)"), v[:, b].rearrange("p i j h d -> p i (j h d)"))\
                    .then_inc(v_stored[b], 16)

            for b in range(2):
                sp.sem_inc(xn_stored[b], 32)
                sp.sem_inc(v_stored[b], 16)
                sp.sem_inc(qk_stored[b], 16 * CH)

            def step(at):
                if at[0]:
                    load(*at[0])
                    if not at[1]:
                        load_weights()
                    load_rope(*at[0])
                if at[1] and not at[2]:
                    late_weights.load(nc, sp, *late_ds)
                if at[1]:
                    store_xn(*at[1])
                if at[3]:
                    store_heads(*at[3])

            rolling(sp, step, 4)
            for b in range(2):
                sp.wait_ge(qk_stored[b], 16 * CH * (1 + G // 2))
                sp.wait_ge(xn_stored[b], 32 * (1 + G // 2))
                sp.wait_ge(v_stored[b], 16 * (1 + G // 2))

        @block.gpsimd
        def _(pool):
            turns_done.open(pool)
            nc.gpsimd.memset(ones[:, :], 1.0)
            nc.gpsimd.memset(v[:, :, :, :, :, D:], 1.0).then_inc(set_done, 1)

            def each(n, b, q):
                for m in range(CH):
                    c = n * CH + m
                    if m == 0:
                        pool.wait_ge(rope_in[b], q * 32 + 32)
                    pool.wait_ge(raw_done.sem, raw_done.done(c))
                    pool.wait_ge(rot_done.sem, rot_done.freed(c, CH))
                    pool.sem_inc(passed, 1)
                    nc.gpsimd.tensor_tensor(by_cos[:, m], raw[:, m], cos[:, b], ALU.mult)
                    nc.gpsimd.tensor_tensor(by_sin[:, m], swapped[:, m], sin[:, b], ALU.mult)\
                        .then_inc(turns_done.sem, 1)

            in_groups(pool, each)

        @block.vector
        def _(dve):
            ln.xn_done.open(dve)
            ln.lo_done.open(dve)
            rot_done.open(dve)

            def weights():
                dve.wait_ge(const_in, 16)
                pairs = ident[:, :].rearrange("p (i two) -> p i two", two=2)
                exchanged = exchange[:, :].rearrange("p (i two) -> p i two", two=2)
                for one in range(2):
                    op = nc.vector.tensor_copy(exchanged[:, :, one], pairs[:, :, 1 - one])
                op.then_inc(exchange_set, 1)
                w.vector(nc, dve, qk_ps[0:1, 0, 0, 0:P], qk_ps[:, 0, 0, P:P + 1], ident)

            def rotated(c, m, b):
                dve.wait_ge(turns_done.sem, turns_done.done(c))
                nc.vector.tensor_tensor(rot[:, m], by_cos[:, m], by_sin[:, m], ALU.add).then_inc(rot_done.sem, 1)

            def middle(c, m, b):
                dve.wait_ge(hi_done.sem, hi_done.done(c))
                nc.vector.tensor_tensor(rest[:, m], rot[:, m], parts[:, b, m, 0], ALU.subtract).then_inc(rest_done.sem, 1)

            def last(c, m, b):
                dve.wait_ge(mid_done.sem, mid_done.done(c))
                nc.vector.tensor_tensor(parts[:, b, m, 2], rest[:, m], parts[:, b, m, 1], ALU.subtract)\
                    .then_inc(parts_done.sem, 1)

            def step(at):
                new, mid, old = at

                def statistics():
                    n, b, q = new
                    dve.wait_ge(x_in[b], q * 16 + 16)
                    ln.statistics(nc, dve, n, xin[:, b])

                def normalise():
                    n, b, q = new
                    ln.normalise(nc, dve, n, b, xin[:, b])
                    if not mid:
                        weights()

                def low():
                    n, b, q = new
                    dve.wait_ge(v_done.sem, v_done.freed(n, 2))
                    dve.wait_ge(xn_stored[b], q * 32 + 32)
                    ln.low(nc, dve, n, b)

                for stage, *m in ((rotated, 0), (statistics,), (rotated, 1), (normalise,), (middle, 0), (rotated, 2),
                                  (middle, 1), (last, 0), (rotated, 3), (middle, 2), (middle, 3), (last, 1), (last, 2),
                                  (low,), (last, 3)):
                    if not m and new:
                        stage()
                    if m and old:
                        stage(old[0] * CH + m[0], m[0], old[1])

            rolling(dve, step, 3)

        @block.scalar
        def _(act):
            ln.hi_done.open(act)
            raw_done.open(act)
            own_done.open(act)
            v_copied.open(act)
            act.wait_ge(set_done, 1)

            def own(n, b, q, m):
                c = n * CH + m
                act.wait_ge(qk_done.sem, qk_done.done(c))
                act.wait_ge(turns_done.sem, turns_done.freed(c, CH))
                nc.scalar.activation(raw[:, m], qk_ps[:, m % 2, 0], ACT.Identity, scale=w.unscale[:, 0:1])\
                    .then_inc(own_done.sem, 1)

            def partner(n, b, q, m):
                c = n * CH + m
                act.wait_ge(partner_done.sem, partner_done.done(c))
                nc.scalar.copy(swapped[:, m], qk_ps[:, m % 2, 1]).then_inc(raw_done.sem, 1)

            def values(n, b, q):
                act.wait_ge(v_done.sem, v_done.done(n))
                act.wait_ge(v_stored[b], q * 16 + 16)
                for j in range(TG):
                    op = nc.scalar.activation(v[:, b, :, j, :, 0:D],
                                              v_ps[:, j].rearrange("p (i h d) -> p i h d", h=HG, d=D),
                                              ACT.Identity, scale=w.unscale[:, 0:1])
                op.then_inc(v_copied.sem, 1)

            def first_part(n, b, q, m):
                c = n * CH + m
                act.wait_ge(rot_done.sem, rot_done.done(c))
                act.wait_ge(qk_stored[b], q * (16 * CH) + 16 * CH)
                nc.scalar.copy(parts[:, b, m, 0], rot[:, m]).then_inc(hi_done.sem, 1)

            def second_part(n, b, q, m):
                c = n * CH + m
                act.wait_ge(rest_done.sem, rest_done.done(c))
                nc.scalar.copy(parts[:, b, m, 1], rest[:, m]).then_inc(mid_done.sem, 1)

            def step(at):
                new, mid, old = at

                def high():
                    n, b, q = new
                    act.wait_ge(v_done.sem, v_done.freed(n, 2))
                    act.wait_ge(xn_stored[b], q * 32 + 32)
                    ln.high(nc, act, n, b)

                for stage, *m in ((own, 0), (first_part, 0), (first_part, 1), (own, 1), (partner, 0), (own, 2),
                                  (second_part, 0), (first_part, 2), (partner, 1), (high,), (second_part, 1),
                                  (first_part, 3), (partner, 2), (own, 3), (second_part, 2), (second_part, 3),
                                  (partner, 3)):
                    group = new if stage is high else mid if stage in (own, partner) else old
                    if group:
                        stage(*(group if m else ()), *m)
                if mid:
                    values(*mid)

            rolling(act, step, 3)

        @block.tensor
        def _(pe):
            ln.turn_done.open(pe)
            v_done.open(pe)
            pe.wait_ge(const_in, 16)
            pe.wait_ge(set_done, 1)
            def weight(k, cols):
                at = slice(k * W3 + cols.start, k * W3 + cols.stop)
                return w.hi[:, at], w.lo[:, at]

            def heads(n, b, q, m):
                acts = [(ln.hi[:, b, k], ln.lo[:, b, k]) for k in range(KC)]
                cols = slice(m * P, (m + 1) * P)
                pe.wait_ge(own_done.sem, own_done.freed(n * CH + m, 2))
                parts_matmul(nc, qk_ps[:, m % 2, 0], [weight(k, cols) for k in range(KC)], acts).then_inc(qk_done.sem, 1)

            def partners(n, b, q, m):
                c = n * CH + m
                pe.wait_ge(own_done.sem, own_done.done(c))
                pe.wait_ge(raw_done.sem, raw_done.freed(c, 2))
                nc.tensor.matmul(qk_ps[:, m % 2, 1], exchange[:, :], raw[:, m], start=True, stop=True)\
                    .then_inc(partner_done.sem, 1)

            def values(n, b, q, tiles):
                if tiles[0] == 0:
                    pe.wait_ge(v_copied.sem, v_copied.freed(n, 1))
                for j in tiles:
                    at = slice(j * P, (j + 1) * P)
                    op = parts_matmul(nc, v_ps[:, j], [weight(k, slice(2 * C, 3 * C)) for k in range(KC)],
                                      [(ln.hi[:, b, k, at], ln.lo[:, b, k, at]) for k in range(KC)],
                                      weights_stationary=False)
                if tiles[-1] == TG - 1:
                    op.then_inc(v_done.sem, 1)

            def step(at):
                new, mid = at
                def turn():
                    ln.turn(nc, pe, new[0], new[1], ident[:, :])
                    if not mid:
                        w.tensor(nc, pe, qk_ps[0:1, 0, 0, 0:P], qk_ps[:, 0, 0, P:P + 1], ident[:, :], ones[:, :])
                        pe.wait_ge(exchange_set, 1)
                        pe.wait_ge(w.found, w.ready)

                if mid:
                    pe.wait_ge(ln.lo_done.sem, ln.lo_done.done(mid[0]))
                first, second = range(0, TG // 2), range(TG // 2, TG)
                for stage, *m in ((heads, 0), (heads, 1), (partners, 0), (heads, 2), (partners, 1), (turn,),
                                  (partners, 2), (heads, 3), (values, first), (partners, 3), (values, second)):
                    if not m and new:
                        stage()
                    if m and mid:
                        stage(*mid, *m)

            rolling(pe, step, 2)


def attention_phase(nc, qk_d, va_d, ident_d, tri_d, late_weights, o_d, den_d):
    ROWS = 6 * D
    MROWS = 2
    QB, KB = T // GT, T // P
    HP = HG // 2
    steps = [(t, j) for t in range(QB) for j in range(TG * (t + 1))]
    NS, NP = len(steps), len(steps) * HP
    last_step = [max(i for i, (t, _) in enumerate(steps) if t == u) for u in range(QB)]
    diagonal = [i for i, (t, j) in enumerate(steps) if j >= TG * t]
    MXR, SCR = 3, 4
    LATE = QB - 1
    LATE_TO = 18

    def chunks(t):
        return [("chunk", t, tt, h, c) for tt in range(TG * t, TG * (t + 1)) for h in range(HG) for c in range(t + 1)]

    def with_turn(t, turned):
        own = chunks(t)
        return own[:MXR] + [("turn", turned)] + own[MXR:]

    late = with_turn(LATE, LATE - 1)
    early = [e for t in range(LATE) for e in with_turn(t, (t - 1) % QB)]
    period = late + early
    ahead = [e for e in early if e != ("turn", LATE)]
    NA, NE = len(ahead), len(period)
    bank_of = {e: i % MXR for i, e in enumerate(period)}

    def entry_done(it, i):
        return it * NE + (NA + i + 1)

    def bank_freed(it, i):
        before = [k for k in range(i) if bank_of[period[k]] == bank_of[period[i]]]
        if before:
            return entry_done(it, before[-1])
        return it * NE + (NA - NE) + 1 + max(k for k in range(NE) if bank_of[period[k]] == bank_of[period[i]])

    HEAD = ahead.index(("turn", 1)) + 1
    AHEAD = 12

    def spread_entries(start=False):
        def pace(pairs, entries):
            work = np.cumsum([300 + GT - max(0, steps[r // HG][1] - TG * steps[r // HG][0]) * P for r in pairs])
            cost = np.cumsum([1.0 if e[0] == "turn" or e[4] < e[2] // TG else 0.35 + 0.17 * (e[2] % TG + 1)
                              for e in entries])
            place = np.searchsorted(work / work[-1], cost / cost[-1] - 1e-9)
            return [pairs[k] for k in place]

        if start:
            order = ahead[HEAD:] + period
            turns = [t for t in range(1, QB) if t >= LATE - 1 or ("turn", t) in ahead[HEAD:]]
            ends = [order.index(("turn", t)) + 1 for t in turns] + [len(order)]
            by = [(last_step[t - 1] + 1) * HG - AHEAD for t in turns] + [NS * HG]
            at, begin = [], 0
            for k, end in enumerate(ends):
                at += pace(range(by[k - 1] if k else 0, by[k]), order[begin:end])
                begin = end
            base = HEAD - NA
        else:
            at, base = pace(range(LATE_TO * HG), late) + pace(range(LATE_TO * HG, NS * HG), early), 0
        return [[base + i for i, r in enumerate(at) if r == k] for k in range(NS * HG)]

    spots, start_spots = spread_entries(), spread_entries(True)
    SCALE = float(D) ** -0.5
    with ExitStack() as ctx:
        s = Space(nc, ctx, "att")
        qop = s.sb("qop", [P, 2, QB, HG, GT], BF16)
        kop = s.sb("kop", [P, 2, HG, T], BF16)
        v = s.sb("v", [P, 2, KB, HG * 2 * D])
        prob = s.sb("prob", [P, 4, 2, GT])
        o = s.sb("o", [P, 2, GT])
        ident = s.sb("ident", [P, P])
        tri = s.sb("tri", [P, GT])
        scratch = s.sb("scratch", [P, SCR, GT], BF16)
        m_part = s.sb("m_part", [P, HG, KB, QB])
        neg_m = s.sb("neg_m", [P, 2, P])
        m_row = s.sb("m_row", [HG * TG, 2, MROWS, P], BF16)
        score = s.ps("score", [P, 2, 2, GT])
        mx = s.ps("mx", [P, MXR, GT])
        pv = s.ps("pv", [P, GT])
        late_weights.open(s)
        late_banks = [score[:, a, b] for a in range(2) for b in range(2)]

        const_in = s.sem("const_in")
        cells_set = s.sem("cells_set")
        ones_set = s.sem("ones_set")
        first_in = [s.sem(f"first_in{p}") for p in range(2)]
        rest_in = [s.sem(f"rest_in{p}") for p in range(2)]
        second_in = s.sem("second_in")
        m_in = [s.sem(f"m_in{t}") for t in range(QB)]
        score_done = s.step("score_done")
        exp_done = s.step("exp_done", credit=2)
        masked = s.step("masked")
        past = s.sem("past")
        pv_done = s.step("pv_done", credit=2)
        o_copied = s.step("o_copied", credit=1)
        mx_done = s.sem("mx_done")
        m_found = s.sem("m_found")
        m_reduced = s.step("m_reduced", credit=QB)
        m_high = s.step("m_high")
        o_stored = [s.sem(f"o_stored{p}") for p in range(2)]
        FIRST, REST = 16 * (6 + 6), 16 * (6 * (QB - 1) + 1)
        O_STORE = 16 * (HG + 1)
        block = ctx.enter_context(nc.Block())

        def schedule(eng, iteration, first):
            first()
            with eng.Fori(0, NIT // 2 - 1) as i:
                iteration(i * 2, 0, i, True, True)
                iteration(i * 2 + 1, 1, i, True, True)
            iteration(NIT - 2, 0, NIT // 2 - 1, True, False)
            iteration(NIT - 1, 1, NIT // 2 - 1, False, False)

        def walk(eng, entry):
            def first():
                for i, e in enumerate(ahead):
                    entry(0, e, i + 1)

            def iteration(it, slot, use, with_next, with_load):
                for i, e in enumerate(period):
                    own = i < len(late) or e == ("turn", LATE)
                    if own or with_next:
                        count = entry_done(it, i if i < len(late) or with_next else len(late))
                        entry(it if own else it + 1, e, count)

            schedule(eng, iteration, first)

        blocks = list(enumerate((i, j) for i in range(3) for j in range(3 - i)))

        def load_k(eng, b, hg, slot):
            for row, (part, _) in blocks:
                eng.dma_start(kop[row * D:(row + 1) * D, slot],
                              qk_d[1, bass.ds(hg * (HG * D), HG * D), part, bass.ds(b * T, T)]
                              .rearrange("(h d) t -> d h t", d=D)).then_inc(first_in[slot], 16)

        def load_q(eng, b, hg, slot, t, signal):
            for row, (_, part) in blocks:
                eng.dma_start(qop[row * D:(row + 1) * D, slot, t],
                              qk_d[0, bass.ds(hg * (HG * D), HG * D), part, bass.ds(b * T + t * GT, GT)]
                              .rearrange("(h d) t -> d h t", d=D)).then_inc(signal, 16)

        @block.sync
        def _(sp):
            for dst, src in ((ident, ident_d), (tri, tri_d)):
                sp.dma_start(dst[:, :], src).then_inc(const_in, 16)

            def load(b, hg, slot):
                load_k(sp, b, hg, slot)
                for t in range(QB):
                    load_q(sp, b, hg, slot, t, first_in[slot] if t == 0 else rest_in[slot])
                load_v(b, hg, slot)

            def load_v(b, hg, slot):
                sp.dma_start(v[:, slot].rearrange("p j n -> p (j n)"),
                             va_d[bass.ds(b * (HEADS // HG) + hg, 1)].rearrange("o p j n -> (o p) (j n)"))\
                    .then_inc(rest_in[slot], 16)

            def send_m(it, slot, t, own, with_next=True):
                i = period.index(("turn", t)) if with_next else len(late)
                sp.wait_ge(m_found, entry_done(it, i if own else i - NE))
                for part in range(MROWS):
                    row = qop[ROWS + part:ROWS + part + 1, slot, t]
                    sp.dma_start(row.rearrange("o h (j t) -> o (h j) t", t=P),
                                 m_row[:, t % 2, part, :]).then_inc(m_in[t], 16)

            def store(it, t):
                b, hg = it // (HEADS // HG), it % (HEADS // HG)
                sp.wait_ge(o_copied.sem, o_copied.done(it * QB + t))
                toks = bass.ds(b * T + t * GT, GT)
                for h in range(HG):
                    sp.dma_start(o_d[bass.ds((hg * HG + h) * D, D), toks], o[2 * D * h:2 * D * h + D, t % 2])\
                        .then_inc(o_stored[t % 2], 16)
                sp.dma_start(den_d[bass.ds(hg * HG, HG), toks], o[D:P:2 * D, t % 2]).then_inc(o_stored[t % 2], 16)

            def first():
                for slot in range(2):
                    sp.sem_inc(o_stored[slot], O_STORE)
                for t in range(QB):
                    sp.sem_inc(m_in[t], 16 * MROWS)
                load_k(sp, 0, 0, 0)
                for t in range(1, QB):
                    load_q(sp, 0, 0, 0, t, second_in if t == 1 else rest_in[0])
                sp.sem_inc(rest_in[0], 16 * 6)
                load_v(0, 0, 0)
                load(0, 1, 1)
                for t in range(LATE - 1):
                    send_m(0, 0, t, False)

            def iteration(it, slot, use, with_next, with_load):
                send_m(it, slot, LATE - 1, True)
                store(it, 0)
                store(it, 1)
                send_m(it, slot, LATE, True, with_next)
                store(it, 2)
                if with_next:
                    for t in range(LATE - 1):
                        send_m(it + 1, 1 - slot, t, False)
                store(it, 3)
                if with_load:
                    sp.wait_ge(pv_done.sem, pv_done.done(it * NS + (NS - 1)))
                    nxt = it + 2
                    load(nxt // (HEADS // HG), nxt % (HEADS // HG), slot)

            schedule(sp, iteration, first)
            for slot in range(2):
                sp.wait_ge(o_stored[slot], O_STORE * (1 + NIT * QB // 2))

        @block.gpsimd
        def _(pool):
            nc.gpsimd.memset(kop[ROWS:ROWS + MROWS], 1.0).then_inc(ones_set, 1)

            def iteration(it, slot, use, with_next, with_load):
                for i, st in enumerate(diagonal):
                    t, j = steps[st]
                    n0 = (j - TG * t) * P
                    for hp in range(HP):
                        r = st * HP + hp
                        pool.wait_ge(exp_done.sem, exp_done.done(it * NP + r))
                        pool.sem_inc(past, 1)
                        at = prob[:, r % 4, :, n0:n0 + P]
                        nc.gpsimd.affine_select(out=at, in_=at, compare_op=ALU.is_ge, fill=0.0, base=0,
                                                pattern=[[0, 2], [1, P]], channel_multiplier=-1)\
                            .then_inc(masked.sem, 1)

            schedule(pool, iteration, lambda: None)

        @block.vector
        def _(dve):
            m_reduced.open(dve)
            nc.vector.memset(m_part[:], LOWEST)
            nc.vector.memset(neg_m[:], 0.0).then_inc(cells_set, 1)
            dve.wait_ge(const_in, 32)
            dve.wait_ge(cells_set, 1)

            def entry(it, e, count):
                dve.wait_ge(mx_done, count)
                if e[0] == "turn":
                    t = e[1]
                    rows = mx[0:HG * TG, bank_of[e], 0:P]
                    dve.wait_ge(m_in[(t - 2) % QB], (it + (t // 2 + 1)) * (16 * MROWS))
                    nc.vector.tensor_copy(m_row[:, t % 2, 0, :], rows).then_inc(m_high.sem, 1)
                    dve.wait_ge(m_high.sem, m_high.done(it * QB + t))
                    nc.vector.tensor_tensor(m_row[:, t % 2, 1, :], rows, m_row[:, t % 2, 0, :], ALU.subtract)\
                        .then_inc(m_found, 1)
                    return
                _, t, tt, h, c = e
                first, last = chunks(t)[0], chunks(t)[-1]
                cell = m_part[:, h, tt, c:c + 1]
                bank = mx[:, bank_of[e]]
                if e == first:
                    dve.wait_ge(m_reduced.sem, m_reduced.freed(it * QB + t, QB))
                if c < tt // TG:
                    nc.vector.tensor_reduce(cell, bank, AX.X, ALU.max).then_inc(m_found, 1)
                else:
                    w = (tt % TG + 1) * P
                    dve.wait_ge(m_found, count - SCR) if not isinstance(count, int) or count > SCR else None
                    dve.sem_inc(past, 1)
                    nc.vector.tensor_tensor_reduce(scratch[:, period.index(e) % SCR, 0:w], bank[:, 0:w], tri[:, GT - w:GT],
                                                   1.0, LOWEST, ALU.add, ALU.max, cell).then_inc(m_found, 1)
                if e == last:
                    dve.wait_ge(m_found, count)
                    nc.vector.tensor_reduce(
                        neg_m[:, t % 2, 0:HG * TG].rearrange("p (h j) -> p h j", h=HG),
                        m_part[:, :, TG * t:TG * (t + 1), :], AX.X, ALU.max, negate=True).then_inc(m_reduced.sem, 1)

            walk(dve, entry)
            late_weights.means(nc, dve)

        @block.scalar
        def _(act):
            exp_done.open(act)
            o_copied.open(act)

            def iteration(it, slot, use, with_next, with_load):
                def copy_out(t):
                    act.wait_ge(pv_done.sem, pv_done.done(it * NS + last_step[t]))
                    act.wait_ge(o_stored[t % 2], it * (O_STORE * QB // 2) + (t // 2 + 1) * O_STORE)
                    nc.scalar.copy(o[:, t % 2], pv[:, :]).then_inc(o_copied.sem, 1)

                for st, (t, j) in enumerate(steps):
                    n0 = max(0, j - TG * t) * P
                    act.wait_ge(pv_done.sem, pv_done.freed(it * NS + st, 2))
                    for hp in range(HP):
                        r = st * HP + hp
                        act.wait_ge(score_done.sem, score_done.done(it * NP + r))
                        nc.scalar.activation(prob[:, r % 4, :, n0:], score[:, r % 2, :, n0:], ACT.Exp, scale=SCALE)\
                            .then_inc(exp_done.sem, 1)
                    if st - 1 in last_step:
                        copy_out(t - 1)
                copy_out(QB - 1)

            def first():
                load_q(act, 0, 0, 0, 0, first_in[0])
                late_weights.scalar(nc, act, late_banks)

            schedule(act, iteration, first)

        @block.tensor
        def _(pe):
            pv_done.open(pe)

            def entry(it, slot, e, freed):
                if freed is not None:
                    pe.wait_ge(m_found, freed)
                if e[0] == "turn":
                    t = e[1]
                    pe.wait_ge(m_reduced.sem, m_reduced.done(it * QB + t))
                    pe.sem_inc(past, 1)
                    nc.tensor.transpose(mx[:, bank_of[e], 0:P], neg_m[:, t % 2], ident[:, :]).then_inc(mx_done, 1)
                    return
                _, t, tt, h, c = e
                w = GT if c < tt // TG else (tt % TG + 1) * P
                nc.tensor.matmul(mx[:, bank_of[e], 0:w], qop[0:ROWS, slot, t, h, (tt - TG * t) * P:(tt - TG * t + 1) * P],
                                 kop[0:ROWS, slot, h, c * GT:c * GT + w], start=True, stop=True).then_inc(mx_done, 1)

            late_signs = late_weights.GROUPS - late_weights.NW
            after = len(chunks(0))
            late_at = [after + (n + 1) * (HEAD - after) // (late_signs + 1) for n in range(late_signs)]

            def entry_ahead(i):
                e = ahead[i]
                if e == chunks(1)[0]:
                    pe.wait_ge(second_in, 16 * 6)
                if e == chunks(2)[0]:
                    pe.wait_ge(rest_in[0], REST)
                before = [k for k in range(i) if bank_of[ahead[k]] == bank_of[e]]
                entry(0, 0, e, before[-1] + 1 if before else None)

            def first():
                pe.wait_ge(const_in, 32)
                pe.wait_ge(cells_set, 1)
                for n in range(late_weights.NW):
                    late_weights.turn(nc, pe, n, late_banks, ident[:, :])
                pe.wait_ge(first_in[0], FIRST)
                for i in range(HEAD):
                    entry_ahead(i)
                    if i in late_at:
                        late_weights.turn(nc, pe, late_weights.NW + late_at.index(i), late_banks, ident[:, :])
                pe.wait_ge(late_weights.copied, late_weights.GROUPS)
                pe.wait_ge(ones_set, 1)

            def iteration(it, slot, use, with_next, spots):
                pe.wait_ge(first_in[slot], use * FIRST + FIRST)
                pe.wait_ge(rest_in[slot], use * REST + REST)
                def products(st):
                    t, j = steps[st]
                    n0 = max(0, j - TG * t) * P
                    if j == 0:
                        pe.wait_ge(o_copied.sem, o_copied.freed(it * QB + t, 1))
                    if st in diagonal:
                        pe.wait_ge(masked.sem, masked.done(it * (len(diagonal) * HP) + (diagonal.index(st) * HP + HP - 1)))
                    else:
                        pe.wait_ge(exp_done.sem, exp_done.done(it * NP + (st * HP + HP - 1)))
                    for h in range(HG):
                        at = slice(2 * D * h, 2 * D * (h + 1))
                        op = nc.tensor.matmul(pv[at, n0:], v[:, slot, j, at], prob[:, (st * HP + h // 2) % 4, h % 2, n0:],
                                              start=(j == 0), stop=(j == TG * (t + 1) - 1))
                    op.then_inc(pv_done.sem, 1)

                for st, (t, j) in enumerate(steps):
                    n0 = max(0, j - TG * t) * P
                    if j == 0:
                        pe.wait_ge(m_in[t], it * (16 * MROWS) + 2 * (16 * MROWS))
                    for hp in range(HP):
                        r = st * HP + hp
                        pe.wait_ge(exp_done.sem, exp_done.freed(it * NP + r, 2))
                        for hh in range(2):
                            op = nc.tensor.matmul(score[:, r % 2, hh, n0:],
                                                  kop[0:ROWS + MROWS, slot, hp * 2 + hh, j * P:(j + 1) * P],
                                                  qop[0:ROWS + MROWS, slot, t, hp * 2 + hh, n0:],
                                                  start=True, stop=True)
                            if hh == 1:
                                op.then_inc(score_done.sem, 1)
                            for i in spots[r * 2 + hh]:
                                if i < 0:
                                    entry_ahead(i + NA)
                                    continue
                                e = period[i]
                                own = i < len(late) or e == ("turn", LATE)
                                if i == len(late):
                                    if with_next:
                                        pe.wait_ge(first_in[1 - slot], (use + slot + 1) * FIRST)
                                        pe.wait_ge(rest_in[1 - slot], (use + slot + 1) * REST)
                                    else:
                                        entry(it, slot, ("turn", LATE), entry_done(it, len(late) - 1))
                                if i < len(late) or with_next:
                                    entry(it if own else it + 1, slot if own else 1 - slot, e, bank_freed(it, i))
                    if st > 0:
                        products(st - 1)
                products(NS - 1)

            first()
            iteration(0, 0, 0, True, start_spots)
            iteration(1, 1, 0, True, spots)
            with pe.Fori(0, NIT // 2 - 2) as i:
                iteration(i * 2 + 2, 0, i + 1, True, spots)
                iteration(i * 2 + 3, 1, i + 1, True, spots)
            iteration(NIT - 2, 0, NIT // 2 - 1, True, spots)
            iteration(NIT - 1, 1, NIT // 2 - 1, False, spots)


def in_groups(eng, each, n=G):
    with eng.Fori(0, n // 2) as i:
        for slot in range(2):
            each(i * 2 + slot, slot, i)


def ffn_phase(nc, x_d, parts_d, o_d, den_d, rden_d, late_weights, b2_d, w_out_d, ident_d, expert_weights,
              expert_ds, x1_d, xn1T_d, parts1_d):
    HALVES = 2
    GELUS = 4
    w1T, w2T, hid_scale = late_weights.w1T, late_weights.w2T, late_weights.hid_scale
    a1, a2_wide, b1 = late_weights.a1, late_weights.a2_wide, late_weights.b1
    with ExitStack() as ctx:
        s = Space(nc, ctx, "ffn")
        ident = s.sb("ident", [P, P])
        ones = s.sb("ones", [1, P])
        zero = s.sb("zero", [P, KC])
        den = s.sb("den", [P, HEADS * N // P])
        rden = s.sb("rden", [P, HEADS * N // P])
        a2_row = s.sb("a2_row", [P, C])
        b2 = s.sb("b2", [P, C])
        wo = s.sb("wo", [P, KC, C])
        xp = s.sb("xp", [P, 2, 2, KC, GT], F16)
        o = s.sb("o", [P, 2, KC, GT])
        rd = s.sb("rd", [P, 2, KC, GT])
        att = s.sb("att", [P, 2, KC, GT])
        xin = s.sb("xin", [P, 2, TG, C])
        xb = s.sb("xb", [P, 2, TG, C])
        gelu = s.sb("gelu", [P, GELUS, GT])
        hid = s.sb("hid", [P, 2, 2, FC, GT], F16)
        scaled = s.sb("scaled", [P, TG, C])
        x1 = s.sb("x1", [P, 2, TG, C])
        hid_ps = s.ps("hid_ps", [P, 2, GT])
        out_ps = s.ps("out_ps", [P, TG, C])
        att_ps = s.ps("att_ps", [P, TG, C])
        turned = s.ps("turned", [P, KC, GT])
        ln = LayerNorm(s, turned, full=True)

        den_in, rden_done, rden_out = s.sem("den_in"), s.sem("rden_done"), s.sem("rden_out")
        ident_in = s.sem("ident_in")
        w_in = s.sem("w_in")
        set_done = s.sem("set_done")
        zero_stored = s.sem("zero_stored")
        a2_done = s.sem("a2_done")
        a2_kept = s.sem("a2_kept")
        xp_in = [s.sem(f"xp_in{p}") for p in range(2)]
        g_in = [s.sem(f"g_in{p}") for p in range(2)]
        att_done = s.step("att_done", credit=2)
        xb_done = s.step("xb_done", credit=2)
        past_wait = s.sem("past_wait")
        hid_done = s.step("hid_done", credit=2 * FC)
        gelu_done = s.step("gelu_done", credit=2)
        high_done = s.step("high_done")
        low_done = s.step("low_done", credit=GELUS)
        out_done = s.step("out_done", credit=2)
        sum_done = s.step("sum_done", credit=HALVES)
        x1_done = s.step("x1_done", credit=2)
        x1_out = [s.sem(f"x1_out{p}") for p in range(2)]
        xn_out = [s.sem(f"xn_out{p}") for p in range(2)]
        G_LOADS = 16 * (1 + KC + 1)
        WLOADS = 16 * 2
        block = ctx.enter_context(nc.Block())

        @block.sync
        def _(sp):
            rows = den_d.rearrange("h (q t) -> (h q) t", q=P // HEADS)
            sp.dma_start(ident[:, :], ident_d).then_inc(ident_in, 16)

            def load_xn(g, slot, use):
                sp.wait_ge(hid_done.sem, hid_done.freed(g * FC + (FC - 1), 2 * FC))
                sp.sem_inc(past_wait, 1)
                for part in range(2):
                    sp.dma_start(xp[:, slot, part], parts_d[part, :, :, bass.ds(g * GT, GT)]).then_inc(xp_in[slot], 16)

            def load(g, slot, use):
                sp.wait_ge(att_done.sem, att_done.freed(g, 2))
                sp.wait_ge(xb_done.sem, xb_done.freed(g, 2))
                sp.sem_inc(past_wait, 1)
                toks = bass.ds(g * GT, GT)
                sp.dma_start(o[:, slot], o_d[:, toks].rearrange("(k p) t -> p k t", p=P)).then_inc(g_in[slot], 16)
                for k in range(KC):
                    heads = rden_d[k * P // D:(k + 1) * P // D, toks]
                    sp.dma_start(rd[:, slot, k], heads.unsqueeze(1).broadcast_to([P // D, D, GT]))\
                        .then_inc(g_in[slot], 16)
                sp.dma_start(xin[:, slot], x_d[toks, :].rearrange("(j p) c -> p j c", p=P)).then_inc(g_in[slot], 16)

            def store(g, slot, use):
                sp.wait_ge(x1_done.sem, x1_done.done(g))
                sp.sem_inc(past_wait, 1)
                sp.dma_start(x1_d[bass.ds(g * GT, GT), :].rearrange("(j p) c -> p j c", p=P), x1[:, slot])\
                    .then_inc(x1_out[slot], 16)

            def store_xn(g, slot, use):
                sp.wait_ge(ln.lo_done.sem, ln.lo_done.done(g))
                sp.sem_inc(past_wait, 1)
                cols = bass.ds(g * GT, GT)
                for part, buf in enumerate((ln.hi, ln.lo)):
                    sp.dma_start(parts1_d[part, :, :, cols], buf[:, slot]).then_inc(xn_out[slot], 16)
                dst = xn1T_d[:, :, bass.ds(g // (T // GT), 1), bass.ds(g % (T // GT) * GT + 1, GT)]
                sp.dma_start(dst.rearrange("p k b t -> p k (b t)"), ln.full[:, slot]).then_inc(xn_out[slot], 16)

            for slot in range(2):
                sp.sem_inc(x1_out[slot], 16)
                sp.sem_inc(xn_out[slot], 48)
            load_xn(0, 0, 0)
            sp.dma_start(den[:, :], rows).then_inc(den_in, 16)
            sp.dma_start(wo[:, :, :], w_out_d.rearrange("(k p) n -> p k n", p=P)).then_inc(w_in, 16)
            sp.dma_start(b2[:, :], b2_d.rearrange("(o c) -> o c", o=1).broadcast_to([P, C])).then_inc(w_in, 16)
            load_xn(1, 1, 0)
            sp.wait_ge(rden_done, 1)
            sp.dma_start(rden_d.rearrange("h (q t) -> (h q) t", q=P // HEADS), rden[:, :]).then_inc(rden_out, 16)
            sp.wait_ge(rden_out, 16)
            for slot in range(2):
                load(slot, slot, 0)
            sp.wait_ge(set_done, 1)
            with nc.allow_non_contiguous_dma(reason="a column of zeros"):
                for b in range(B):
                    sp.dma_start(xn1T_d[:, :, b, 0], zero[:, :]).then_inc(zero_stored, 16)

            def body(m, with_load, with_x1, with_xn):
                g, slot, use = m
                if with_load:
                    load_xn(g + 2, slot, use)
                    load(g + 2, slot, use)
                if with_x1:
                    store(g - 1, 1 - slot, use)
                if with_xn:
                    store_xn(g - 2, slot, use)

            body((0, 0, 0), True, False, False)
            body((1, 1, 0), True, True, False)
            with sp.Fori(0, (G - 4) // 2) as i:
                for r in range(2):
                    body((i * 2 + (2 + r), r, i), True, True, True)
            expert_weights.load(sp, *expert_ds)
            for g in range(G - 2, G + 2):
                body((g, g % 2, 0), False, g - 1 < G, True)
            for slot in range(2):
                sp.wait_ge(x1_out[slot], 16 * (1 + G // 2))
                sp.wait_ge(xn_out[slot], 48 * (1 + G // 2))
            sp.wait_ge(zero_stored, 16 * B)

        @block.gpsimd
        def _(pool):
            att_done.open(pool)
            xb_done.open(pool)
            nc.gpsimd.memset(ones[:, :], 1.0)
            nc.gpsimd.memset(zero[:, :], 0.0).then_inc(set_done, 1)
            pool.wait_ge(w_in, WLOADS)

            def each(g, slot, use):
                pool.wait_ge(g_in[slot], use * G_LOADS + G_LOADS)
                pool.wait_ge(out_done.sem, out_done.freed(g, 2))
                pool.wait_ge(x1_done.sem, x1_done.freed(g, 2))
                pool.sem_inc(past_wait, 1)
                nc.gpsimd.tensor_tensor(att[:, slot], o[:, slot], rd[:, slot], ALU.mult).then_inc(att_done.sem, 1)
                for j in range(TG):
                    op = nc.gpsimd.tensor_tensor(xb[:, slot, j], xin[:, slot, j], b2[:, :], ALU.add)
                op.then_inc(xb_done.sem, 1)

            in_groups(pool, each)

        @block.vector
        def _(dve):
            x1_done.open(dve)
            sum_done.open(dve)
            low_done.open(dve)
            ln.xn_done.open(dve)
            ln.lo_done.open(dve)
            dve.wait_ge(ident_in, 16)
            hid_scale.vector(nc, dve, out_ps[0:1, 0, 0:P], out_ps[:, 0, P:P + 1], ident)
            dve.wait_ge(a2_done, 1)
            dve.wait_ge(hid_scale.found, hid_scale.ready)
            nc.vector.tensor_scalar(a2_row[:, :], att_ps[:, 0, :], hid_scale.unscale[:, 0:1], None, ALU.mult)\
                .then_inc(a2_kept, 1)
            dve.wait_ge(den_in, 16)
            nc.vector.reciprocal(rden[:, :], den[:, :]).then_inc(rden_done, 1)
            dve.wait_ge(a2_kept, 1)

            def low(g, slot, use, chunks):
                for m in chunks:
                    c = g * FC + m
                    dve.wait_ge(high_done.sem, high_done.done(c))
                    nc.vector.scalar_tensor_tensor(hid[:, slot, 1, m], gelu[:, m % GELUS], hid_scale.scale[:, 0:1],
                                                   hid[:, slot, 0, m], ALU.mult, ALU.subtract).then_inc(low_done.sem, 1)

            def output(g, slot, use):
                dve.wait_ge(out_done.sem, out_done.done(g))
                dve.wait_ge(xb_done.sem, xb_done.done(g))
                dve.wait_ge(x1_out[slot], use * 16 + 16)
                dve.wait_ge(ln.xn_done.sem, ln.xn_done.freed(g, 2))
                dve.wait_ge(x1_done.sem, x1_done.freed(g, 1))
                for half in range(HALVES):
                    tiles = slice(half * TG // HALVES, (half + 1) * TG // HALVES)
                    nc.vector.tensor_tensor(scaled[:, tiles], out_ps[:, tiles],
                                            a2_row[:, :].unsqueeze(1).broadcast_to([P, TG // HALVES, C]), ALU.mult)
                    nc.vector.tensor_tensor(x1[:, slot, tiles], att_ps[:, tiles], xb[:, slot, tiles], ALU.add)\
                        .then_inc(sum_done.sem, 1)
                dve.wait_ge(sum_done.sem, sum_done.done(g * HALVES + (HALVES - 1)))
                nc.vector.tensor_tensor(x1[:, slot], x1[:, slot], scaled[:, :, :], ALU.add).then_inc(x1_done.sem, 1)

            def step(at):
                new, _, old, older = at
                if old:
                    output(*old)
                if older:
                    g, slot, use = older
                    dve.wait_ge(xn_out[slot], use * 48 + 48)
                    ln.low(nc, dve, g, slot)
                if old:
                    dve.wait_ge(x1_done.sem, x1_done.done(old[0]))
                    ln.statistics(nc, dve, old[0], x1[:, old[1]])
                if new:
                    low(*new, range(0, 2))
                if old:
                    ln.normalise(nc, dve, old[0], old[1], x1[:, old[1]])
                if new:
                    low(*new, range(2, FC))

            rolling(dve, step, 4)
            expert_weights.maxima(nc, dve)

        @block.scalar
        def _(act):
            gelu_done.open(act)
            ln.hi_done.open(act)
            act.wait_ge(hid_scale.found, hid_scale.ready)

            def hidden(g, slot, use):
                act.wait_ge(out_done.sem, out_done.freed(g, 2))
                for m in range(FC):
                    c = g * FC + m
                    act.wait_ge(hid_done.sem, hid_done.done(c))
                    act.wait_ge(low_done.sem, low_done.freed(c, GELUS))
                    nc.scalar.activation(gelu[:, m % GELUS], hid_ps[:, m % 2], ACT.Gelu, scale=a1[:, m:m + 1],
                                         bias=b1[:, m:m + 1]).then_inc(gelu_done.sem, 1)
                    if m > 0:
                        high(g, slot, m - 1)
                high(g, slot, FC - 1)

            def high(g, slot, m):
                act.wait_ge(gelu_done.sem, gelu_done.done(g * FC + m))
                nc.scalar.activation(hid[:, slot, 0, m], gelu[:, m % GELUS], ACT.Identity,
                                     scale=hid_scale.scale[:, 0:1]).then_inc(high_done.sem, 1)

            def step(at):
                new, _, old = at
                if new:
                    hidden(*new)
                if old:
                    g, slot, use = old
                    act.wait_ge(xn_out[slot], use * 48 + 48)
                    ln.high(nc, act, g, slot)

            rolling(act, step, 3)

        @block.tensor
        def _(pe):
            out_done.open(pe)
            hid_done.open(pe)
            ln.turn_done.open(pe)
            pe.wait_ge(ident_in, 16)
            pe.wait_ge(set_done, 1)
            hid_scale.tensor(nc, pe, out_ps[0:1, 0, 0:P], out_ps[:, 0, P:P + 1], ident[:, :], ones[:, :])
            for k in range(KC):
                op = nc.tensor.matmul(att_ps[:, 0, k * P:(k + 1) * P], a2_wide[:, k], ident[:, :], start=True, stop=True)
            op.then_inc(a2_done, 1)

            def hidden(g, slot, use, chunks):
                for m in chunks:
                    if m == 0:
                        pe.wait_ge(xp_in[slot], use * 32 + 32)
                    pe.wait_ge(gelu_done.sem, gelu_done.freed(g * FC + m, 2))
                    for k in range(KC):
                        for part in range(2):
                            op = nc.tensor.matmul(hid_ps[:, m % 2], w1T[:, k, m * P:(m + 1) * P],
                                                  xp[:, slot, part, k], start=(k == 0 and part == 0),
                                                  stop=(k == KC - 1 and part == 1))
                    op.then_inc(hid_done.sem, 1)

            def output(g, slot, use, j):
                if j == 0:
                    pe.wait_ge(w_in, WLOADS)
                    pe.wait_ge(a2_kept, 1)
                    pe.wait_ge(att_done.sem, att_done.done(g))
                    pe.wait_ge(low_done.sem, low_done.done(g * FC + FC - 1))
                if j % (TG // HALVES) == 0:
                    pe.wait_ge(sum_done.sem, sum_done.freed(g * HALVES + j // (TG // HALVES), HALVES))
                at = slice(j * P, (j + 1) * P)
                for k in range(KC):
                    nc.tensor.matmul(att_ps[:, j], att[:, slot, k, at], wo[:, k], start=(k == 0), stop=(k == KC - 1))
                for m in range(FC):
                    for part in range(2):
                        op = nc.tensor.matmul(out_ps[:, j], hid[:, slot, part, m, at], w2T[:, m],
                                              start=(m == 0 and part == 0), stop=(m == FC - 1 and part == 1))
                if j == TG - 1:
                    op.then_inc(out_done.sem, 1)

            def step(at):
                new, mid, old = at
                for chunks, tile in (((0, 1, 2), 0), ((3, 4), 1), ((5, 6), 2), ((7,), 3)):
                    if new:
                        hidden(*new, chunks)
                    if old and tile == 2:
                        ln.turn(nc, pe, old[0], old[1], ident[:, :])
                    if mid:
                        output(*mid, tile)

            rolling(pe, step, 3)


def rwkv_phase(nc, xnT_d, late_weights, expert_weights, mixed_d):
    NW = 3
    NO = NW * KC
    STEPS = G
    wT, mix, unmix = late_weights.mixT, late_weights.mix, late_weights.unmix
    decay, first = late_weights.decay, late_weights.first
    with ExitStack() as ctx:
        s = Space(nc, ctx, "rwkv")
        x = s.sb("x", [P, B, KC, GT + 1])
        xm = s.sb("xm", [P, B, NW, KC, GT])
        kvr = s.sb("kvr", [P, B, NW, KC, GT])
        p = s.sb("p", [P, B, KC, GT + 1])
        q = s.sb("q", [P, B, KC, GT + 1])
        d_raw = s.sb("d_raw", [P, KC, GT])
        e_raw = s.sb("e_raw", [P, KC, GT])
        d = s.sb("d", [P, B, KC, GT])
        e_old = s.sb("e_old", [P, B, KC, GT])
        e_new = s.sb("e_new", [P, B, KC, GT])
        by_q = s.sb("by_q", [P, B, KC, GT])
        by_v = s.sb("by_v", [P, B, KC, GT])
        y = s.sb("y", [P, B, KC, GT])
        out = s.sb("out", [P, B, TG, C])
        prod = s.ps("prod", [P, NO, GT])
        out_ps = s.ps("out_ps", [P, GT])

        state_set = s.sem("state_set")
        x_in = [s.sem(f"x_in{b}") for b in range(B)]
        past = s.sem("past")
        prev_done = s.step("prev_done")
        xm_done = s.step("xm_done", credit=2 * NW)
        prod_done = s.step("prod_done", credit=2 * NO)
        kvr_done = s.step("kvr_done", credit=NO)
        p_carried = s.step("p_carried")
        p_done = s.step("p_done")
        raw_done = s.step("raw_done")
        arg_done = s.step("arg_done", credit=2)
        gates_done = s.step("gates_done")
        times_v = s.step("times_v", credit=2)
        q_carried = s.step("q_carried")
        q_done = s.step("q_done", credit=2)
        wkv_done = s.step("wkv_done")
        y_done = s.step("y_done", credit=2)
        half_done = s.step("half_done", credit=4)
        out_done = s.step("out_done", credit=2)
        out_stored = [s.sem(f"out_stored{b}") for b in range(B)]
        HALVES = TG * C // GT
        block = ctx.enter_context(nc.Block())

        @block.sync
        def _(sp):
            def load(n, b, use):
                sp.wait_ge(xm_done.sem, xm_done.freed(n * NW + (NW - 1), 2 * NW))
                src = xnT_d[:, :, b, bass.ds(use * GT, GT + 1)]
                sp.dma_start(x[:, b], src).then_inc(x_in[b], 16)

            def store(n, b, use):
                sp.wait_ge(out_done.sem, out_done.done(n * HALVES + (HALVES - 1)))
                dst = mixed_d[bass.ds(use * GT + b * T, GT), :].rearrange("(j p) c -> p j c", p=P)
                sp.dma_start(dst, out[:, b]).then_inc(out_stored[b], 16)

            for b in range(B):
                sp.sem_inc(out_stored[b], 16)

            def step(at):
                if at[0]:
                    load(*at[0])
                if at[4]:
                    store(*at[4])

            rolling(sp, step, 5)
            for b in range(B):
                sp.wait_ge(out_stored[b], 16 * (1 + STEPS // 2))

        @block.gpsimd
        def _(pool):
            times_v.open(pool)
            y_done.open(pool)
            nc.gpsimd.memset(expert_weights.ones[:, :], 1.0).then_inc(expert_weights.ones_set, 1)
            for b in range(B):
                nc.gpsimd.memset(p[:, b, :, GT:], LOWEST)
                op = nc.gpsimd.memset(q[:, b, :, GT:], 0.0)
            op.then_inc(state_set, 1)

            def step(at):
                new, _, old, last = at
                if new:
                    n, b, use = new
                    pool.wait_ge(x_in[b], use * 16 + 16)
                    pool.wait_ge(prod_done.sem, prod_done.freed(n * NO + (NO - 1), 2 * NO))
                    pool.sem_inc(past, 1)
                    for w in range(NW):
                        for c in range(KC):
                            op = nc.gpsimd.tensor_scalar(xm[:, b, w, c], x[:, b, c, 0:GT], unmix[:, w, c:c + 1], 0.0,
                                                         ALU.mult, ALU.add)
                        op.then_inc(prev_done.sem, 1)
                if last:
                    n, b, use = last
                    pool.wait_ge(wkv_done.sem, wkv_done.done(n * 2 + 1))
                    pool.wait_ge(kvr_done.sem, kvr_done.done(n * NO + (NO - 1)))
                    pool.wait_ge(half_done.sem, half_done.freed(n * HALVES + (HALVES - 1), 2 * HALVES))
                    pool.sem_inc(past, 1)
                    nc.gpsimd.tensor_tensor(y[:, b], by_q[:, b], kvr[:, b, 2], ALU.mult).then_inc(y_done.sem, 1)
                if old:
                    n, b, use = old
                    pool.wait_ge(gates_done.sem, gates_done.done(n))
                    pool.wait_ge(kvr_done.sem, kvr_done.done(n * NO + (2 * KC - 1)))
                    pool.sem_inc(past, 1)
                    nc.gpsimd.tensor_tensor(e_new[:, b], e_new[:, b], kvr[:, b, 1], ALU.mult)
                    nc.gpsimd.tensor_tensor(by_v[:, b], by_v[:, b], kvr[:, b, 1], ALU.mult)\
                        .then_inc(times_v.sem, 1)

            rolling(pool, step, 4)

        @block.vector
        def _(dve):
            xm_done.open(dve)
            q_done.open(dve)
            arg_done.open(dve)
            expert_weights.vector(nc, dve, out_ps)
            dve.wait_ge(state_set, 1)

            def blend(n, b, use):
                for w in range(NW):
                    dve.wait_ge(prev_done.sem, prev_done.done(n * NW + w))
                    for c in range(KC):
                        op = nc.vector.scalar_tensor_tensor(xm[:, b, w, c], x[:, b, c, 1:], mix[:, w, c:c + 1],
                                                            xm[:, b, w, c], ALU.mult, ALU.add)
                    op.then_inc(xm_done.sem, 1)

            def state(n, b, use):
                dve.wait_ge(kvr_done.sem, kvr_done.done(n * NO + (KC - 1)))
                dve.wait_ge(q_done.sem, q_done.freed(n, 2))
                nc.vector.tensor_copy(p[:, b, :, 0:1], p[:, b, :, GT:]).then_inc(p_carried.sem, 1)
                dve.wait_ge(p_carried.sem, p_carried.done(n))
                for c in range(KC):
                    op = nc.vector.tensor_tensor_scan(p[:, b, c, 1:], decay[:, c:c + 1].broadcast_to([P, GT]),
                                                      kvr[:, b, 0, c], p[:, b, c, 0:1], ALU.add, ALU.max)
                op.then_inc(p_done.sem, 1)
                dve.wait_ge(p_done.sem, p_done.done(n))
                dve.wait_ge(arg_done.sem, arg_done.freed(n, 1))
                for c in range(KC):
                    nc.vector.scalar_tensor_tensor(d_raw[:, c], p[:, b, c, 0:GT], first[:, c:c + 1], kvr[:, b, 0, c],
                                                   ALU.subtract, ALU.subtract)
                    op = nc.vector.scalar_tensor_tensor(e_raw[:, c], p[:, b, c, 0:GT], decay[:, c:c + 1],
                                                        kvr[:, b, 0, c], ALU.add, ALU.subtract)
                op.then_inc(raw_done.sem, 1)
                dve.wait_ge(raw_done.sem, raw_done.done(n))
                nc.vector.tensor_scalar(d[:, b], d_raw[:, :, :], CLAMP, -CLAMP, ALU.min, ALU.max)
                nc.vector.tensor_scalar(e_old[:, b], e_raw[:, :, :], 0.0, -CLAMP, ALU.min, ALU.max)
                nc.vector.tensor_scalar(e_new[:, b], e_raw[:, :, :], CLAMP, 0.0, ALU.min, ALU.max)\
                    .then_inc(arg_done.sem, 1)

            def outcome(n, b, use):
                nc.vector.tensor_copy(q[:, b, :, 0:1], q[:, b, :, GT:]).then_inc(q_carried.sem, 1)
                dve.wait_ge(times_v.sem, times_v.done(n))
                dve.wait_ge(q_carried.sem, q_carried.done(n))
                for c in range(KC):
                    op = nc.vector.tensor_tensor_scan(q[:, b, c, 1:], e_old[:, b, c], e_new[:, b, c], q[:, b, c, 0:1],
                                                      ALU.mult, ALU.add)
                op.then_inc(q_done.sem, 1)
                dve.wait_ge(q_done.sem, q_done.done(n))
                nc.vector.tensor_tensor(by_q[:, b], by_q[:, b], q[:, b, :, 0:GT], ALU.mult).then_inc(wkv_done.sem, 1)
                dve.wait_ge(wkv_done.sem, wkv_done.done(n * 2))
                nc.vector.tensor_tensor(by_q[:, b], by_q[:, b], by_v[:, b], ALU.add).then_inc(wkv_done.sem, 1)

            def step(at):
                for stage, group in zip((blend, state, outcome), at):
                    if group:
                        stage(*group)

            rolling(dve, step, 3)
            expert_weights.parts(nc, dve)

        @block.scalar
        def _(act):
            kvr_done.open(act)
            out_done.open(act)

            def products(n, b, use, which):
                for o in which:
                    w, c = o // KC, o % KC
                    if c == 0:
                        read = (arg_done, times_v, y_done)[w]
                        act.wait_ge(read.sem, read.freed(n, 2))
                    act.wait_ge(prod_done.sem, prod_done.done(n * NO + o))
                    nc.scalar.activation(kvr[:, b, w, c], prod[:, o], ACT.Sigmoid if w == 2 else ACT.Identity)\
                        .then_inc(kvr_done.sem, 1)

            def step(at):
                new, old, last = at[0], at[1], at[3]
                if old:
                    n, b, use = old
                    act.wait_ge(arg_done.sem, arg_done.done(n))
                    act.wait_ge(y_done.sem, y_done.freed(n, 2))
                    nc.scalar.activation(by_q[:, b], d[:, b], ACT.Sigmoid)
                    nc.scalar.activation(by_v[:, b], d[:, b], ACT.Sigmoid, scale=-1.0)
                    nc.scalar.activation(e_old[:, b], e_old[:, b], ACT.Exp)
                    nc.scalar.activation(e_new[:, b], e_new[:, b], ACT.Exp, scale=-1.0).then_inc(gates_done.sem, 1)
                for half in range(HALVES):
                    if new:
                        products(*new, range(half * NO // HALVES, (half + 1) * NO // HALVES))
                    if last:
                        n, b, use = last
                        h = n * HALVES + half
                        act.wait_ge(half_done.sem, half_done.done(h))
                        act.wait_ge(out_stored[b], use * 16 + 16)
                        tiles = slice(half * TG // HALVES, (half + 1) * TG // HALVES)
                        nc.scalar.copy(out[:, b, tiles].rearrange("p j c -> p (j c)"), out_ps[:, :])\
                            .then_inc(out_done.sem, 1)

            rolling(act, step, 4)

        @block.tensor
        def _(pe):
            prod_done.open(pe)
            half_done.open(pe)
            expert_weights.tensor(nc, pe, out_ps)

            def products(n, b, use, which):
                for o in which:
                    w, c = o // KC, o % KC
                    if c == 0:
                        pe.wait_ge(xm_done.sem, xm_done.done(n * NW + w))
                    pe.wait_ge(kvr_done.sem, kvr_done.freed(n * NO + o, NO))
                    for k in range(KC):
                        op = nc.tensor.matmul(prod[:, o], wT[:, w, k, c * P:(c + 1) * P], xm[:, b, w, k],
                                              start=(k == 0), stop=(k == KC - 1))
                    op.then_inc(prod_done.sem, 1)

            def output(n, b, use, half):
                h = n * HALVES + half
                pe.wait_ge(y_done.sem, y_done.done(n))
                pe.wait_ge(out_done.sem, out_done.freed(h, 1))
                for i in range(TG // HALVES):
                    j = half * (TG // HALVES) + i
                    for k in range(KC):
                        op = nc.tensor.matmul(out_ps[:, i * C:(i + 1) * C], y[:, b, k, j * P:(j + 1) * P], wT[:, NW, k],
                                              start=(k == 0), stop=(k == KC - 1))
                op.then_inc(half_done.sem, 1)

            def step(at):
                new, last = at[0], at[3]
                for half in range(HALVES):
                    if new:
                        products(*new, range(half * NO // HALVES, (half + 1) * NO // HALVES))
                    if last:
                        output(*last, half)

            rolling(pe, step, 4)


def moe_phase(nc, x1_d, parts_d, mixed_d, expert_weights, lower_d, coef_d, out_d):
    UNITS = E + ES // P
    SHARED = ES // P
    w = expert_weights
    router_p, shared_p, expert_w = w.router_p, w.shared_p, w.expert_w
    scales, up_scale, ident = w.scales, w.up_scale, w.ident
    EXPERTS, split, unit_split = w.EXPERTS, w.split, w.unit_split
    down_w, down_scale, out_unscale = w.down_w, scales.scale[:, w.DOWN:], w.out_unscale
    with ExitStack() as ctx:
        s = Space(nc, ctx, "moe")
        expert_p = s.sb("expert_p", [P, 2, 2, KC, E, ED], F16)
        down_p = s.sb("down_p", [P, 2, UNITS, C], F16)
        lower = s.sb("lower", [P, E, E])
        xp = s.sb("xp", [P, 2, 2, KC, GT], F16)
        mixed = s.sb("mixed", [P, 2, TG, C])
        x1 = s.sb("x1", [P, 2, TG, C])
        sums = s.sb("sums", [P, 2, TG, C])
        top = s.sb("top", [P, TG])
        z = s.sb("z", [P, TG, E])
        ex = s.sb("ex", [P, TG, E])
        total = s.sb("total", [P, TG])
        inv = s.sb("inv", [P, TG])
        prob = s.sb("prob", [P, TG, E])
        above = s.sb("above", [P, TG, E, E])
        equal = s.sb("equal", [P, TG, E, E])
        rank = s.sb("rank", [P, TG, E])
        coef = s.sb("coef", [P, TG, E])
        coefT = s.sb("coefT", [TG * E, P])
        spread = s.sb("spread", [P, 2, TG, E, P])
        silu = s.sb("silu", [P, 2, GT])
        weighted = s.sb("weighted", [P, 2, GT])
        hid = s.sb("hid", [P, 2, GT])
        hid_p = s.sb("hid_p", [P, 2, UNITS, GT], F16)
        out = s.sb("out", [P, 2, TG, C])
        gate_ps = s.ps("gate_ps", [P, 2, GT])
        up_ps = s.ps("up_ps", [P, 2, GT])
        out_ps = s.ps("out_ps", [P, TG, C])
        logit_ps = s.ps("logit_ps", [P, GT])
        turn_ps = s.ps("turn_ps", [P, GT])

        lower_in = s.sem("lower_in")
        expert_high = s.sem("expert_high")
        down_high = s.sem("down_high")
        down_low = s.sem("down_low")
        xp_in = [s.sem(f"xp_in{p}") for p in range(2)]
        late_in = [s.sem(f"late_in{p}") for p in range(2)]
        spread_in = [s.sem(f"spread_in{p}") for p in range(2)]
        logit_done = s.step("logit_done")
        route = s.sem("route")
        exp_done = s.step("exp_done")
        past = s.sem("past")
        coef_turned = s.step("coef_turned", credit=1)
        coefT_done = s.step("coefT_done")
        coef_out = s.step("coef_out", credit=1, unit=16)
        gate_done = s.step("gate_done")
        up_done = s.step("up_done", credit=2 * UNITS)
        silu_done = s.step("silu_done", credit=2)
        weighted_done = s.step("weighted_done", credit=2 * E)
        hid_done = s.step("hid_done", credit=2)
        high_done = s.step("high_done")
        low_done = s.step("low_done", credit=2)
        down_done = s.step("down_done", credit=2)
        sums_done = s.step("sums_done", credit=2)
        out_done = s.step("out_done", credit=2)
        stored = [s.sem(f"stored{p}") for p in range(2)]
        ROUTE = 11
        DOWN_PARTS_AT = 4
        block = ctx.enter_context(nc.Block())

        @block.sync
        def _(sp):
            def load_constants():
                sp.dma_start(lower[:, :, :], lower_d).then_inc(lower_in, 16)

            def load(g, slot):
                toks = bass.ds(g * GT, GT)
                sp.wait_ge(up_done.sem, up_done.freed(g * UNITS + (UNITS - 1), 2 * UNITS))
                for part in range(2):
                    sp.dma_start(xp[:, slot, part], parts_d[part, :, :, toks]).then_inc(xp_in[slot], 16)

            def load_late(g, slot):
                toks = bass.ds(g * GT, GT)
                sp.wait_ge(sums_done.sem, sums_done.freed(g, 2))
                sp.sem_inc(past, 1)
                for dst, src in ((mixed, mixed_d), (x1, x1_d)):
                    sp.dma_start(dst[:, slot], src[toks, :].rearrange("(j p) c -> p j c", p=P)).then_inc(late_in[slot], 16)

            def coefficients(g, slot):
                sp.wait_ge(coefT_done.sem, coefT_done.done(g))
                sp.dma_start(coef_d[bass.ds(g, 1), :, :].rearrange("o r t -> (o r) t"), coefT[:, :])\
                    .then_inc(coef_out.sem, 16)
                sp.wait_ge(coef_out.sem, coef_out.done(g))
                sp.wait_ge(weighted_done.sem, weighted_done.freed(g * E + (E - 1), 2 * E))
                row = coef_d[bass.ds(g, 1), :, :].rearrange("o r t -> o (r t)")
                sp.dma_start(spread[:, slot].rearrange("p j e t -> p (j e t)"), row.broadcast_to([P, TG * E * P]))\
                    .then_inc(spread_in[slot], 16)

            def store(g, slot):
                sp.wait_ge(out_done.sem, out_done.done(g))
                dst = out_d[bass.ds(g * GT, GT), :].rearrange("(j p) c -> p j c", p=P)
                sp.dma_start(dst, out[:, slot]).then_inc(stored[slot], 16)

            sp.sem_inc(coef_out.sem, 16)
            for slot in range(2):
                sp.sem_inc(stored[slot], 16)

            def step(at):
                new, old = at
                if new:
                    g, slot, use = new
                    load(g, slot)
                    if not old:
                        load_constants()
                    load_late(g, slot)
                    coefficients(g, slot)
                if old:
                    store(old[0], old[1])

            rolling(sp, step, 2)
            for slot in range(2):
                sp.wait_ge(stored[slot], 16 * (1 + G // 2))

        @block.gpsimd
        def _(pool):
            weighted_done.open(pool)
            sums_done.open(pool)
            for e in range(E):
                for n in range(2):
                    nc.gpsimd.tensor_scalar(expert_p[:, 0, n, :, e], expert_w[:, n, :, e], w.expert_scale(n, e), 0.0,
                                            ALU.mult, ALU.add).then_inc(expert_high, 1)

            def each(g, slot, use):
                pool.wait_ge(spread_in[slot], use * 16 + 16)
                for e in range(E):
                    u = SHARED + e
                    pool.wait_ge(silu_done.sem, silu_done.done(g * UNITS + u))
                    pool.wait_ge(hid_done.sem, hid_done.freed(g * UNITS + u, 2))
                    pool.sem_inc(past, 1)
                    nc.gpsimd.tensor_tensor(weighted[:, u % 2].rearrange("p (j t) -> p j t", j=TG), silu[:, u % 2].rearrange("p (j t) -> p j t", j=TG), spread[:, slot, :, e, :], ALU.mult)\
                        .then_inc(weighted_done.sem, 1)
                pool.wait_ge(late_in[slot], use * 32 + 32)
                pool.wait_ge(out_done.sem, out_done.freed(g, 2))
                pool.sem_inc(past, 1)
                nc.gpsimd.tensor_tensor(sums[:, slot], mixed[:, slot], x1[:, slot], ALU.add).then_inc(sums_done.sem, 1)

            in_groups(pool, each)

        @block.vector
        def _(dve):
            hid_done.open(dve)
            out_done.open(dve)
            low_done.open(dve)

            def unit_weights(u):
                e = u - SHARED
                for n in range(2):
                    dve.wait_ge(expert_high, e * 2 + n + 1)
                    nc.vector.scalar_tensor_tensor(expert_p[:, 1, n, :, e], expert_w[:, n, :, e], w.expert_scale(n, e),
                                                   expert_p[:, 0, n, :, e], ALU.mult, ALU.subtract).then_inc(split, 2)

            def down_weights():
                dve.wait_ge(down_high, 1)
                nc.vector.scalar_tensor_tensor(down_p[:, 1], down_w[:, :, :], down_scale, down_p[:, 0],
                                               ALU.mult, ALU.subtract).then_inc(down_low, 1)

            def over_e(t):
                return t.unsqueeze(2).broadcast_to([P, TG, E])

            def routing(g, slot, use):
                logits = logit_ps[:, 0:TG * E].rearrange("p (j e) -> p j e", j=TG)
                others = prob[:, :, :].unsqueeze(2).broadcast_to([P, TG, E, E])
                own = prob[:, :, :].unsqueeze(3).broadcast_to([P, TG, E, E])
                masks = lower[:, :, :].unsqueeze(1).broadcast_to([P, TG, E, E])
                at = g * ROUTE
                dve.wait_ge(logit_done.sem, logit_done.done(g))
                nc.vector.tensor_reduce(top[:, :], logits, AX.X, ALU.max).then_inc(route, 1)
                dve.wait_ge(route, at + 1)
                nc.vector.tensor_tensor(z[:, :, :], logits, over_e(top[:, :]), ALU.subtract).then_inc(route, 1)
                dve.wait_ge(exp_done.sem, exp_done.done(g))
                nc.vector.tensor_reduce(total[:, :], ex[:, :, :], AX.X, ALU.add).then_inc(route, 1)
                dve.wait_ge(route, at + 3)
                nc.vector.reciprocal(inv[:, :], total[:, :]).then_inc(route, 1)
                dve.wait_ge(route, at + 4)
                nc.vector.tensor_tensor(prob[:, :, :], ex[:, :, :], over_e(inv[:, :]), ALU.mult).then_inc(route, 1)
                dve.wait_ge(route, at + 5)
                nc.vector.tensor_tensor(above[:, :, :, :], others, own, ALU.is_gt).then_inc(route, 1)
                nc.vector.tensor_tensor(equal[:, :, :, :], others, own, ALU.is_equal).then_inc(route, 1)
                dve.wait_ge(route, at + 7)
                nc.vector.tensor_tensor(equal[:, :, :, :], equal[:, :, :, :], masks, ALU.mult).then_inc(route, 1)
                dve.wait_ge(route, at + 8)
                nc.vector.tensor_tensor(above[:, :, :, :], above[:, :, :, :], equal[:, :, :, :], ALU.add)\
                    .then_inc(route, 1)
                dve.wait_ge(route, at + 9)
                nc.vector.tensor_reduce(rank[:, :, :], above[:, :, :, :], AX.X, ALU.add).then_inc(route, 1)
                dve.wait_ge(route, at + 10)
                dve.wait_ge(coef_turned.sem, coef_turned.freed(g, 1))
                nc.vector.scalar_tensor_tensor(coef[:, :, :], rank[:, :, :], 1.5, prob[:, :, :], ALU.is_lt, ALU.mult)\
                    .then_inc(route, 1)
                dve.wait_ge(coef_turned.sem, coef_turned.done(g))
                dve.wait_ge(coef_out.sem, coef_out.freed(g, 1))
                nc.vector.tensor_copy(coefT[:, :], turn_ps[0:TG * E, 0:P]).then_inc(coefT_done.sem, 1)

            def low(n, u):
                dve.wait_ge(high_done.sem, high_done.done(n))
                nc.vector.tensor_tensor(hid_p[:, 1, u], hid[:, u % 2], hid_p[:, 0, u], ALU.subtract)\
                    .then_inc(low_done.sem, 1)

            def hidden(g, slot, use, beginning):
                dve.wait_ge(down_done.sem, down_done.freed(g, 1))
                for u in range(UNITS):
                    n = g * UNITS + u
                    if beginning and u + 2 < UNITS:
                        unit_weights(u + 2)
                    dve.wait_ge(up_done.sem, up_done.done(n))
                    if u < SHARED:
                        dve.wait_ge(silu_done.sem, silu_done.done(n))
                    else:
                        dve.wait_ge(weighted_done.sem, weighted_done.done(g * E + (u - SHARED)))
                    dve.wait_ge(low_done.sem, low_done.freed(n, 2))
                    act = (silu if u < SHARED else weighted)[:, u % 2]
                    of = max(0, u - SHARED + 1)
                    nc.vector.scalar_tensor_tensor(hid[:, u % 2], up_ps[:, u % 2], up_scale[:, of:of + 1], act,
                                                   ALU.mult, ALU.mult).then_inc(hid_done.sem, 1)
                    if u > 0:
                        low(n - 1, u - 1)
                    if beginning and u == DOWN_PARTS_AT:
                        down_weights()
                low(g * UNITS + (UNITS - 1), UNITS - 1)

            def output(g, slot, use):
                dve.wait_ge(down_done.sem, down_done.done(g))
                dve.wait_ge(sums_done.sem, sums_done.done(g))
                dve.wait_ge(stored[slot], use * 16 + 16)
                nc.vector.scalar_tensor_tensor(out[:, slot], out_ps[:, :, :], out_unscale[:, 0:1], sums[:, slot],
                                               ALU.mult, ALU.add).then_inc(out_done.sem, 1)

            def step(at):
                new, old, _ = at
                if new and not old:
                    dve.wait_ge(lower_in, 16)
                    routing(*new)
                    return
                beginning = isinstance(old[0], int) and old[0] == 0 if old else False
                if old:
                    hidden(*old, beginning)
                if new:
                    routing(*new)
                if old:
                    output(*old)

            rolling(dve, step, 3)

        @block.scalar
        def _(act):
            silu_done.open(act)

            def high(n, u):
                act.wait_ge(hid_done.sem, hid_done.done(n))
                nc.scalar.copy(hid_p[:, 0, u], hid[:, u % 2]).then_inc(high_done.sem, 1)

            def hidden(g, slot, use, beginning):
                act.wait_ge(down_done.sem, down_done.freed(g, 1))
                for u in range(UNITS):
                    n = g * UNITS + u
                    act.wait_ge(gate_done.sem, gate_done.done(n))
                    act.wait_ge(hid_done.sem, hid_done.freed(n, 2))
                    of = w.GATE if u < SHARED else EXPERTS + u - SHARED
                    scale = scales.unscale[:, of:of + 1]
                    nc.scalar.activation(silu[:, u % 2], gate_ps[:, u % 2], ACT.Silu, scale=scale)\
                        .then_inc(silu_done.sem, 1)
                    if u > 0:
                        high(n - 1, u - 1)
                    if beginning and u == DOWN_PARTS_AT:
                        nc.scalar.activation(down_p[:, 0], down_w[:, :, :], ACT.Identity, scale=down_scale)\
                            .then_inc(down_high, 1)
                high(g * UNITS + (UNITS - 1), UNITS - 1)

            def step(at):
                new, old, _ = at
                if old:
                    hidden(*old, isinstance(old[0], int) and old[0] == 0)
                if new:
                    g, slot, use = new
                    act.wait_ge(route, g * ROUTE + 2)
                    nc.scalar.activation(ex[:, :, :], z[:, :, :], ACT.Exp, scale=scales.unscale[:, w.ROUTER:w.ROUTER + 1])\
                        .then_inc(exp_done.sem, 1)

            rolling(act, step, 3)

        @block.tensor
        def _(pe):
            up_done.open(pe)
            down_done.open(pe)
            coef_turned.open(pe)
            def routing(g, slot, use):
                pe.wait_ge(xp_in[slot], use * 32 + 32)
                pe.sem_inc(past, 1)
                for j in range(TG):
                    at = slice(j * P, (j + 1) * P)
                    op = parts_matmul(nc, logit_ps[:, j * E:(j + 1) * E],
                                      [(router_p[:, 0, k], router_p[:, 1, k]) for k in range(KC)],
                                      [(xp[:, slot, 0, k, at], xp[:, slot, 1, k, at]) for k in range(KC)],
                                      weights_stationary=False)
                op.then_inc(logit_done.sem, 1)

            def turn(g, slot, use):
                pe.wait_ge(route, g * ROUTE + ROUTE)
                pe.sem_inc(past, 1)
                nc.tensor.transpose(turn_ps[0:TG * E, 0:P], coef[:, :, :].rearrange("p j e -> p (j e)"), ident[:, :])\
                    .then_inc(coef_turned.sem, 1)

            def hidden(g, slot, use, beginning):
                acts = [(xp[:, slot, 0, k], xp[:, slot, 1, k]) for k in range(KC)]

                def weight(n, u, k):
                    if u < SHARED:
                        return tuple(shared_p[:, part, n, k, u * P:(u + 1) * P] for part in range(2))
                    return tuple(expert_p[:, part, n, k, u - SHARED] for part in range(2))

                for u in range(UNITS):
                    n = g * UNITS + u
                    if beginning and u >= SHARED:
                        pe.wait_ge(split, unit_split(u))
                    pe.wait_ge(silu_done.sem, silu_done.freed(n, 2))
                    parts_matmul(nc, gate_ps[:, u % 2], [weight(0, u, k) for k in range(KC)], acts)\
                        .then_inc(gate_done.sem, 1)
                    pe.wait_ge(hid_done.sem, hid_done.freed(n, 2))
                    parts_matmul(nc, up_ps[:, u % 2], [weight(1, u, k) for k in range(KC)], acts)\
                        .then_inc(up_done.sem, 1)

            def output(g, slot, tiles, units):
                for j in tiles:
                    at = slice(j * P, (j + 1) * P)
                    for u in units:
                        for n, (h, d) in enumerate(((0, 0), (0, 1), (1, 0))):
                            op = nc.tensor.matmul(out_ps[:, j], hid_p[:, h, u, at], down_p[:, d, u],
                                                  start=(u == 0 and n == 0), stop=(u == UNITS - 1 and n == 2))
                return op

            def step(at):
                new, old, _ = at
                beginning = isinstance(old[0], int) and old[0] == 0 if old else False
                if old:
                    hidden(*old, beginning)
                if beginning:
                    pe.wait_ge(down_low, 1)
                if new:
                    routing(*new)
                if old:
                    g, slot, use = old
                    pe.wait_ge(out_done.sem, out_done.freed(g, 1))
                    for units in (range(UNITS - 2), [UNITS - 2], [UNITS - 1]):
                        pe.wait_ge(low_done.sem, low_done.done(g * UNITS + units[-1]))
                        output(g, slot, range(0, TG, 2), units)
                if new:
                    turn(*new)
                if old:
                    output(g, slot, range(1, TG, 2), range(UNITS)).then_inc(down_done.sem, 1)

            rolling(pe, step, 3)


def program(nc, x, w_qkv, w_out, w1, b1, w2, b2, mix_k, mix_v, mix_r, w_k, w_v, w_r, w_o, decay, first,
            router, gate, up, down, sgate, sup, sdown, ident, cos, sin, tri, lower, out):

    def scratch(name, shape, dt=F32):
        return nc.dram_tensor(name, shape, dt, kind="Internal").ap()

    x = x.rearrange("b t c -> (b t) c")
    out = out.rearrange("b t c -> (b t) c")
    parts0 = scratch("parts0", [2, P, KC, N], F16)
    qk = scratch("qk", [2, C, 3, N], BF16)
    va = scratch("va", [NIT, P, T // P, HG * 2 * D])
    heads_out = scratch("heads_out", [C, N])
    den = scratch("den", [HEADS, N])
    rden = scratch("rden", [HEADS, N])
    x1 = scratch("x1", [N, C])
    xn1T = scratch("xn1T", [P, KC, B, T + 1])
    parts1 = scratch("parts1", [2, P, KC, N], F16)
    mixed = scratch("mixed", [N, C])
    coef = scratch("coef", [G, TG * E, P])

    with ExitStack() as ctx:
        with ExitStack() as staging_ctx:
            late_weights = LateWeights(Space(nc, ctx, "late"), Space(nc, staging_ctx, "staging"))
            late_ds = w1, b1, w2, (w_k, w_v, w_r, w_o), (mix_k, mix_v, mix_r), decay, first
            qkv_phase(nc, x, w_qkv, cos, sin, ident, late_weights, late_ds, parts0, qk, va)
            attention_phase(nc, qk, va, ident, tri, late_weights, heads_out, den)
        expert_weights = ExpertWeights(Space(nc, ctx, "experts"))
        expert_ds = router, gate, up, down, sgate, sup, sdown, ident
        ffn_phase(nc, x, parts0, heads_out, den, rden, late_weights, b2, w_out, ident, expert_weights, expert_ds,
                  x1, xn1T, parts1)
        rwkv_phase(nc, xn1T, late_weights, expert_weights, mixed)
        moe_phase(nc, x1, parts1, mixed, expert_weights, lower, coef, out)


def shape_tables():
    row = np.arange(P)
    freqs = np.arange(T, dtype=np.float32)[None] * (
        1.0 / np.float32(10000.0) ** (np.arange(0, D, 2, dtype=np.float32) / np.float32(D))
    ).astype(np.float32)[row % D // 2][:, None]
    sign = np.where(row % 2 == 0, -1.0, 1.0)[:, None]
    tri = np.zeros((P, GT), np.float32)
    tri[:, GT - P:] = np.where(row[None] > row[:, None], -1e37, 0.0)
    lower = np.broadcast_to(np.tril(np.ones((E, E), np.float32), -1), (P, E, E))
    return {
        "ident": np.eye(P, dtype=np.float32),
        "cos": np.cos(freqs).astype(np.float32),
        "sin": (np.sin(freqs) * sign).astype(np.float32),
        "tri": tri,
        "lower": np.ascontiguousarray(lower),
    }


INPUTS = (
    "L0_attn_x", "L0_attn_w_qkv", "L0_attn_w_out", "L0_ffn_w1", "L0_ffn_b1", "L0_ffn_w2", "L0_ffn_b2",
    "L1_attn_time_mix_k", "L1_attn_time_mix_v", "L1_attn_time_mix_r", "L1_attn_W_k", "L1_attn_W_v", "L1_attn_W_r",
    "L1_attn_W_o", "L1_attn_time_decay", "L1_attn_time_first", "L1_ffn_router", "L1_ffn_experts_gate",
    "L1_ffn_experts_up", "L1_ffn_experts_down", "L1_ffn_shared_gate", "L1_ffn_shared_up", "L1_ffn_shared_down",
)


def kernel(**inputs):
    import concourse.bacc as bacc
    from concourse.bass_utils import run_bass_kernel_spmd

    nc = bacc.Bacc("TRN2", target_bir_lowering=False, num_devices=1)
    arrays = {name: np.ascontiguousarray(inputs[name]) for name in INPUTS}
    arrays.update(shape_tables())
    args = [nc.dram_tensor(f"in_{name}", a.shape, mybir.dt.from_np(a.dtype), kind="ExternalInput").ap()
            for name, a in arrays.items()]
    out = nc.dram_tensor("out", (B, T, C), F32, kind="ExternalOutput").ap()
    program(nc, *args, out)
    result = run_bass_kernel_spmd(nc, [{f"in_{name}": a for name, a in arrays.items()}], core_ids=[0])
    return result.results[0]["out"]
```
